# Optimizing a Trainium2 kernel written in Bass

```python
import numpy as np
import jax
import jax.numpy as jnp

def _softmax(x, axis=-1):
    return jax.nn.softmax(x, axis=axis)

def _gelu(x):
    return jax.nn.gelu(x, approximate=True)

def _silu(x):
    return jax.nn.silu(x)

def _sigmoid(x):
    return jax.nn.sigmoid(x)

def _layernorm(x, axis=-1, eps=1e-05):
    m = jnp.mean(x, axis=axis, keepdims=True)
    v = jnp.var(x, axis=axis, keepdims=True)
    return (x - m) / jnp.sqrt(v + eps)

def _scatter_add(tgt, idx, src, axis=0):
    return tgt.at[idx].add(src)

def _segment_sum(src, seg, n):
    return jax.ops.segment_sum(src, seg, n)
kernel_name = 'mk_xattn_seq_d4_seqx_r4_6188cc'

def setup_inputs(seed: int=0):
    np.random.seed(seed)
    _w = jnp.asarray

    def _rec_inputs():
        import jax
        import jax.numpy as jnp
        _rk = jax.random.key(seed)
        x = -0.0002928 + 1 * jax.random.normal(jax.random.fold_in(_rk, 1), (16, 256, 256), jnp.float32)
        _lenS = 256 - jax.random.randint(jax.random.fold_in(_rk, 7), (16,), 0, max(1, 256 // 4) + 1, jnp.int32)
        _lenS2 = 256 - jax.random.randint(jax.random.fold_in(_rk, 8), (16,), 0, max(1, 256 // 4) + 1, jnp.int32)
        _ctx_1024P = jax.random.normal(jax.random.fold_in(_rk, 11), (16, 16, 256), jnp.float32)
        _ctx_1024c = jax.random.dirichlet(jax.random.fold_in(_rk, 511), 0.3 * jnp.ones((16,), jnp.float32), (16, 256))
        _ctx_1024t = jnp.einsum('bsk,bkd->bsd', _ctx_1024c, _ctx_1024P)
        _ctx_1024t = _ctx_1024t * jax.lax.rsqrt(jnp.mean(jnp.square(_ctx_1024t)) + 1e-12) * 0.953939
        ctx_1024 = -1.39393e-06 + 0.999914 * (_ctx_1024t + 0.3 * jax.random.normal(jax.random.fold_in(_rk, 611), (16, 256, 256), jnp.float32))
        _validS = jnp.arange(256)[None, :] < _lenS[:, None]
        _validS2 = jnp.arange(256)[None, :] < _lenS2[:, None]
        _causal = jnp.tril(jnp.ones((256, 256), dtype=bool))
        mask_Bx1xSxS2_if1 = jnp.where(jnp.ones((16, 1, 256, 256), dtype=bool), 1, 0).astype(jnp.int32)
        mask_Bx1xSxS2_ik0 = jnp.where(jnp.broadcast_to(_validS2[:, None, None, :], (16, 1, 256, 256)), 0, 1).astype(jnp.int32)
        return (x, ctx_1024, mask_Bx1xSxS2_if1, mask_Bx1xSxS2_ik0)
    x, ctx_1024, mask_Bx1xSxS2_if1, mask_Bx1xSxS2_ik0 = _rec_inputs()

    def _L0_xattn_setup():
        import jax, jax.numpy as jnp
        import numpy as np
        B, S, E, H, FF = (2, 512, 256, 16, 1024)
        HD = E // H
        EPS = 1e-05

        def _layernorm(x, g, b):
            mu = jnp.mean(x, axis=-1, keepdims=True)
            var = jnp.mean(jnp.square(x - mu), axis=-1, keepdims=True)
            return (x - mu) * jax.lax.rsqrt(var + EPS) * g + b

        def _attention(v_in, k_in, q_in, mask, Wv, Wk, Wq, Wo, bo):
            N, Sk, _ = k_in.shape
            Sq = q_in.shape[1]
            v = v_in.reshape(N, Sk, H, HD)
            k = k_in.reshape(N, Sk, H, HD)
            q = q_in.reshape(N, Sq, H, HD)
            v = jnp.einsum('nkhd,ed->nkhe', v, Wv)
            k = jnp.einsum('nkhd,ed->nkhe', k, Wk)
            q = jnp.einsum('nqhd,ed->nqhe', q, Wq)
            energy = jnp.einsum('nqhd,nkhd->nhqk', q, k)
            energy = jnp.where(mask == 0, jnp.float32(-1e+20), energy)
            attn = jax.nn.softmax(energy / jnp.sqrt(jnp.float32(E)), axis=-1)
            out = jnp.einsum('nhqk,nkhd->nqhd', attn, v).reshape(N, Sq, E)
            return out @ Wo.T + bo
        key = jax.random.key(seed)
        ks = jax.random.split(key, 16)
        p = lambda k, shp: jax.random.normal(k, shp, dtype=jnp.float32) * 0.02
        x = jax.random.normal(ks[0], (B, S, E), dtype=jnp.float32)
        encoder_output = jax.random.normal(ks[1], (B, S, E), dtype=jnp.float32)
        tgt_mask = jnp.tril(jnp.ones((S, S), dtype=jnp.int32))[None, None].repeat(B, 0)
        src_mask = jnp.ones((B, 1, S, S), dtype=jnp.int32)
        return {'x': x, 'encoder_output': encoder_output, 'src_mask': src_mask, 'tgt_mask': tgt_mask, 'msa_Wv': p(ks[2], (HD, HD)), 'msa_Wk': p(ks[3], (HD, HD)), 'msa_Wq': p(ks[4], (HD, HD)), 'msa_Wo': p(ks[5], (E, E)), 'msa_bo': jnp.zeros((E,), jnp.float32), 'ca_Wv': p(ks[6], (HD, HD)), 'ca_Wk': p(ks[7], (HD, HD)), 'ca_Wq': p(ks[8], (HD, HD)), 'ca_Wo': p(ks[9], (E, E)), 'ca_bo': jnp.zeros((E,), jnp.float32), 'ff_W1': p(ks[10], (FF, E)), 'ff_b1': jnp.zeros((FF,), jnp.float32), 'ff_W2': p(ks[11], (E, FF)), 'ff_b2': jnp.zeros((E,), jnp.float32), 'ln1_g': jnp.ones((E,), jnp.float32), 'ln1_b': jnp.zeros((E,), jnp.float32), 'ln2_g': jnp.ones((E,), jnp.float32), 'ln2_b': jnp.zeros((E,), jnp.float32), 'ln3_g': jnp.ones((E,), jnp.float32), 'ln3_b': jnp.zeros((E,), jnp.float32)}
    _L0_xattn_all = _L0_xattn_setup()
    _L0_xattn_in = {k: v for k, v in _L0_xattn_all.items() if k in ('msa_Wv', 'msa_Wk', 'msa_Wq', 'msa_Wo', 'msa_bo', 'ca_Wv', 'ca_Wk', 'ca_Wq', 'ca_Wo', 'ca_bo', 'ff_W1', 'ff_b1', 'ff_W2', 'ff_b2', 'ln1_g', 'ln1_b', 'ln2_g', 'ln2_b', 'ln3_g', 'ln3_b')}
    del _L0_xattn_all

    def _L1_xattn_setup():
        import jax, jax.numpy as jnp
        import numpy as np
        DIM = 256
        N_HEADS = 16
        HEAD_DIM = DIM // N_HEADS
        LN_EPS = 1e-05

        def layer_norm(x, gamma, beta, eps=LN_EPS):
            mu = jnp.mean(x, axis=-1, keepdims=True)
            var = jnp.var(x, axis=-1, keepdims=True)
            return (x - mu) * jax.lax.rsqrt(var + eps) * gamma + beta
        key = jax.random.key(seed)
        ks = jax.random.split(key, 12)
        B, Nq, Nc, D = (2, 256, 1024, DIM)
        s = 1.0 / np.sqrt(D)
        inp = {'query': jax.random.normal(ks[0], (B, Nq, D), jnp.float32), 'context': jax.random.normal(ks[1], (B, Nc, D), jnp.float32), 'wq': jax.random.uniform(ks[2], (D, D), jnp.float32, -s, s), 'bq': jax.random.uniform(ks[3], (D,), jnp.float32, -s, s), 'wk': jax.random.uniform(ks[4], (D, D), jnp.float32, -s, s), 'bk': jax.random.uniform(ks[5], (D,), jnp.float32, -s, s), 'wv': jax.random.uniform(ks[6], (D, D), jnp.float32, -s, s), 'bv': jax.random.uniform(ks[7], (D,), jnp.float32, -s, s), 'wo': jax.random.uniform(ks[8], (D, D), jnp.float32, -s, s), 'bo': jax.random.uniform(ks[9], (D,), jnp.float32, -s, s), 'g_q': jnp.ones((D,), jnp.float32), 'b_q': jnp.zeros((D,), jnp.float32), 'g_kv': jnp.ones((D,), jnp.float32), 'b_kv': jnp.zeros((D,), jnp.float32)}
        return inp
    _L1_xattn_all = _L1_xattn_setup()
    _L1_xattn_in = {k: v for k, v in _L1_xattn_all.items() if k in ('wq', 'bq', 'wk', 'bk', 'wv', 'bv', 'wo', 'bo', 'g_q', 'b_q', 'g_kv', 'b_kv')}
    del _L1_xattn_all

    def _L2_xattn_setup():
        import jax, jax.numpy as jnp
        import numpy as np
        D_MODEL = 256
        N_HEADS = 16
        N_KV_HEADS = 1
        HEAD_DIM = D_MODEL // N_HEADS
        WINDOW = 128
        EPS = 1e-06
        NEG = -1000000000.0

        def _window_mask(S):
            i = jnp.arange(S)[:, None]
            j = jnp.arange(S)[None, :]
            half = WINDOW // 2
            return (j >= i - half) & (j < i + half + 1)
        key = jax.random.key(seed)
        ks = jax.random.split(key, 16)
        B, S, D = (2, 512, D_MODEL)
        kv_out = HEAD_DIM * N_KV_HEADS
        s = 0.02
        return {'query': jax.random.normal(ks[0], (B, S, D), jnp.float32), 'key': jax.random.normal(ks[1], (B, S, D), jnp.float32), 'value': jax.random.normal(ks[2], (B, S, D), jnp.float32), 'Wq': jax.random.normal(ks[3], (D, D), jnp.float32) * s, 'bq': jnp.zeros((D,), jnp.float32), 'Wk': jax.random.normal(ks[4], (D, kv_out), jnp.float32) * s, 'bk': jnp.zeros((kv_out,), jnp.float32), 'Wv': jax.random.normal(ks[5], (D, kv_out), jnp.float32) * s, 'bv': jnp.zeros((kv_out,), jnp.float32), 'Wo': jax.random.normal(ks[6], (D, D), jnp.float32) * s, 'bo': jnp.zeros((D,), jnp.float32), 'Wg': jax.random.normal(ks[7], (2 * D, D), jnp.float32) * s, 'bg': jnp.zeros((D,), jnp.float32), 'rms_w': jnp.ones((D,), jnp.float32)}
    _L2_xattn_all = _L2_xattn_setup()
    _L2_xattn_in = {k: v for k, v in _L2_xattn_all.items() if k in ('Wq', 'bq', 'Wk', 'bk', 'Wv', 'bv', 'Wo', 'bo', 'Wg', 'bg', 'rms_w')}
    del _L2_xattn_all

    def _L3_xattn_setup():
        import jax, jax.numpy as jnp
        import numpy as np
        E = 256
        H = 16
        HD = E // H
        EPS = 1e-05

        def _layer_norm(x, g, b):
            mu = jnp.mean(x, axis=-1, keepdims=True)
            var = jnp.var(x, axis=-1, keepdims=True)
            return (x - mu) * jax.lax.rsqrt(var + EPS) * g + b
        key = jax.random.key(seed)
        ks = jax.random.split(key, 16)
        s = 0.02
        inp = {'query': jax.random.normal(ks[0], (4, 256, E), jnp.float32), 'key': jax.random.normal(ks[1], (4, 512, E), jnp.float32), 'value': jax.random.normal(ks[2], (4, 512, E), jnp.float32), 'wq': jax.random.normal(ks[3], (E, E), jnp.float32) * s, 'bq': jnp.zeros((E,), jnp.float32), 'wk': jax.random.normal(ks[4], (E, E), jnp.float32) * s, 'bk': jnp.zeros((E,), jnp.float32), 'wv': jax.random.normal(ks[5], (E, E), jnp.float32) * s, 'bv': jnp.zeros((E,), jnp.float32), 'wo': jax.random.normal(ks[6], (E, E), jnp.float32) * s, 'bo': jnp.zeros((E,), jnp.float32), 'ln1_g': jnp.ones((E,), jnp.float32), 'ln1_b': jnp.zeros((E,), jnp.float32), 'ln2_g': jnp.ones((E,), jnp.float32), 'ln2_b': jnp.zeros((E,), jnp.float32), 'w1': jax.random.normal(ks[7], (E, 4 * E), jnp.float32) * s, 'b1': jnp.zeros((4 * E,), jnp.float32), 'w2': jax.random.normal(ks[8], (4 * E, E), jnp.float32) * s, 'b2': jnp.zeros((E,), jnp.float32)}
        return inp
    _L3_xattn_all = _L3_xattn_setup()
    _L3_xattn_in = {k: v for k, v in _L3_xattn_all.items() if k in ('wq', 'bq', 'wk', 'bk', 'wv', 'bv', 'wo', 'bo', 'ln1_g', 'ln1_b', 'ln2_g', 'ln2_b', 'w1', 'b1', 'w2', 'b2')}
    del _L3_xattn_all
    return {'x': x, 'ctx_1024': ctx_1024, 'mask_Bx1xSxS2_if1': mask_Bx1xSxS2_if1, 'mask_Bx1xSxS2_ik0': mask_Bx1xSxS2_ik0, 'L0_xattn_msa_Wv': _L0_xattn_in['msa_Wv'], 'L0_xattn_msa_Wk': _L0_xattn_in['msa_Wk'], 'L0_xattn_msa_Wq': _L0_xattn_in['msa_Wq'], 'L0_xattn_msa_Wo': _L0_xattn_in['msa_Wo'], 'L0_xattn_msa_bo': _L0_xattn_in['msa_bo'], 'L0_xattn_ca_Wv': _L0_xattn_in['ca_Wv'], 'L0_xattn_ca_Wk': _L0_xattn_in['ca_Wk'], 'L0_xattn_ca_Wq': _L0_xattn_in['ca_Wq'], 'L0_xattn_ca_Wo': _L0_xattn_in['ca_Wo'], 'L0_xattn_ca_bo': _L0_xattn_in['ca_bo'], 'L0_xattn_ff_W1': _L0_xattn_in['ff_W1'], 'L0_xattn_ff_b1': _L0_xattn_in['ff_b1'], 'L0_xattn_ff_W2': _L0_xattn_in['ff_W2'], 'L0_xattn_ff_b2': _L0_xattn_in['ff_b2'], 'L0_xattn_ln1_g': _L0_xattn_in['ln1_g'], 'L0_xattn_ln1_b': _L0_xattn_in['ln1_b'], 'L0_xattn_ln2_g': _L0_xattn_in['ln2_g'], 'L0_xattn_ln2_b': _L0_xattn_in['ln2_b'], 'L0_xattn_ln3_g': _L0_xattn_in['ln3_g'], 'L0_xattn_ln3_b': _L0_xattn_in['ln3_b'], 'L1_xattn_wq': _L1_xattn_in['wq'], 'L1_xattn_bq': _L1_xattn_in['bq'], 'L1_xattn_wk': _L1_xattn_in['wk'], 'L1_xattn_bk': _L1_xattn_in['bk'], 'L1_xattn_wv': _L1_xattn_in['wv'], 'L1_xattn_bv': _L1_xattn_in['bv'], 'L1_xattn_wo': _L1_xattn_in['wo'], 'L1_xattn_bo': _L1_xattn_in['bo'], 'L1_xattn_g_q': _L1_xattn_in['g_q'], 'L1_xattn_b_q': _L1_xattn_in['b_q'], 'L1_xattn_g_kv': _L1_xattn_in['g_kv'], 'L1_xattn_b_kv': _L1_xattn_in['b_kv'], 'L2_xattn_Wq': _L2_xattn_in['Wq'], 'L2_xattn_bq': _L2_xattn_in['bq'], 'L2_xattn_Wk': _L2_xattn_in['Wk'], 'L2_xattn_bk': _L2_xattn_in['bk'], 'L2_xattn_Wv': _L2_xattn_in['Wv'], 'L2_xattn_bv': _L2_xattn_in['bv'], 'L2_xattn_Wo': _L2_xattn_in['Wo'], 'L2_xattn_bo': _L2_xattn_in['bo'], 'L2_xattn_Wg': _L2_xattn_in['Wg'], 'L2_xattn_bg': _L2_xattn_in['bg'], 'L2_xattn_rms_w': _L2_xattn_in['rms_w'], 'L3_xattn_wq': _L3_xattn_in['wq'], 'L3_xattn_bq': _L3_xattn_in['bq'], 'L3_xattn_wk': _L3_xattn_in['wk'], 'L3_xattn_bk': _L3_xattn_in['bk'], 'L3_xattn_wv': _L3_xattn_in['wv'], 'L3_xattn_bv': _L3_xattn_in['bv'], 'L3_xattn_wo': _L3_xattn_in['wo'], 'L3_xattn_bo': _L3_xattn_in['bo'], 'L3_xattn_ln1_g': _L3_xattn_in['ln1_g'], 'L3_xattn_ln1_b': _L3_xattn_in['ln1_b'], 'L3_xattn_ln2_g': _L3_xattn_in['ln2_g'], 'L3_xattn_ln2_b': _L3_xattn_in['ln2_b'], 'L3_xattn_w1': _L3_xattn_in['w1'], 'L3_xattn_b1': _L3_xattn_in['b1'], 'L3_xattn_w2': _L3_xattn_in['w2'], 'L3_xattn_b2': _L3_xattn_in['b2']}

def reference(x, ctx_1024, mask_Bx1xSxS2_if1, mask_Bx1xSxS2_ik0, L0_xattn_msa_Wv, L0_xattn_msa_Wk, L0_xattn_msa_Wq, L0_xattn_msa_Wo, L0_xattn_msa_bo, L0_xattn_ca_Wv, L0_xattn_ca_Wk, L0_xattn_ca_Wq, L0_xattn_ca_Wo, L0_xattn_ca_bo, L0_xattn_ff_W1, L0_xattn_ff_b1, L0_xattn_ff_W2, L0_xattn_ff_b2, L0_xattn_ln1_g, L0_xattn_ln1_b, L0_xattn_ln2_g, L0_xattn_ln2_b, L0_xattn_ln3_g, L0_xattn_ln3_b, L1_xattn_wq, L1_xattn_bq, L1_xattn_wk, L1_xattn_bk, L1_xattn_wv, L1_xattn_bv, L1_xattn_wo, L1_xattn_bo, L1_xattn_g_q, L1_xattn_b_q, L1_xattn_g_kv, L1_xattn_b_kv, L2_xattn_Wq, L2_xattn_bq, L2_xattn_Wk, L2_xattn_bk, L2_xattn_Wv, L2_xattn_bv, L2_xattn_Wo, L2_xattn_bo, L2_xattn_Wg, L2_xattn_bg, L2_xattn_rms_w, L3_xattn_wq, L3_xattn_bq, L3_xattn_wk, L3_xattn_bk, L3_xattn_wv, L3_xattn_bv, L3_xattn_wo, L3_xattn_bo, L3_xattn_ln1_g, L3_xattn_ln1_b, L3_xattn_ln2_g, L3_xattn_ln2_b, L3_xattn_w1, L3_xattn_b1, L3_xattn_w2, L3_xattn_b2):
    import jax
    import jax.numpy as jnp

    def _L0_xattn_ref(x, encoder_output, src_mask, tgt_mask, msa_Wv, msa_Wk, msa_Wq, msa_Wo, msa_bo, ca_Wv, ca_Wk, ca_Wq, ca_Wo, ca_bo, ff_W1, ff_b1, ff_W2, ff_b2, ln1_g, ln1_b, ln2_g, ln2_b, ln3_g, ln3_b):
        import jax, jax.numpy as jnp
        import numpy as np
        B, S, E, H, FF = (2, 512, 256, 16, 1024)
        HD = E // H
        EPS = 1e-05

        def _layernorm(x, g, b):
            mu = jnp.mean(x, axis=-1, keepdims=True)
            var = jnp.mean(jnp.square(x - mu), axis=-1, keepdims=True)
            return (x - mu) * jax.lax.rsqrt(var + EPS) * g + b

        def _attention(v_in, k_in, q_in, mask, Wv, Wk, Wq, Wo, bo):
            N, Sk, _ = k_in.shape
            Sq = q_in.shape[1]
            v = v_in.reshape(N, Sk, H, HD)
            k = k_in.reshape(N, Sk, H, HD)
            q = q_in.reshape(N, Sq, H, HD)
            v = jnp.einsum('nkhd,ed->nkhe', v, Wv)
            k = jnp.einsum('nkhd,ed->nkhe', k, Wk)
            q = jnp.einsum('nqhd,ed->nqhe', q, Wq)
            energy = jnp.einsum('nqhd,nkhd->nhqk', q, k)
            energy = jnp.where(mask == 0, jnp.float32(-1e+20), energy)
            attn = jax.nn.softmax(energy / jnp.sqrt(jnp.float32(E)), axis=-1)
            out = jnp.einsum('nhqk,nkhd->nqhd', attn, v).reshape(N, Sq, E)
            return out @ Wo.T + bo
        sa = _attention(x, x, x, tgt_mask, msa_Wv, msa_Wk, msa_Wq, msa_Wo, msa_bo)
        out = _layernorm(x + sa, ln1_g, ln1_b)
        ca = _attention(encoder_output, encoder_output, out, src_mask, ca_Wv, ca_Wk, ca_Wq, ca_Wo, ca_bo)
        out = _layernorm(out + ca, ln2_g, ln2_b)
        h = jax.nn.relu(out @ ff_W1.T + ff_b1)
        ff = h @ ff_W2.T + ff_b2
        out = _layernorm(out + ff, ln3_g, ln3_b)
        return out

    def _L1_xattn_ref(query, context, wq, bq, wk, bk, wv, bv, wo, bo, g_q, b_q, g_kv, b_kv):
        import jax, jax.numpy as jnp
        import numpy as np
        DIM = 256
        N_HEADS = 16
        HEAD_DIM = DIM // N_HEADS
        LN_EPS = 1e-05

        def layer_norm(x, gamma, beta, eps=LN_EPS):
            mu = jnp.mean(x, axis=-1, keepdims=True)
            var = jnp.var(x, axis=-1, keepdims=True)
            return (x - mu) * jax.lax.rsqrt(var + eps) * gamma + beta
        B, Nq, D = query.shape
        Nc = context.shape[1]
        H, Hd = (N_HEADS, HEAD_DIM)
        qn = layer_norm(query, g_q, b_q)
        cn = layer_norm(context, g_kv, b_kv)
        Q = (jnp.einsum('bnd,ed->bne', qn, wq) + bq).reshape(B, Nq, H, Hd)
        K = (jnp.einsum('bnd,ed->bne', cn, wk) + bk).reshape(B, Nc, H, Hd)
        V = (jnp.einsum('bnd,ed->bne', cn, wv) + bv).reshape(B, Nc, H, Hd)
        scale = 1.0 / np.sqrt(Hd)
        scores = jnp.einsum('bqhd,bkhd->bhqk', Q, K) * scale
        attn = jax.nn.softmax(scores, axis=-1)
        out = jnp.einsum('bhqk,bkhd->bqhd', attn, V).reshape(B, Nq, D)
        return qn + (jnp.einsum('bnd,ed->bne', out, wo) + bo)

    def _L2_xattn_ref(query, key, value, Wq, bq, Wk, bk, Wv, bv, Wo, bo, Wg, bg, rms_w):
        import jax, jax.numpy as jnp
        import numpy as np
        D_MODEL = 256
        N_HEADS = 16
        N_KV_HEADS = 1
        HEAD_DIM = D_MODEL // N_HEADS
        WINDOW = 128
        EPS = 1e-06
        NEG = -1000000000.0

        def _window_mask(S):
            i = jnp.arange(S)[:, None]
            j = jnp.arange(S)[None, :]
            half = WINDOW // 2
            return (j >= i - half) & (j < i + half + 1)
        B, S, D = query.shape
        q = (query @ Wq + bq).reshape(B, S, N_HEADS, HEAD_DIM).transpose(0, 2, 1, 3)
        k = (key @ Wk + bk).reshape(B, S, N_KV_HEADS, HEAD_DIM).transpose(0, 2, 1, 3)
        v = (value @ Wv + bv).reshape(B, S, N_KV_HEADS, HEAD_DIM).transpose(0, 2, 1, 3)
        scale = 1.0 / jnp.sqrt(jnp.float32(HEAD_DIM))
        scores = jnp.matmul(q, jnp.swapaxes(k, -1, -2)) * scale
        keep = _window_mask(S)
        scores = jnp.where(keep[None, None], scores, NEG)
        probs = jax.nn.softmax(scores, axis=-1)
        attn = jnp.matmul(probs, v)
        attn = attn.transpose(0, 2, 1, 3).reshape(B, S, D)
        attn = attn @ Wo + bo
        gate = jax.nn.silu(jnp.concatenate([attn, query], axis=-1) @ Wg + bg)
        out = attn * gate + query * (1.0 - gate)
        x_hat = out * jax.lax.rsqrt(jnp.mean(out * out, axis=-1, keepdims=True) + EPS) * rms_w
        return x_hat - jnp.mean(x_hat, axis=1, keepdims=True)

    def _L3_xattn_ref(query, key, value, wq, bq, wk, bk, wv, bv, wo, bo, ln1_g, ln1_b, ln2_g, ln2_b, w1, b1, w2, b2):
        import jax, jax.numpy as jnp
        import numpy as np
        E = 256
        H = 16
        HD = E // H
        EPS = 1e-05

        def _layer_norm(x, g, b):
            mu = jnp.mean(x, axis=-1, keepdims=True)
            var = jnp.var(x, axis=-1, keepdims=True)
            return (x - mu) * jax.lax.rsqrt(var + EPS) * g + b
        B, Sq, _ = query.shape
        Sk = key.shape[1]
        residual = query
        qn = _layer_norm(query, ln1_g, ln1_b)
        kn = _layer_norm(key, ln1_g, ln1_b)
        vn = _layer_norm(value, ln1_g, ln1_b)
        Q = (qn @ wq + bq).reshape(B, Sq, H, HD)
        K = (kn @ wk + bk).reshape(B, Sk, H, HD)
        V = (vn @ wv + bv).reshape(B, Sk, H, HD)
        scores = jnp.einsum('bqhd,bkhd->bhqk', Q, K) / jnp.sqrt(jnp.float32(HD))
        attn = jax.nn.softmax(scores, axis=-1)
        out = jnp.einsum('bhqk,bkhd->bqhd', attn, V).reshape(B, Sq, E)
        out = out @ wo + bo
        x = residual + out
        residual2 = x
        y = _layer_norm(x, ln2_g, ln2_b)
        y = jax.nn.gelu(y @ w1 + b1, approximate=False)
        y = y @ w2 + b2
        return residual2 + y
    x = _L0_xattn_ref(x, ctx_1024, mask_Bx1xSxS2_if1, mask_Bx1xSxS2_ik0, L0_xattn_msa_Wv, L0_xattn_msa_Wk, L0_xattn_msa_Wq, L0_xattn_msa_Wo, L0_xattn_msa_bo, L0_xattn_ca_Wv, L0_xattn_ca_Wk, L0_xattn_ca_Wq, L0_xattn_ca_Wo, L0_xattn_ca_bo, L0_xattn_ff_W1, L0_xattn_ff_b1, L0_xattn_ff_W2, L0_xattn_ff_b2, L0_xattn_ln1_g, L0_xattn_ln1_b, L0_xattn_ln2_g, L0_xattn_ln2_b, L0_xattn_ln3_g, L0_xattn_ln3_b)
    x = _L1_xattn_ref(x, ctx_1024, L1_xattn_wq, L1_xattn_bq, L1_xattn_wk, L1_xattn_bk, L1_xattn_wv, L1_xattn_bv, L1_xattn_wo, L1_xattn_bo, L1_xattn_g_q, L1_xattn_b_q, L1_xattn_g_kv, L1_xattn_b_kv)
    x = _L2_xattn_ref(x, ctx_1024, ctx_1024, L2_xattn_Wq, L2_xattn_bq, L2_xattn_Wk, L2_xattn_bk, L2_xattn_Wv, L2_xattn_bv, L2_xattn_Wo, L2_xattn_bo, L2_xattn_Wg, L2_xattn_bg, L2_xattn_rms_w)
    x = _L3_xattn_ref(x, ctx_1024, ctx_1024, L3_xattn_wq, L3_xattn_bq, L3_xattn_wk, L3_xattn_bk, L3_xattn_wv, L3_xattn_bv, L3_xattn_wo, L3_xattn_bo, L3_xattn_ln1_g, L3_xattn_ln1_b, L3_xattn_ln2_g, L3_xattn_ln2_b, L3_xattn_w1, L3_xattn_b1, L3_xattn_w2, L3_xattn_b2)
    return x

_drawn_inputs = setup_inputs


def setup_inputs(seed=0):
    import zlib

    import numpy as np

    out = dict(_drawn_inputs(seed))
    spreads = {'L0_xattn_msa_bo': (0.0, 0.271),
     'L0_xattn_ca_bo': (0.0, 0.301),
     'L0_xattn_ff_b1': (0.0, 0.278),
     'L0_xattn_ff_b2': (0.0, 0.335),
     'L0_xattn_ln1_g': (1.0, 0.2),
     'L0_xattn_ln1_b': (0.0, 0.301),
     'L0_xattn_ln2_g': (1.0, 0.2),
     'L0_xattn_ln2_b': (0.0, 0.32),
     'L0_xattn_ln3_g': (1.0, 0.2),
     'L0_xattn_ln3_b': (0.0, 0.274),
     'L1_xattn_g_q': (1.0, 0.2),
     'L1_xattn_b_q': (0.0, 0.338),
     'L1_xattn_g_kv': (1.0, 0.6),
     'L1_xattn_b_kv': (0.0, 0.8),
     'L2_xattn_bq': (0.0, 0.8),
     'L2_xattn_bk': (0.0, 0.8),
     'L2_xattn_bv': (0.0, 0.8),
     'L2_xattn_bo': (0.0, 0.328),
     'L2_xattn_bg': (0.0, 0.1),
     'L2_xattn_rms_w': (1.0, 0.2),
     'L3_xattn_bq': (0.0, 0.8),
     'L3_xattn_bk': (0.0, 0.8),
     'L3_xattn_bv': (0.0, 0.1),
     'L3_xattn_bo': (0.0, 0.1),
     'L3_xattn_ln1_g': (1.0, 0.6),
     'L3_xattn_ln1_b': (0.0, 0.759),
     'L3_xattn_ln2_g': (1.0, 0.6),
     'L3_xattn_ln2_b': (0.0, 0.63),
     'L3_xattn_b1': (0.0, 0.1),
     'L3_xattn_b2': (0.0, 0.1)}
    factors = {'L0_xattn_msa_Wv': 8.0,
     'L0_xattn_msa_Wk': 8.0,
     'L0_xattn_msa_Wq': 8.0,
     'L0_xattn_msa_Wo': 8.0,
     'L0_xattn_ca_Wv': 8.0,
     'L0_xattn_ca_Wk': 8.0,
     'L0_xattn_ca_Wq': 8.0,
     'L0_xattn_ca_Wo': 8.0,
     'L1_xattn_wq': 2.718,
     'L1_xattn_bq': 8.0,
     'L1_xattn_wk': 2.706,
     'L1_xattn_bk': 8.0,
     'L1_xattn_bv': 8.0,
     'L1_xattn_bo': 6.174,
     'L2_xattn_Wq': 8.0,
     'L2_xattn_Wk': 8.0,
     'L2_xattn_Wv': 4.856,
     'L2_xattn_Wo': 3.777,
     'L3_xattn_wq': 8.0,
     'L3_xattn_wk': 8.0}
    for name, (base, spread) in spreads.items():
        noise = np.random.default_rng([zlib.crc32(name.encode()), seed]).standard_normal(out[name].shape)
        drawn = base * np.exp(spread * noise) if base else spread * noise
        out[name] = jnp.asarray(drawn.astype(out[name].dtype))
    for name, factor in factors.items():
        out[name] = (out[name] * factor).astype(out[name].dtype)
    return out
```

```python
import concourse.bass as bass
import concourse.mybir as mybir
import numpy as np
from contextlib import ExitStack

FP32 = mybir.dt.float32
BF16 = mybir.dt.bfloat16
I32 = mybir.dt.int32
ALU = mybir.AluOpType
ACT = mybir.ActivationFunctionType
AX = mybir.AxisListType

B, S, E, H, HD, FF = 16, 256, 256, 16, 16, 1024
P = 128
T = S // P
C = E // P
FC = FF // P
HC = P // HD
NG, NJ = 4, 4
Q = 32
STREAMS = 2
PAIRS = B // STREAMS
WINDOW_HALF = 64
MASKED = -float(2 ** 66)
LAYERS = ["self", "cross", "l1", "l2", "l3"]
SCALE = {"self": 1 / 16, "cross": 1 / 16, "l1": 0.25, "l2": 0.25, "l3": 0.25}
EPS = 1e-5
RMS_EPS = 1e-6

QUERY_PIECES = [0, 0, 0, 1, 1, 2]
KEY_PIECES = [0, 1, 2, 0, 1, 0]
ROWS = HD * len(QUERY_PIECES)
MAX_ROWS = ROWS + 3

PACK = [
    ("wo_self", 512), ("wo_cross", 512),
    ("l0_w1", C * FF), ("l0_w2", FC * E), ("l0_b1", FC),
    ("ln1_g", E), ("ln1_b", E), ("ln2_g", E), ("ln2_b", E), ("ln3_g", E), ("ln3_b", E),
    ("bo_self", E), ("bo_cross", E), ("l0_b2", E),
    ("wq_l1", C * E), ("wk_l1", C * E), ("wv_l1", C * E), ("wo_l1", C * E),
    ("bq_l1", C), ("bk_l1", C), ("g_kv", C), ("b_kv", C), ("bv_l1", C),
    ("g_q", E), ("b_q", E), ("bo_l1", E),
    ("wq_l2", C * E), ("wk_l2", C * HD), ("wv_l2", C * HD), ("wo_l2", C * E), ("wg", 2 * C * E),
    ("bq_l2", C), ("bk_l2", 1), ("bv_l2", C), ("bo_l2", E), ("bg", E), ("rms_w", E),
    ("wq_l3", C * E), ("wk_l3", C * E), ("wv_l3", C * E), ("wo_l3", C * E),
    ("l3_w1", C * FF), ("l3_w2", FC * E),
    ("bq_l3", C), ("bk_l3", C), ("g_in", C), ("b_in", C), ("bv_l3", C), ("g_mlp", C), ("b_mlp", C),
    ("l3_b1", FC), ("bo_l3", E), ("l3_b2", E),
]
SETUP = ["wq_self", "wk_self", "wq_cross", "wk_cross", "wv_self", "wv_cross"]
AT = {}
_n = 0
for _name, _w in PACK:
    AT[_name] = (_n, _w)
    _n += _w
PACKED = _n

BIAS_SOURCES = {"bk_l1": ("wk_l1", "b_kv"), "bv_l1": ("wv_l1", "b_kv"), "bq_l3": ("wq_l3", "b_in"),
                "bk_l3": ("wk_l3", "b_in"), "bv_l3": ("wv_l3", "b_in"), "l3_b1": ("l3_w1", "b_mlp")}
BIAS_COLUMNS = {}
_n = 0
for _name in BIAS_SOURCES:
    BIAS_COLUMNS[_name] = _n
    _n += AT[_name][1]
VALUE_BIASES = ["bv_l1", "bv_l2", "bv_l3"]
START = 1

UNITS = H // 2
UNIT_BUFS = 2
PROB_BUFS = 4
WORK = 2

ATTENTION = (
    [f"max{u}" for u in range(4)] + ["pieces0"] + [f"max{u}" for u in range(4, 6)] + ["turn0", "max6", "max7", "pieces1"]
    + ["exp0", "exp1", "turn1", "exp2", "exp3", "weigh0", "exp4", "exp5", "weigh1", "exp6", "exp7", "weigh2", "weigh3"]
)
DENSE = {
    "self": ["inputs", "xT", "ksplit", "q", "qsplit", "ctxln", "ctxT", "ctxnT", "next_x"],
    "cross": ["out", "ksplit", "mix0", "mix1", "values", "outT", "proj", "ln1", "lnT", "q", "qsplit"],
    "l1": ["out", "keys", "ksplit", "mix0", "mix1", "outT", "v", "proj", "ln2", "next_c", "lnT",
           "hid0", "hid1", "hid2", "hid3", "hid_out", "ln3", "lnq", "lnqT", "q", "qsplit"],
    "l2": ["out", "keys", "ksplit", "mix0", "mix1", "outT", "proj", "lnT", "q", "qsplit"],
    "l3": ["out", "keys", "ksplit", "mix0", "mix1", "outT", "v", "proj", "attnT", "gate", "rms",
           "mean", "lnin", "lnT", "q", "qsplit"],
    "end": ["out", "mix0", "mix1", "outT", "proj", "lnmlp", "lnT",
            "hid0", "hid1", "hid2", "hid3", "hid_out", "store"],
}
NORMS = ("ctxln", "ln1", "ln2", "ln3", "lnq", "rms", "lnin", "lnmlp")
THROUGH_WORK = ("xT", "q", "ctxT", "ctxnT", "mix0", "mix1", "outT", "proj", "lnT", "lnqT", "keys", "v",
                "hid0", "hid1", "hid2", "hid3", "hid_out", "attnT", "gate", "mean", "turn0", "turn1")


def weave(attention, dense):
    out, d = [], 0
    for n, a in enumerate(attention):
        out.append(a)
        upto = (n + 1) * len(dense) // len(attention)
        out += dense[d:upto]
        d = upto
    return out


def schedule():
    def att(s, l):
        return [(s, l, step) for step in ATTENTION]

    def dense(s, l):
        return [(s, l, step) for step in DENSE[l]]

    out = dense(0, "self")
    follows = LAYERS[1:] + ["end"]
    for n, l in enumerate(LAYERS):
        out += weave(att(0, l), dense(1, l))
        out += weave(att(1, l), dense(0, follows[n]))
    return out + dense(1, "end")


SCHEDULE = schedule()
BEFORE = {l: p for p, l in zip(LAYERS, LAYERS[1:] + ["end"])}


def numbered(chosen):
    return {key: n for n, key in enumerate(k for k in SCHEDULE if chosen(k[2]))}


WORK_NO = numbered(lambda step: step in THROUGH_WORK)
UNIT_NO = numbered(lambda step: step[:3] in ("max", "exp"))
MAX_NO = numbered(lambda step: step[:3] == "max")
EXP_NO = numbered(lambda step: step[:3] == "exp")
WEIGH_NO = numbered(lambda step: step.startswith("weigh"))
PIECES_NO = numbered(lambda step: step.startswith("pieces"))
TURN_NO = numbered(lambda step: step.startswith("turn"))
KSPLIT_NO = numbered(lambda step: step == "ksplit")
QSPLIT_NO = numbered(lambda step: step == "qsplit")
OUT_NO = numbered(lambda step: step == "out")
NORM_NO = numbered(lambda step: step in NORMS)
STORE_NO = numbered(lambda step: step == "store")
assert len(WORK_NO) % WORK == 0 and len(UNIT_NO) % UNIT_BUFS == 0 and len(EXP_NO) % PROB_BUFS == 0
WORKS = len(WORK_NO) // WORK


def head_in(slot):
    return slot % C * HC + slot // C


def build(nc, x, ctx, mask_cross, mask_self, params, setup_params, out):
    stack = ExitStack()
    with stack:
        def sb(name, shape, dt=FP32):
            return stack.enter_context(nc.sbuf_tensor(name, shape, dt))

        def ps(name, shape, dt=FP32):
            return stack.enter_context(nc.psum_tensor(name, shape, dt))

        def sem(name):
            return stack.enter_context(nc.semaphore(name))

        def each(name, shape, dt=FP32):
            return [sb(f"{name}_{s}", shape, dt) for s in range(STREAMS)]

        par = sb("par", [P, PACKED])

        def pv(name, parts=1):
            a, w = AT[name]
            v = par[:, a:a + w]
            return v if parts == 1 else v.rearrange("p (c n) -> p c n", c=parts)

        def row(name):
            return pv(name).unsqueeze(1).broadcast_to((P, T, E))

        ident = sb("ident", [P, P])
        ident_b = sb("ident_b", [P, P], BF16)
        mean_w = sb("mean_w", [P, P])
        minus_half = sb("minus_half", [P, T])
        neg_band = sb("neg_band", [P, T, S], BF16)
        fold = {l: sb(f"fold_{l}", [P, P]) for l in ("self", "cross")}
        bv_col = sb("bv_col", [P, 3, C])
        c_in = each("c_in", [P, T, E])
        neg = {l: each(f"neg_{l}", [P, T, S], BF16) for l in ("self", "cross")}
        neg["l2"] = [neg_band] * STREAMS
        tok_t = each("tok_t", [P, C, S])
        ctx_t = each("ctx_t", [P, C, S])
        ctxn_t = each("ctxn_t", [P, C, S])
        query_stack = each("query_stack", [P, H, S], BF16)
        key_stack = each("key_stack", [P, H, S], BF16)
        values = each("values", [P, T, H, Q])
        values_l2 = each("values_l2", [P, T, Q])
        x_b = each("x_b", [P, T, E])
        summed = each("summed", [P, T, E])
        x_in = sb("x_in", [P, T, E])
        m_self = sb("m_self", [P, T, S], I32)
        m_cross = sb("m_cross", [P, T, S], I32)
        key_pieces = sb("key_pieces", [P, 3, C, S], BF16)
        query_pieces = sb("query_pieces", [P, 3, C, S], BF16)
        key_rest = sb("key_rest", [P, C, S])
        query_rest = key_rest
        probs = sb("probs", [P, PROB_BUFS, T, 2, S])
        neg_max = sb("neg_max", [P, 2, T, HC])
        max_rest = sb("max_rest", [P, 2, T, HC])
        max_pieces = sb("max_pieces", [P, 2, T, 3, HC], BF16)
        max_rows = sb("max_rows", [3 * HC, 2, S], BF16)
        out_t = sb("out_t", [P, NG, S])
        recip = sb("recip", [P, T, H])
        out_tok = sb("out_tok", [P, T, E])
        turned_t = sb("turned_t", [P, C, S])
        hidden_t = sb("hidden_t", [P, FC, S])
        norm = sb("norm", [P, T, E])
        resid = sb("resid", [P, T, E])
        xhat = sb("xhat", [P, T, E])
        stats = sb("stats", [P, T, 6])
        mv = sb("mv", [P, T, 2])
        sumsq = sb("sumsq", [P, T])
        var_eps = sb("var_eps", [P, T])
        rstd = sb("rstd", [P, T])
        result = sb("result", [P, T, E])
        attn, diff, gate_in, gate = (hidden_t[:, T * i:T * (i + 1), :] for i in range(4))
        scaled = attn
        flat = probs[:].rearrange("p b k i s -> p (b k i s)")
        setup = {name: flat[:, n * P:(n + 1) * P] for n, name in enumerate(SETUP)}
        used = len(SETUP) * P
        bv_wide = flat[:, used:used + 3 * C * P].rearrange("p (i c n) -> p i c n", i=3, c=C)
        used += 3 * C * P
        ones = flat[:, used:used + P]
        used += P
        band = flat[:, used:used + T * S].rearrange("p (t s) -> p t s", t=T)

        unit_psum = [ps(f"unit{i}", [P, T, 2, S]) for i in range(UNIT_BUFS)]
        out_psum = [ps(f"out{a}", [P, 2, S]) for a in range(2)]
        work_psum = [ps(f"work{i}", [P, 2, S]) for i in range(WORK)]

        ev = {n: [sem(f"{n}_{s}") for s in range(STREAMS)] for n in [
            "values_self", "values_cross", "negs", "bias_self", "bias_cross", "bias_ff", "bias_l1", "diff",
            "bias_l3", "bias_mlp", "ctx_norm", "ln1", "ln2", "lnq", "gate_tanh", "xhat", "lnin", "lnmlp",
            "c_loaded"]}
        x_loaded = sem("x_loaded")
        m_loaded = sem("m_loaded")
        stored = sem("stored")
        keys_placed = sem("keys_placed")
        queries_placed = sem("queries_placed")
        max_placed = sem("max_placed")
        unit_filled = [sem(f"unit_filled{i}") for i in range(UNIT_BUFS)]
        work_filled = [sem(f"work_filled{i}") for i in range(WORK)]
        work_emptied = [sem(f"work_emptied{i}") for i in range(WORK)]
        maxed = sem("maxed")
        exped = sem("exped")
        weighed = sem("weighed")
        out_taken = sem("out_taken")
        max_cut = sem("max_cut")
        key_high = sem("key_high")
        key_low = sem("key_low")
        query_high = sem("query_high")
        query_low = sem("query_low")
        stats_ready = sem("stats_ready")
        rstd_ready = sem("rstd_ready")
        const_ready = sem("const_ready")
        sp_waits = sem("sp_waits")
        pool_waits = sem("pool_waits")
        loaded = sem("loaded")
        fold_products = sem("fold_products")
        fold_wide = sem("fold_wide")
        fold_rows = sem("fold_rows")
        folded = sem("folded")

        def count(numbers, r, key):
            return r * len(numbers) + (numbers[key] + 1)

        def wait_free_unit(pe, r, key):
            n = UNIT_NO[key]
            if n < UNIT_BUFS:
                pe.wait_ge(exped, r * len(EXP_NO) + START)
            else:
                before = next(k for k, m in UNIT_NO.items() if m == n - UNIT_BUFS)
                if before[2][:3] == "max":
                    pe.wait_ge(maxed, count(MAX_NO, r, before))
                else:
                    pe.wait_ge(exped, count(EXP_NO, r, before) + START)
            return unit_psum[n % UNIT_BUFS], unit_filled[n % UNIT_BUFS]

        def wait_full_unit(eng, r, key):
            n = UNIT_NO[key]
            eng.wait_ge(unit_filled[n % UNIT_BUFS], r * (len(UNIT_NO) // UNIT_BUFS) + (n // UNIT_BUFS + 1))
            return unit_psum[n % UNIT_BUFS]

        def wait_free_work(pe, r, key):
            n = WORK_NO[key]
            pe.wait_ge(work_emptied[n % WORK], r * WORKS + (n // WORK + START))
            return work_psum[n % WORK], work_filled[n % WORK]

        def wait_full_work(eng, r, key):
            n = WORK_NO[key]
            eng.wait_ge(work_filled[n % WORK], r * WORKS + (n // WORK + 1))
            return work_psum[n % WORK], work_emptied[n % WORK]

        def wait_taken(eng, r, *keys, before=None):
            last = {}
            for key in keys:
                n = WORK_NO[key]
                if before is None or n % WORK != WORK_NO[before] % WORK:
                    last[n % WORK] = max(last.get(n % WORK, 0), n // WORK + 1 + START)
            for i, k in last.items():
                eng.wait_ge(work_emptied[i], r * WORKS + k)

        def flatten(t):
            return t.rearrange("p a n -> p (a n)")

        block = stack.enter_context(nc.Block())

        @block.sync
        def _(sp):
            x_tok = x.rearrange("b (t p) e -> b p t e", p=P)
            c_tok = ctx.rearrange("b (t p) e -> b p t e", p=P)
            ms_tok = mask_self.rearrange("b o (t p) k -> (b o) p t k", p=P)
            mc_tok = mask_cross.rearrange("b o (t p) k -> (b o) p t k", p=P)
            o_tok = out.rearrange("b (t p) e -> b p t e", p=P)

            def one(v, b):
                return v[bass.ds(b, 1)].rearrange("o p t e -> p (o t) e")

            def load_x(b):
                sp.dma_start(x_in[:], one(x_tok, b)).then_inc(x_loaded, 16)
                sp.dma_start(m_self[:], one(ms_tok, b)).then_inc(m_loaded, 16)
                sp.dma_start(m_cross[:], one(mc_tok, b)).then_inc(m_loaded, 16)

            def load_c(s, b):
                sp.dma_start(c_in[s][:], one(c_tok, b)).then_inc(ev["c_loaded"][s], 16)

            sp.sem_inc(stored, 16)
            sp.sem_inc(keys_placed, 16)
            sp.sem_inc(queries_placed, 16)
            load_x(0)
            load_c(0, 0)
            load_c(1, 1)
            sp.dma_start(flat[:, 0:len(SETUP) * P], setup_params).then_inc(loaded, 16)
            cut = [0, PACKED // 3, 2 * PACKED // 3, PACKED]
            for i in range(3):
                sp.dma_start(par[:, cut[i]:cut[i + 1]], params[:, cut[i]:cut[i + 1]]).then_inc(loaded, 16)
            with sp.Fori(0, PAIRS) as r:
                now = [sp.snap(r * STREAMS + s) for s in range(STREAMS)]
                later = [sp.snap((r * STREAMS + (STREAMS + s)) % B) for s in range(STREAMS)]

                def wait(s, value):
                    sp.wait_ge(s, value)
                    sp.sem_inc(sp_waits, 1)

                def split(s, l, what):
                    keys = what == "ksplit"
                    pieces, stack_, rows = ((key_pieces, key_stack[s], KEY_PIECES) if keys
                                            else (query_pieces, query_stack[s], QUERY_PIECES))
                    high, low, placed = ((key_high, key_low, keys_placed) if keys
                                         else (query_high, query_low, queries_placed))
                    no = KSPLIT_NO if keys else QSPLIT_NO
                    if l == "self":
                        wait(weighed, r * len(WEIGH_NO) + START)
                    else:
                        wait(weighed, count(WEIGH_NO, r, (s, BEFORE[l], "weigh3")) + START)
                    n = no[s, l, what]
                    for piece in range(3):
                        if piece == 0:
                            sp.wait_ge(high, r * len(no) + (n + 1))
                        else:
                            sp.wait_ge(low, r * (2 * len(no)) + (2 * n + piece))
                        for at, which in enumerate(rows):
                            if which != piece:
                                continue
                            dst = stack_[HD * at:HD * (at + 1), :, :]
                            if keys and l == "l2":
                                sp.dma_start(dst[:, 0, :], pieces[0:HD, piece, 0, :]).then_inc(placed, 16)
                            else:
                                sp.dma_start(dst.rearrange("d h n -> d (h n)"),
                                             pieces[:, piece].rearrange("p c n -> p (c n)")).then_inc(placed, 16)

                for key in SCHEDULE:
                    s, l, step = key
                    if step in ("ksplit", "qsplit"):
                        split(s, l, step)
                    elif step in ("turn0", "turn1"):
                        a = int(step[-1])
                        wait_taken(sp, r, key)
                        sp.dma_start(query_stack[s][ROWS:MAX_ROWS, HC * a:HC * (a + 1), :],
                                     max_rows[:, a, :]).then_inc(max_placed, 16)
                    elif step == "next_x":
                        wait_taken(sp, r, (s, "self", "xT"))
                        sp.sem_inc(sp_waits, 1)
                        wait(ev["negs"][s], r + 1)
                        load_x(now[1] if s == 0 else later[0])
                    elif step == "next_c":
                        wait_taken(sp, r, (s, "self", "ctxT"))
                        sp.sem_inc(sp_waits, 1)
                        wait(ev["ctx_norm"][s], r + 1)
                        wait(ev["values_cross"][s], r + 1)
                        load_c(s, later[s])
                    elif step == "store":
                        wait_taken(sp, r, (s, l, "hid_out"))
                        sp.sem_inc(sp_waits, 1)
                        sp.dma_start(one(o_tok, now[s]), result[:]).then_inc(stored, 16)
            sp.wait_ge(stored, 16 * B + 16)
            sp.wait_ge(x_loaded, 16 * (B + 1))
            sp.wait_ge(m_loaded, 32 * (B + 1))
            for s in range(STREAMS):
                sp.wait_ge(ev["c_loaded"][s], 16 * (PAIRS + 1))

        @block.gpsimd
        def _(pool):
            g = nc.gpsimd
            g.memset(ident[:], 0.0)
            g.memset(ones, 1.0)
            g.memset(mean_w[:], 1.0 / S)
            g.memset(minus_half[:], -0.5)
            g.memset(band, 0.0)
            for s in range(STREAMS):
                g.memset(values[s][:], 1.0)
                g.memset(values_l2[s][:], 1.0)
            g.drain()
            for s in range(STREAMS):
                g.memset(key_stack[s][ROWS:P, :, :], 1.0)
            g.drain()
            g.affine_select(out=ident[:], in_=ident[:], compare_op=ALU.not_equal, fill=1.0, base=0,
                            pattern=[[-1, P]], channel_multiplier=1)
            g.affine_select(out=band, in_=band, compare_op=ALU.is_ge, fill=MASKED, base=WINDOW_HALF,
                            pattern=[[-P, T], [1, S]], channel_multiplier=-1)
            g.drain()
            g.affine_select(out=band, in_=band, compare_op=ALU.is_ge, fill=MASKED, base=WINDOW_HALF,
                            pattern=[[P, T], [-1, S]], channel_multiplier=1)
            g.drain()
            g.tensor_copy(neg_band[:], band)
            g.tensor_copy(ident_b[:], ident[:]).then_inc(const_ready, 1)
            pool.wait_ge(folded, 1)

            with pool.Fori(0, PAIRS) as r:
                def wait(s, value):
                    pool.wait_ge(s, value)
                    pool.sem_inc(pool_waits, 1)

                def wait_step(key):
                    wait_taken(pool, r, key)
                    pool.sem_inc(pool_waits, 1)

                def reciprocal_root(key):
                    wait(stats_ready, count(NORM_NO, r, key))
                    if key[2] == "rms":
                        g.tensor_scalar(var_eps[:], sumsq[:], 1.0 / E, RMS_EPS, ALU.mult, ALU.add)
                    else:
                        g.tensor_scalar(var_eps[:], mv[:, :, 1], EPS, None, ALU.add)
                    g.drain()
                    g.tensor_tensor(rstd[:], var_eps[:], minus_half[:], ALU.pow).then_inc(rstd_ready, 1)

                def spread(dst, src):
                    for t in range(T):
                        last = g.tensor_copy(dst[:, t, :, 0:HD].rearrange("p (c h) d -> p c h d", c=C),
                                             src[:, t, :].rearrange("p (c d h) -> p c h d", c=C, d=HD))
                    return last

                def with_bias(s, src, bias, done):
                    g.tensor_tensor(x_b[s][:], src, row(bias), ALU.add).then_inc(ev[done][s], 1)

                for key in SCHEDULE:
                    s, l, step = key
                    if step in NORMS:
                        reciprocal_root(key)
                    if step == "inputs":
                        wait(weighed, r * len(WEIGH_NO) + START)
                        n = (r + (s + 0)) if s else r
                        wait(x_loaded, r * (16 * STREAMS) + 16 * (s + 1))
                        spread(values[s], x_in).then_inc(ev["values_self"][s], 1)
                        wait(work_emptied[WORK_NO[s, "end", "hid_out"] % WORK], r * WORKS + START)
                        with_bias(s, x_in[:], "bo_self", "bias_self")
                        wait(m_loaded, r * (32 * STREAMS) + 32 * (s + 1))
                        for name, m in (("self", m_self), ("cross", m_cross)):
                            last = g.tensor_scalar(neg[name][s][:], m[:], 0, MASKED, ALU.is_equal, ALU.mult)
                        last.then_inc(ev["negs"][s], 1)
                    elif step == "values":
                        wait(weighed, count(WEIGH_NO, r, (s, "self", "weigh3")) + START)
                        wait(ev["c_loaded"][s], 16 * r + 16)
                        spread(values[s], c_in[s]).then_inc(ev["values_cross"][s], 1)
                    elif step == "ln1":
                        wait(ev["ln1"][s], r + 1)
                        with_bias(s, resid[:], "bo_cross", "bias_cross")
                    elif step == "ln2":
                        wait(ev["ln2"][s], r + 1)
                        with_bias(s, resid[:], "l0_b2", "bias_ff")
                    elif step == "lnq":
                        wait(ev["lnq"][s], r + 1)
                        with_bias(s, resid[:], "bo_l1", "bias_l1")
                    elif step == "attnT":
                        wait_step((s, l, "proj"))
                        g.tensor_tensor(diff, attn, summed[s][:], ALU.subtract).then_inc(ev["diff"][s], 1)
                    elif step == "mean":
                        wait_step(key)
                        with_bias(s, summed[s][:], "bo_l3", "bias_l3")
                    elif step == "proj" and l == "end":
                        wait_step(key)
                        with_bias(s, resid[:], "l3_b2", "bias_mlp")
                    elif step in ("pieces0", "pieces1"):
                        a = int(step[-1])
                        wait(maxed, count(MAX_NO, r, (s, l, f"max{4 * a + 3}")))
                        for piece in range(3):
                            src = neg_max if piece == 0 else max_rest
                            last = g.tensor_copy(max_pieces[:, a, :, piece, :], src[:, a])
                            if piece < 2:
                                g.drain()
                                g.tensor_tensor(max_rest[:, a], src[:, a], max_pieces[:, a, :, piece, :], ALU.subtract)
                                g.drain()
                        last.then_inc(max_cut, 1)

        @block.scalar
        def _(act):
            a_ = nc.scalar
            act.wait_ge(folded, 1)
            act.sem_inc(exped, START)
            act.sem_inc(out_taken, START)
            with act.Fori(0, PAIRS) as r:
                def take(key, dst):
                    bank, taken = wait_full_work(act, r, key)
                    a_.copy(dst[:], bank[:]).then_inc(taken, 1)

                def high(s, l, what):
                    keys = what == "ksplit"
                    pieces, done, placed, no = ((key_pieces, key_high, keys_placed, KSPLIT_NO) if keys
                                                else (query_pieces, query_high, queries_placed, QSPLIT_NO))
                    act.wait_ge(placed, r * (96 * len(no)) + (96 * no[s, l, what] + 16))
                    dst = pieces[:, 0]
                    if keys and l in ("self", "cross"):
                        src = (tok_t if l == "self" else ctx_t)[s]
                        wait_taken(act, r, (s, "self", "xT" if l == "self" else "ctxT"))
                        last = a_.copy(dst, src[:])
                    else:
                        bank, _ = wait_full_work(act, r, (s, l, "keys" if keys else "q"))
                        if l in ("self", "cross"):
                            last = a_.copy(dst, bank[:])
                        elif keys and l == "l2":
                            last = a_.activation(dst[0:HD, 0, :], bank[0:HD, 0, :], ACT.Identity,
                                                 bias=pv("bk_l2")[0:HD, :])
                        else:
                            bias = pv(("bk_" if keys else "bq_") + l)
                            for c in range(C):
                                last = a_.activation(dst[:, c, :], bank[:, c, :], ACT.Identity, bias=bias[:, c:c + 1])
                    last.then_inc(done, 1)

                for key in SCHEDULE:
                    s, l, step = key
                    if step[:3] == "exp":
                        n = EXP_NO[key]
                        bank = wait_full_unit(act, r, key)
                        act.wait_ge(weighed, r * len(WEIGH_NO) + max((n - PROB_BUFS) // 2 + 1, 0) + START)
                        a_.activation(probs[:, n % PROB_BUFS], bank[:], ACT.Exp, scale=SCALE[l]).then_inc(exped, 1)
                    elif step in ("turn0", "turn1"):
                        bank, taken = wait_full_work(act, r, key)
                        a_.copy(max_rows[:, int(step[-1]), :], bank[0:3 * HC, 0, :]).then_inc(taken, 1)
                    elif step == "out":
                        act.wait_ge(weighed, count(WEIGH_NO, r, (s, BEFORE[l], "weigh3")) + START)
                        a_.copy(out_t[:, 0:2, :], out_psum[0][:])
                        a_.copy(out_t[:, 2:4, :], out_psum[1][:]).then_inc(out_taken, 1)
                    elif step in ("ksplit", "qsplit"):
                        high(s, l, step)
                    elif step in ("xT", "lnT", "lnqT"):
                        take(key, tok_t[s])
                    elif step == "ctxT":
                        take(key, ctx_t[s])
                    elif step == "ctxnT":
                        take(key, ctxn_t[s])
                    elif step in ("outT", "attnT"):
                        take(key, turned_t)
                    elif step[:3] == "hid" and step != "hid_out":
                        bank, taken = wait_full_work(act, r, key)
                        func, bias = (ACT.Relu, "l0_b1") if l == "l1" else (ACT.Gelu, "l3_b1")
                        for k in range(2):
                            f = 2 * int(step[-1]) + k
                            last = a_.activation(hidden_t[:, f, :], bank[:, k, :], func, bias=pv(bias)[:, f:f + 1])
                        last.then_inc(taken, 1)
                    elif step == "rms":
                        wait_taken(act, r, (s, l, "gate"))
                        a_.activation(gate, gate_in, ACT.Tanh, scale=0.5).then_inc(ev["gate_tanh"][s], 1)

        @block.vector
        def _(dve):
            v = nc.vector
            dve.wait_ge(loaded, 64)
            dve.wait_ge(const_ready, 1)
            dve.wait_ge(fold_products, 1)
            v.tensor_copy(fold["self"][:], unit_psum[0][:, 0, 0, 0:P])
            v.tensor_copy(fold["cross"][:], unit_psum[0][:, 0, 0, P:2 * P])
            v.tensor_copy(pv("wo_self", C), unit_psum[0][:, 1])
            v.tensor_copy(pv("wo_cross", C), unit_psum[1][:, 0])
            sums = flatten(unit_psum[1][:, 1])
            for name, a in BIAS_COLUMNS.items():
                w = AT[name][1]
                dst = bv_col[:, VALUE_BIASES.index(name), :] if name in VALUE_BIASES else pv(name)
                v.tensor_tensor(dst, sums[:, a:a + w], pv(name), ALU.add)
            v.tensor_copy(bv_col[:, 1, :], pv("bv_l2"))
            v.drain()
            for i in range(3):
                for c in range(C):
                    last = v.tensor_scalar(bv_wide[:, i, c, :], ones, bv_col[:, i, c:c + 1], None, ALU.mult)
            last.then_inc(fold_wide, 1)
            for name, gain in (("wk_l1", "g_kv"), ("wv_l1", "g_kv"), ("wq_l3", "g_in"), ("wk_l3", "g_in"),
                               ("wv_l3", "g_in"), ("l3_w1", "g_mlp")):
                for c in range(C):
                    w = pv(name, C)[:, c, :]
                    v.tensor_scalar(w, w, pv(gain)[:, c:c + 1], None, ALU.mult)
            dve.wait_ge(fold_rows, 1)
            for i, name in enumerate(("bo_l1", "bo_l2", "bo_l3")):
                last = v.tensor_tensor(pv(name), (out_psum + work_psum)[i][:, 0, :], pv(name), ALU.add)
            last.then_inc(folded, 1)
            for i in range(WORK):
                dve.sem_inc(work_emptied[i], START)

            with dve.Fori(0, PAIRS) as r:
                def moments(src, key):
                    for t in range(T):
                        v.bn_stats(stats[:, t, :], src[:, t, :])
                    v.drain()
                    for t in range(T):
                        last = v.bn_aggr(mv[:, t, :], stats[:, t, :])
                    last.then_inc(stats_ready, 1)
                    dve.wait_ge(rstd_ready, count(NORM_NO, r, key))

                def layer_norm(src, key, done):
                    moments(src, key)
                    for t in range(T):
                        last = v.tensor_scalar(norm[:, t, :], src[:, t, :], mv[:, t, 0:1], rstd[:, t:t + 1],
                                               ALU.subtract, ALU.mult)
                    last.then_inc(ev[done][key[0]], 1)

                def layer_norm_affine(src, dst, key, gain, bias, done=None):
                    moments(src, key)
                    for t in range(T):
                        v.scalar_tensor_tensor(out=scaled[:, t, :], in0=src[:, t, :], scalar=mv[:, t, 0:1],
                                               in1=pv(gain), op0=ALU.subtract, op1=ALU.mult)
                    v.drain()
                    for t in range(T):
                        last = v.scalar_tensor_tensor(out=dst[:, t, :], in0=scaled[:, t, :],
                                                      scalar=rstd[:, t:t + 1], in1=pv(bias),
                                                      op0=ALU.mult, op1=ALU.add)
                    if done:
                        last.then_inc(ev[done][key[0]], 1)
                    else:
                        v.drain()

                def plus(key, addend, dst):
                    bank, taken = wait_full_work(dve, r, key)
                    v.tensor_tensor(dst, bank[:], addend, ALU.add).then_inc(taken, 1)

                def low(s, l, what):
                    keys = what == "ksplit"
                    pieces, rest, done, ready, no = (
                        (key_pieces, key_rest, key_low, key_high, KSPLIT_NO) if keys
                        else (query_pieces, query_rest, query_low, query_high, QSPLIT_NO))
                    dve.wait_ge(ready, count(no, r, (s, l, what)))
                    if keys and l in ("self", "cross"):
                        v.tensor_tensor(rest[:], (tok_t if l == "self" else ctx_t)[s][:], pieces[:, 0], ALU.subtract)
                    else:
                        bank, taken = wait_full_work(dve, r, (s, l, "keys" if keys else "q"))
                        if l in ("self", "cross"):
                            last = v.tensor_tensor(rest[:], bank[:], pieces[:, 0], ALU.subtract)
                        elif keys and l == "l2":
                            v.tensor_copy(values_l2[s][:, :, 0:HD],
                                          bank[:, 1, 0:T * HD].rearrange("p (t d) -> p t d", t=T))
                            last = v.scalar_tensor_tensor(
                                out=rest[0:HD, 0, :], in0=bank[0:HD, 0, :], scalar=pv("bk_l2")[0:HD, :],
                                in1=pieces[0:HD, 0, 0, :], op0=ALU.add, op1=ALU.subtract)
                        else:
                            bias = pv(("bk_" if keys else "bq_") + l)
                            for c in range(C):
                                last = v.scalar_tensor_tensor(
                                    out=rest[:, c, :], in0=bank[:, c, :], scalar=bias[:, c:c + 1],
                                    in1=pieces[:, 0, c, :], op0=ALU.add, op1=ALU.subtract)
                        last.then_inc(taken, 1)
                    v.drain()
                    part = (slice(0, HD), slice(0, 1)) if keys and l == "l2" else (slice(0, P), slice(0, C))
                    v.tensor_copy(pieces[part[0], 1, part[1], :], rest[part[0], part[1], :]).then_inc(done, 1)
                    v.drain()
                    v.tensor_tensor(pieces[part[0], 2, part[1], :], rest[part[0], part[1], :],
                                    pieces[part[0], 1, part[1], :], ALU.subtract).then_inc(done, 1)
                    v.drain()

                for key in SCHEDULE:
                    s, l, step = key
                    if step[:3] == "max":
                        u = int(step[3:])
                        bank = wait_full_unit(dve, r, key)
                        v.tensor_reduce(neg_max[:, u // 4, :, 2 * (u % 4):2 * (u % 4) + 2], bank[:], AX.X, ALU.max,
                                        negate=True).then_inc(maxed, 1)
                    elif step in ("ksplit", "qsplit"):
                        low(s, l, step)
                    elif step == "ctxln":
                        dve.wait_ge(ev["c_loaded"][s], 16 * r + 16)
                        layer_norm(c_in[s], key, "ctx_norm")
                    elif step in ("mix0", "mix1"):
                        t = int(step[-1])
                        bank, taken = wait_full_work(dve, r, key)
                        slots = flatten(bank[:, :, :]).rearrange("p (h n) -> p h n", h=H)
                        v.reciprocal(recip[:, t, :], slots[:, :, HD])
                        v.drain()
                        for c in range(C):
                            last = v.tensor_tensor(
                                out_tok[:, t, c * P:(c + 1) * P].rearrange("p (d h) -> p h d", h=HC),
                                slots[:, c::C, 0:HD], recip[:, t, c::C].unsqueeze(2).broadcast_to((P, HC, HD)),
                                ALU.mult)
                        last.then_inc(taken, 1)
                    elif step == "v":
                        bank, taken = wait_full_work(dve, r, key)
                        for t in range(T):
                            last = v.tensor_copy(
                                values[s][:, t, :, 0:HD].rearrange("p (c h) d -> p c h d", c=C),
                                bank[:, t, :].rearrange("p (c d h) -> p c h d", c=C, d=HD))
                        last.then_inc(taken, 1)
                    elif step == "proj":
                        if l == "l3":
                            plus(key, row("bo_l2"), attn)
                            continue
                        wait_for = {"cross": "bias_self", "l1": "bias_cross", "l2": "bias_l1", "end": "bias_l3"}[l]
                        dve.wait_ge(ev[wait_for][s], r + 1)
                        plus(key, x_b[s][:], resid[:] if l == "end" else summed[s][:])
                        v.drain()
                    elif step == "ln1":
                        layer_norm_affine(summed[s], resid, key, "ln1_g", "ln1_b", "ln1")
                    elif step == "ln2":
                        layer_norm_affine(summed[s], resid, key, "ln2_g", "ln2_b", "ln2")
                    elif step == "ln3":
                        layer_norm_affine(summed[s], norm, key, "ln3_g", "ln3_b")
                    elif step == "lnq":
                        layer_norm_affine(norm, resid, key, "g_q", "b_q", "lnq")
                    elif step == "hid_out" and l == "l1":
                        dve.wait_ge(ev["bias_ff"][s], r + 1)
                        plus(key, x_b[s][:], summed[s][:])
                        v.drain()
                    elif step == "gate":
                        plus(key, row("bg"), gate_in)
                    elif step == "rms":
                        dve.wait_ge(ev["gate_tanh"][s], r + 1)
                        v.scalar_tensor_tensor(out=gate, in0=gate, scalar=1.0, in1=gate_in, op0=ALU.add, op1=ALU.mult)
                        v.drain()
                        dve.wait_ge(ev["diff"][s], r + 1)
                        v.scalar_tensor_tensor(out=gate, in0=gate, scalar=0.5, in1=diff, op0=ALU.mult, op1=ALU.mult)
                        v.drain()
                        v.tensor_tensor(norm[:], gate, summed[s][:], ALU.add)
                        v.drain()
                        for t in range(T):
                            last = v.tensor_tensor_reduce(gate[:, t, :], norm[:, t, :], norm[:, t, :], 1.0, 0.0,
                                                          ALU.mult, ALU.add, sumsq[:, t:t + 1])
                        last.then_inc(stats_ready, 1)
                        dve.wait_ge(rstd_ready, count(NORM_NO, r, key))
                        for t in range(T):
                            last = v.scalar_tensor_tensor(out=xhat[:, t, :], in0=norm[:, t, :],
                                                          scalar=rstd[:, t:t + 1], in1=pv("rms_w"),
                                                          op0=ALU.mult, op1=ALU.mult)
                        last.then_inc(ev["xhat"][s], 1)
                    elif step == "mean":
                        bank, taken = wait_full_work(dve, r, key)
                        v.tensor_tensor(summed[s][:], xhat[:], bank[:, 0, :].unsqueeze(1).broadcast_to((P, T, E)),
                                        ALU.subtract).then_inc(taken, 1)
                        v.drain()
                    elif step == "lnin":
                        layer_norm(summed[s], key, "lnin")
                    elif step == "lnmlp":
                        layer_norm(resid, key, "lnmlp")
                    elif step == "hid_out" and l == "end":
                        dve.wait_ge(ev["bias_mlp"][s], r + 1)
                        dve.wait_ge(stored, r * (16 * STREAMS) + 16 * (s + 1))
                        plus(key, x_b[s][:], result[:])

        @block.tensor
        def _(pe):
            pe.wait_ge(loaded, 64)
            pe.wait_ge(const_ready, 1)
            for n, l in enumerate(("self", "cross")):
                pe.matmul(unit_psum[0][:, 0, 0, n * P:(n + 1) * P], setup[f"wq_{l}"], setup[f"wk_{l}"],
                          start=True, stop=True)
            pe.matmul(unit_psum[0][:, 1], setup["wv_self"], pv("wo_self", C), start=True, stop=True)
            pe.matmul(unit_psum[1][:, 0], setup["wv_cross"], pv("wo_cross", C), start=True, stop=True)
            sums = flatten(unit_psum[1][:, 1])
            for name, a in BIAS_COLUMNS.items():
                weight, vector = BIAS_SOURCES[name]
                for m in range(AT[name][1]):
                    for c in range(C):
                        last = pe.matmul(sums[:, a + m:a + m + 1], pv(weight, C)[:, c, m * P:(m + 1) * P],
                                         pv(vector)[:, c:c + 1], start=(c == 0), stop=(c == C - 1))
            last.then_inc(fold_products, 1)
            pe.wait_ge(fold_wide, 1)
            for i, name in enumerate(("wo_l1", "wo_l2", "wo_l3")):
                for c in range(C):
                    last = pe.matmul((out_psum + work_psum)[i][:, 0, :], bv_wide[:, i, c, :], pv(name, C)[:, c, :],
                                     start=(c == 0), stop=(c == C - 1))
            last.then_inc(fold_rows, 1)
            pe.wait_ge(folded, 1)
            pe.sem_inc(weighed, START)

            with pe.Fori(0, PAIRS) as r:
                def turn(key, src):
                    bank, filled = wait_free_work(pe, r, key)
                    for c in range(C):
                        for t in range(T):
                            last = pe.transpose(bank[:, c, t * P:(t + 1) * P], src[:, t, c * P:(c + 1) * P], ident[:])
                    last.then_inc(filled, 1)

                def to_features(key, weight, src, column=0):
                    bank, filled = wait_free_work(pe, r, key)
                    for k in range(2):
                        for c in range(C):
                            last = pe.matmul(bank[:, k, :], pv(weight, C)[:, c, column + k * P:column + (k + 1) * P],
                                             src[:, c, :], start=(c == 0), stop=(c == C - 1))
                    last.then_inc(filled, 1)

                def to_tokens(key, parts):
                    bank, filled = wait_free_work(pe, r, key)
                    for t in range(T):
                        for n, (src, weight) in enumerate(parts):
                            last = pe.matmul(bank[:, t, :], src[:, t * P:(t + 1) * P], weight,
                                             start=(n == 0), stop=(n == len(parts) - 1))
                    last.then_inc(filled, 1)

                def dense(src, weight, n=C):
                    return [(src[:, c, :], pv(weight, n)[:, c, :]) for c in range(n)]

                def twice(ap, n):
                    return ap.unsqueeze(1).broadcast_to((P, 2, n))

                def scores_for_max(key):
                    s, l, step = key
                    u = int(step[3:])
                    if u == 0:
                        pe.wait_ge(keys_placed, r * (96 * len(KSPLIT_NO)) + (96 * (KSPLIT_NO[s, l, "ksplit"] + 1) + 16))
                        pe.wait_ge(queries_placed,
                                   r * (96 * len(QSPLIT_NO)) + (96 * (QSPLIT_NO[s, l, "qsplit"] + 1) + 16))
                        if l == "self":
                            pe.wait_ge(ev["negs"][s], r + 1)
                    bank, filled = wait_free_unit(pe, r, key)
                    masked = neg[l][s] if l in neg else None
                    for t in range(T):
                        if masked is not None:
                            pe.matmul(bank[:, t], ident_b[:], twice(masked[:, t, :], S), start=True, stop=False)
                        for i in range(2):
                            h = 2 * u + i
                            last = pe.matmul(bank[:, t, i, :], query_stack[s][0:ROWS, h, t * P:(t + 1) * P],
                                             key_stack[s][0:ROWS, 0 if l == "l2" else h, :],
                                             start=masked is None, stop=masked is None or i == 1)
                    last.then_inc(filled, 1)

                def scores_for_exp(key):
                    s, l, step = key
                    u = int(step[3:])
                    if u % 4 == 0:
                        pe.wait_ge(max_placed, r * (16 * len(TURN_NO)) + 16 * (TURN_NO[s, l, f"turn{u // 4}"] + 1))
                    bank, filled = wait_free_unit(pe, r, key)
                    masked = neg[l][s] if l in neg else None
                    for k in range(T):
                        if masked is not None:
                            for t in range(T):
                                pe.matmul(bank[:, k, :, t * P:(t + 1) * P], masked[:, t, k * P:(k + 1) * P],
                                          twice(ident_b[:], P), start=(t == 0), stop=False)
                        for i in range(2):
                            h = 2 * u + i
                            last = pe.matmul(bank[:, k, i, :],
                                             key_stack[s][0:MAX_ROWS, 0 if l == "l2" else h, k * P:(k + 1) * P],
                                             query_stack[s][0:MAX_ROWS, h, :],
                                             start=masked is None, stop=masked is None or i == 1)
                    last.then_inc(filled, 1)

                def weigh(key):
                    s, l, step = key
                    g = int(step[-1])
                    if g == 0:
                        if l == "self":
                            pe.wait_ge(ev["values_self"][s], r + 1)
                        elif l == "cross":
                            pe.wait_ge(ev["values_cross"][s], r + 1)
                        n = sum(1 for k in SCHEDULE[:SCHEDULE.index(key)] if k[2] == "out")
                        pe.wait_ge(out_taken, r * len(OUT_NO) + (n + START))
                    pe.wait_ge(exped, count(EXP_NO, r, (s, l, f"exp{2 * g + 1}")) + START)
                    for k in range(T):
                        for j in range(NJ):
                            n = EXP_NO[s, l, f"exp{2 * g + j // 2}"]
                            w = values_l2[s][:, k, :] if l == "l2" else values[s][:, k, head_in(NJ * g + j), :]
                            last = pe.matmul(out_psum[g // 2][Q * j:Q * (j + 1), g % 2, :], w,
                                             probs[:, n % PROB_BUFS, k, j % 2, :], start=(k == 0), stop=(k == T - 1))
                    last.then_inc(weighed, 1)

                for key in SCHEDULE:
                    s, l, step = key
                    if step[:3] == "max":
                        scores_for_max(key)
                    elif step[:3] == "exp":
                        scores_for_exp(key)
                    elif step.startswith("weigh"):
                        weigh(key)
                    elif step in ("turn0", "turn1"):
                        a = int(step[-1])
                        pe.wait_ge(max_cut, count(PIECES_NO, r, (s, l, f"pieces{a}")))
                        bank, filled = wait_free_work(pe, r, key)
                        for t in range(T):
                            last = pe.matmul(bank[0:3 * HC, 0, t * P:(t + 1) * P],
                                             max_pieces[:, a, t].rearrange("p i h -> p (i h)"), ident_b[:],
                                             start=True, stop=True)
                        last.then_inc(filled, 1)
                    elif step == "xT":
                        pe.wait_ge(x_loaded, r * (16 * STREAMS) + 16 * (s + 1))
                        turn(key, x_in)
                    elif step == "ctxT":
                        pe.wait_ge(ev["c_loaded"][s], 16 * r + 16)
                        turn(key, c_in[s])
                    elif step == "ctxnT":
                        pe.wait_ge(ev["ctx_norm"][s], r + 1)
                        turn(key, norm)
                    elif step == "keys" and l == "l2":
                        bank, filled = wait_free_work(pe, r, key)
                        for c in range(C):
                            pe.matmul(bank[0:HD, 0, :], pv("wk_l2", C)[:, c, :], ctx_t[s][:, c, :],
                                      start=(c == 0), stop=(c == C - 1))
                        for t in range(T):
                            for c in range(C):
                                last = pe.matmul(bank[:, 1, t * HD:(t + 1) * HD], ctx_t[s][:, c, t * P:(t + 1) * P],
                                                 pv("wv_l2", C)[:, c, :], start=(c == 0), stop=(c == C - 1))
                        last.then_inc(filled, 1)
                    elif step == "keys":
                        if l == "l1":
                            wait_taken(pe, r, (s, "self", "ctxnT"), before=key)
                        to_features(key, f"wk_{l}", ctxn_t[s])
                    elif step == "v":
                        to_tokens(key, dense(ctxn_t[s], f"wv_{l}"))
                    elif step in ("mix0", "mix1"):
                        t = int(step[-1])
                        pe.wait_ge(out_taken, count(OUT_NO, r, (s, l, "out")) + START)
                        bank, filled = wait_free_work(pe, r, key)
                        for g in range(NG):
                            last = pe.transpose(flatten(bank[:])[:, g * P:(g + 1) * P],
                                                out_t[:, g, t * P:(t + 1) * P], ident[:])
                        last.then_inc(filled, 1)
                    elif step == "outT":
                        wait_taken(pe, r, (s, l, "mix0"), (s, l, "mix1"), before=key)
                        turn(key, out_tok)
                    elif step == "proj":
                        wait_taken(pe, r, (s, l, "outT"), before=key)
                        to_tokens(key, dense(turned_t, f"wo_{BEFORE[l]}"))
                    elif step in ("lnT", "lnqT"):
                        if l == "l2":
                            wait_taken(pe, r, (s, l, "proj"), before=key)
                            turn(key, summed[s])
                        else:
                            done, src = {"cross": ("ln1", resid), "l1": ("ln2", resid), "l3": ("lnin", norm),
                                         "end": ("lnmlp", norm)}[l]
                            if step == "lnqT":
                                done = "lnq"
                            pe.wait_ge(ev[done][s], r + 1)
                            turn(key, src)
                    elif step == "q":
                        wait_taken(pe, r, (s, l, {"self": "xT", "l1": "lnqT"}.get(l, "lnT")), before=key)
                        if l in ("self", "cross"):
                            bank, filled = wait_free_work(pe, r, key)
                            for c in range(C):
                                last = pe.matmul(bank[:, c, :], fold[l][:], tok_t[s][:, c, :], start=True, stop=True)
                            last.then_inc(filled, 1)
                        else:
                            to_features(key, f"wq_{l}", tok_t[s])
                    elif step == "hid_out":
                        wait_taken(pe, r, *[(s, l, f"hid{i}") for i in range(FC // 2)], before=key)
                        to_tokens(key, dense(hidden_t, "l0_w2" if l == "l1" else "l3_w2", FC))
                    elif step[:3] == "hid":
                        if step == "hid0":
                            wait_taken(pe, r, (s, l, "lnT"), before=key)
                        to_features(key, "l0_w1" if l == "l1" else "l3_w1", tok_t[s], int(step[-1]) * 2 * P)
                    elif step == "attnT":
                        wait_taken(pe, r, (s, l, "proj"), before=key)
                        turn(key, attn)
                    elif step == "gate":
                        wait_taken(pe, r, (s, l, "attnT"), before=key)
                        w = pv("wg", 2 * C)
                        to_tokens(key, [(turned_t[:, c, :], w[:, c, :]) for c in range(C)]
                                  + [(tok_t[s][:, c, :], w[:, C + c, :]) for c in range(C)])
                    elif step == "mean":
                        pe.wait_ge(ev["xhat"][s], r + 1)
                        bank, filled = wait_free_work(pe, r, key)
                        for t in range(T):
                            last = pe.matmul(bank[:, 0, :], mean_w[:], xhat[:, t, :], start=(t == 0), stop=(t == T - 1))
                        last.then_inc(filled, 1)


def heads_first(w, axis=0):
    w = np.moveaxis(w, axis, 0)
    w = w.reshape((C, HC, HD) + w.shape[1:]).swapaxes(1, 2).reshape(w.shape)
    return np.moveaxis(w, 0, axis)


def pack(i):
    got = {}

    def chunks(w):
        k, n = w.shape
        return w.reshape(k // P, P, n).transpose(1, 0, 2).reshape(P, -1)

    def column(v):
        return v.reshape(-1, P).T


    def rows(v):
        return np.repeat(heads_first(v).reshape(1, -1), P, axis=0)

    def both(w):
        return heads_first(heads_first(w), 1)

    got["wo_self"] = chunks(both(i["L0_xattn_msa_Wo"].T))
    got["wo_cross"] = chunks(both(i["L0_xattn_ca_Wo"].T))
    got["l0_w1"] = chunks(heads_first(i["L0_xattn_ff_W1"].T))
    got["l0_w2"] = chunks(heads_first(i["L0_xattn_ff_W2"].T, 1))
    got["l0_b1"] = column(i["L0_xattn_ff_b1"])
    for n in (1, 2, 3):
        got[f"ln{n}_g"] = rows(i[f"L0_xattn_ln{n}_g"])
        got[f"ln{n}_b"] = rows(i[f"L0_xattn_ln{n}_b"])
    got["bo_self"] = rows(i["L0_xattn_msa_bo"])
    got["bo_cross"] = rows(i["L0_xattn_ca_bo"])
    got["l0_b2"] = rows(i["L0_xattn_ff_b2"])
    L1, L2, L3 = "L1_xattn_", "L2_xattn_", "L3_xattn_"
    got["wq_l1"] = chunks(both(i[L1 + "wq"].T))
    got["wk_l1"] = chunks(both(i[L1 + "wk"].T))
    got["wv_l1"] = chunks(both(i[L1 + "wv"].T))
    got["wo_l1"] = chunks(both(i[L1 + "wo"].T))
    got["bq_l1"] = column(heads_first(i[L1 + "bq"]))
    got["bk_l1"] = column(heads_first(i[L1 + "bk"]))
    got["g_kv"] = column(heads_first(i[L1 + "g_kv"]))
    got["b_kv"] = column(heads_first(i[L1 + "b_kv"]))
    got["bv_l1"] = column(heads_first(i[L1 + "bv"]))
    got["g_q"] = rows(i[L1 + "g_q"])
    got["b_q"] = rows(i[L1 + "b_q"])
    got["bo_l1"] = rows(i[L1 + "bo"])
    got["wq_l2"] = chunks(both(i[L2 + "Wq"]))
    got["wk_l2"] = chunks(heads_first(i[L2 + "Wk"]))
    got["wv_l2"] = chunks(heads_first(i[L2 + "Wv"]))
    got["wo_l2"] = chunks(both(i[L2 + "Wo"]))
    got["wg"] = np.concatenate([chunks(both(w)) for w in (i[L2 + "Wg"][:E], i[L2 + "Wg"][E:])], axis=1)
    got["bq_l2"] = column(heads_first(i[L2 + "bq"]))
    one = np.zeros((P, 1), np.float32)
    one[:HD, 0] = i[L2 + "bk"]
    got["bk_l2"] = one
    got["bv_l2"] = column(heads_first(np.tile(i[L2 + "bv"], H)))
    got["bo_l2"] = rows(i[L2 + "bo"])
    got["bg"] = rows(i[L2 + "bg"])
    got["rms_w"] = rows(i[L2 + "rms_w"])
    got["wq_l3"] = chunks(both(i[L3 + "wq"]))
    got["wk_l3"] = chunks(both(i[L3 + "wk"]))
    got["wv_l3"] = chunks(both(i[L3 + "wv"]))
    got["wo_l3"] = chunks(both(i[L3 + "wo"]))
    got["l3_w1"] = chunks(heads_first(i[L3 + "w1"]))
    got["l3_w2"] = chunks(heads_first(i[L3 + "w2"], 1))
    got["bq_l3"] = column(heads_first(i[L3 + "bq"]))
    got["bk_l3"] = column(heads_first(i[L3 + "bk"]))
    got["g_in"] = column(heads_first(i[L3 + "ln1_g"]))
    got["b_in"] = column(heads_first(i[L3 + "ln1_b"]))
    got["bv_l3"] = column(heads_first(i[L3 + "bv"]))
    got["g_mlp"] = column(heads_first(i[L3 + "ln2_g"]))
    got["b_mlp"] = column(heads_first(i[L3 + "ln2_b"]))
    got["l3_b1"] = column(i[L3 + "b1"])
    got["bo_l3"] = rows(i[L3 + "bo"])
    got["l3_b2"] = rows(i[L3 + "b2"])
    return np.ascontiguousarray(np.concatenate([got[name] for name, _ in PACK], axis=1))


def pack_setup(i):
    blocks = np.zeros((P, len(SETUP), P), np.float32)
    for n, name in enumerate(SETUP):
        w = i["L0_xattn_" + {"self": "msa_W", "cross": "ca_W"}[name[3:]] + name[1]]
        for k in range(HC):
            blocks[k::HC, n, k::HC] = w
    return blocks.reshape(P, -1)


def kernel(**inputs):
    import concourse.bacc as bacc
    from concourse.bass_utils import run_bass_kernel_spmd

    i = {k: np.asarray(v) for k, v in inputs.items()}
    arrays = {
        "in_x": np.ascontiguousarray(heads_first(i["x"], 2)),
        "in_ctx": np.ascontiguousarray(heads_first(i["ctx_1024"], 2)),
        "in_mask_cross": np.ascontiguousarray(i["mask_Bx1xSxS2_if1"]),
        "in_mask_self": np.ascontiguousarray(i["mask_Bx1xSxS2_ik0"]),
        "in_params": pack(i),
        "in_setup": pack_setup(i),
    }
    nc = bacc.Bacc("TRN2", target_bir_lowering=False, num_devices=1)
    args = [nc.dram_tensor(n, a.shape, mybir.dt.from_np(a.dtype), kind="ExternalInput").ap()
            for n, a in arrays.items()]
    args.append(nc.dram_tensor("out", (B, S, E), FP32, kind="ExternalOutput").ap())
    build(nc, *args)
    r = run_bass_kernel_spmd(nc, [arrays], core_ids=[0])
    return r.results[0]["out"].reshape(B, S, C, HD, HC).swapaxes(3, 4).reshape(B, S, E)
```

```python
import concourse.bass as bass
import concourse.mybir as mybir
import numpy as np
from contextlib import ExitStack

FP32 = mybir.dt.float32
BF16 = mybir.dt.bfloat16
I32 = mybir.dt.int32
ALU = mybir.AluOpType
ACT = mybir.ActivationFunctionType
AX = mybir.AxisListType

B, S, E, H, HD, FF = 16, 256, 256, 16, 16, 1024
P = 128
T = S // P
C = E // P
FC = FF // P
HC = P // HD
NG, NJ = 4, 4
Q = 32
STREAMS = 2
PAIRS = B // STREAMS
WINDOW_HALF = 64
MASKED = -float(2 ** 66)
LAYERS = ["self", "cross", "l1", "l2", "l3"]
SCALE = {"self": 1 / 16, "cross": 1 / 16, "l1": 0.25, "l2": 0.25, "l3": 0.25}
EPS = 1e-5
RMS_EPS = 1e-6

QUERY_PIECES = [0, 0, 0, 1, 1, 2]
KEY_PIECES = [0, 1, 2, 0, 1, 0]
ROWS = HD * len(QUERY_PIECES)
MAX_ROWS = ROWS + 3

PACK = [
    ("wo_self", 512), ("wo_cross", 512),
    ("l0_w1", C * FF), ("l0_w2", FC * E), ("l0_b1", FC),
    ("ln1_g", E), ("ln1_b", E), ("ln2_g", E), ("ln2_b", E), ("ln3_g", E), ("ln3_b", E),
    ("bo_self", E), ("bo_cross", E), ("l0_b2", E),
    ("wq_l1", C * E), ("wk_l1", C * E), ("wv_l1", C * E), ("wo_l1", C * E),
    ("bq_l1", C), ("bk_l1", C), ("g_kv", C), ("b_kv", C), ("bv_l1", C),
    ("g_q", E), ("b_q", E), ("bo_l1", E),
    ("wq_l2", C * E), ("wk_l2", C * HD), ("wv_l2", C * HD), ("wo_l2", C * E), ("wg", 2 * C * E),
    ("bq_l2", C), ("bk_l2", 1), ("bv_l2", C), ("bo_l2", E), ("bg", E), ("rms_w", E),
    ("wq_l3", C * E), ("wk_l3", C * E), ("wv_l3", C * E), ("wo_l3", C * E),
    ("l3_w1", C * FF), ("l3_w2", FC * E),
    ("bq_l3", C), ("bk_l3", C), ("g_in", C), ("b_in", C), ("bv_l3", C), ("g_mlp", C), ("b_mlp", C),
    ("l3_b1", FC), ("bo_l3", E), ("l3_b2", E),
]
SETUP = ["wq_self", "wk_self", "wq_cross", "wk_cross", "wv_self", "wv_cross"]
AT = {}
_n = 0
for _name, _w in PACK:
    AT[_name] = (_n, _w)
    _n += _w
PACKED = _n

BIAS_SOURCES = {"bk_l1": ("wk_l1", "b_kv"), "bv_l1": ("wv_l1", "b_kv"), "bq_l3": ("wq_l3", "b_in"),
                "bk_l3": ("wk_l3", "b_in"), "bv_l3": ("wv_l3", "b_in"), "l3_b1": ("l3_w1", "b_mlp")}
BIAS_COLUMNS = {}
_n = 0
for _name in BIAS_SOURCES:
    BIAS_COLUMNS[_name] = _n
    _n += AT[_name][1]
VALUE_BIASES = ["bv_l1", "bv_l2", "bv_l3"]

UNITS = H // 2
UNIT_BUFS = 2
PROB_BUFS = 4
WORK = 2

ATTENTION = (
    [f"max{u}" for u in range(4)] + ["pieces0"] + [f"max{u}" for u in range(4, 6)] + ["turn0", "max6", "max7", "pieces1"]
    + ["exp0", "exp1", "turn1", "exp2", "exp3", "weigh0", "exp4", "exp5", "weigh1", "exp6", "exp7", "out0", "weigh2",
       "weigh3"]
)
DENSE = {
    "cross": ["out1", "ksplit", "mix0", "mix1", "values", "outT", "proj", "ln1", "lnT", "q", "qsplit"],
    "l1": ["out1", "mix0", "mix1", "outT", "proj", "keys", "ln2", "ksplit", "next_c", "lnT",
           "hid0", "hid1", "hid2", "hid3", "hid_out", "v", "ln3", "lnq", "lnqT", "q", "qsplit"],
    "l2": ["out1", "mix0", "mix1", "outT", "proj", "keys", "ksplit", "lnT", "q", "qsplit"],
    "l3": ["out1", "mix0", "mix1", "outT", "proj", "attnT", "gate", "keys", "rms",
           "ksplit", "mean", "v", "lnin", "lnT", "q", "qsplit"],
    "end": ["out1", "mix0", "mix1", "outT", "proj", "+ctxT", "lnmlp", "lnT", "+ctxln",
            "hid0", "hid1", "hid2", "+ctxnT", "hid3", "hid_out", "store", "+inputs", "+xT", "+ksplit", "+q",
            "+next_x", "+qsplit"],
}
WEAVE = {
    "cross": "aadadaadddaaadaddaaadaddaaaaaaaaaaaa",
    "l1": "aaaddddadaddadadadadadadaddadadaadadaddaaaaaaa",
    "l2": "aadaddaadaddadaaaddadaaaaaaaaaaaaaa",
    "l3": "aadddaaddadadadaadddaddaadaaaaddaaaaaaaaa",
    "end": "aaddadaaddaddaadaaadddddadadadaddaddaadaadaaaaa",
}
NORMS = ("ctxln", "ln1", "ln2", "ln3", "lnq", "rms", "lnin", "lnmlp")
THROUGH_WORK = ("xT", "q", "ctxT", "ctxnT", "mix0", "mix1", "outT", "proj", "lnT", "lnqT", "keys", "v",
                "hid0", "hid1", "hid2", "hid3", "hid_out", "attnT", "gate", "mean", "turn0", "turn1")


def attention(s, l):
    return [(s, l, step) for step in ATTENTION]


def dense(s, l):
    return [(s, "self", step[1:]) if step[0] == "+" else (s, l, step) for step in DENSE[l]]


def weave(att, den, pattern):
    att, den = list(att), list(den)
    out = []
    for which in pattern:
        source = att if which == "a" else den
        if source:
            out.append(source.pop(0))
    assert not att and not den
    return out


def round_steps():
    out = []
    for l, after in zip(LAYERS, LAYERS[1:] + ["end"]):
        out += weave(attention(1, l), dense(0, after), WEAVE[after])
        out += weave(attention(0, LAYERS[(LAYERS.index(l) + 1) % len(LAYERS)]), dense(1, after), WEAVE[after])
    return out


SCHEDULE = round_steps()
BEFORE = {l: p for p, l in zip(LAYERS, LAYERS[1:] + ["end"])}


def ahead(key):
    s, l, step = key
    return l == "self" and (s == 0 or step not in ATTENTION)


FIRST = [(s, "self", step[1:]) for s in range(STREAMS) for step in DENSE["end"] if step[0] == "+"] + attention(0, "self")
assert sorted(FIRST) == sorted(k for k in SCHEDULE if ahead(k))


class Numbers:

    def __init__(self, chosen):
        self.keys = [k for k in SCHEDULE if chosen(k[2])]
        self.place = {k: n for n, k in enumerate(self.keys)}
        self.first_keys = [k for k in FIRST if chosen(k[2])]
        self.first_place = {k: n for n, k in enumerate(self.first_keys)}
        self.round = len(self.keys)
        self.first = len(self.first_keys)
        self.start = self.round

    def done(self, r, key, rounds=0, less=0, times=1):
        if r.i is None:
            return times * (self.start + self.first_place[key] + 1 - less)
        return r.value(times * self.round, times * (self.start + self.first + self.place[key] + 1 - less
                                                    + (rounds - ahead(key)) * self.round))

    def position(self, r, key):
        return self.first_place[key] if r.i is None else self.first + self.place[key]

    def buffer_before(self, r, key, buffers):
        if r.i is None:
            n = self.first_place[key] - buffers
            return (self.first_keys[n], 0) if n >= 0 else None
        n = self.place[key] - buffers
        return (self.keys[n], 0) if n >= 0 else (self.keys[n + self.round], -1)

    def done_in_round(self, r, key, back):
        if r.i is None:
            return self.start + self.first_place[key] + 1
        return r.i * self.round + (self.start + self.first + self.place[key] + 1 + back * self.round)


class Round:

    def __init__(self, i, key):
        self.i = i
        self.shift = 1 if i is not None and ahead(key) else 0

    def value(self, per, constant):
        if self.i is None:
            return constant
        return self.i * per + (self.shift * per + constant)


WORK_NO = Numbers(lambda step: step in THROUGH_WORK)
UNIT_NO = Numbers(lambda step: step[:3] in ("max", "exp"))
MAX_NO = Numbers(lambda step: step[:3] == "max")
EXP_NO = Numbers(lambda step: step[:3] == "exp")
WEIGH_NO = Numbers(lambda step: step.startswith("weigh"))
PIECES_NO = Numbers(lambda step: step.startswith("pieces"))
TURN_NO = Numbers(lambda step: step.startswith("turn"))
KSPLIT_NO = Numbers(lambda step: step == "ksplit")
QSPLIT_NO = Numbers(lambda step: step == "qsplit")
OUT_NO = Numbers(lambda step: step == "out1")
NORM_NO = Numbers(lambda step: step in NORMS)
for _n, (_s, _l, _step) in enumerate(WORK_NO.keys[:-WORK]):
    if _step in ("keys", "q"):
        _take = (_s, _l, "ksplit" if _step == "keys" else "qsplit")
        assert SCHEDULE.index(_take) < SCHEDULE.index(WORK_NO.keys[_n + WORK]), _take
for _numbers, _buffers in ((WORK_NO, WORK), (UNIT_NO, UNIT_BUFS), (EXP_NO, PROB_BUFS)):
    assert _numbers.round % _buffers == 0 and _numbers.first % _buffers == 0


def head_in(slot):
    return slot % C * HC + slot // C


def build(nc, x, ctx, mask_cross, mask_self, params, setup_params, out):
    stack = ExitStack()
    with stack:
        def sb(name, shape, dt=FP32):
            return stack.enter_context(nc.sbuf_tensor(name, shape, dt))

        def ps(name, shape, dt=FP32):
            return stack.enter_context(nc.psum_tensor(name, shape, dt))

        def sem(name):
            return stack.enter_context(nc.semaphore(name))

        def each(name, shape, dt=FP32):
            return [sb(f"{name}_{s}", shape, dt) for s in range(STREAMS)]

        par = sb("par", [P, PACKED])

        def pv(name, parts=1):
            a, w = AT[name]
            v = par[:, a:a + w]
            return v if parts == 1 else v.rearrange("p (c n) -> p c n", c=parts)

        def row(name):
            return pv(name).unsqueeze(1).broadcast_to((P, T, E))

        ident = sb("ident", [P, P])
        ident_b = sb("ident_b", [P, P], BF16)
        mean_w = sb("mean_w", [P, P])
        minus_half = sb("minus_half", [P, T])
        neg_band = sb("neg_band", [P, T, S], BF16)
        fold = {l: sb(f"fold_{l}", [P, P]) for l in ("self", "cross")}
        bv_col = sb("bv_col", [P, 3, C])
        c_in = each("c_in", [P, T, E])
        neg = {l: each(f"neg_{l}", [P, T, S], BF16) for l in ("self", "cross")}
        neg["l2"] = [neg_band] * STREAMS
        tok_t = each("tok_t", [P, C, S])
        ctx_t = each("ctx_t", [P, C, S])
        ctxn_t = each("ctxn_t", [P, C, S])
        query_stack = each("query_stack", [P, H, S], BF16)
        key_stack = each("key_stack", [P, H, S], BF16)
        values = each("values", [P, T, H, Q])
        values_l2 = each("values_l2", [P, T, Q])
        x_b = each("x_b", [P, T, E])
        summed = each("summed", [P, T, E])
        x_in = sb("x_in", [P, T, E])
        m_self = sb("m_self", [P, T, S], I32)
        m_cross = sb("m_cross", [P, T, S], I32)
        key_pieces = sb("key_pieces", [P, 3, C, S], BF16)
        query_pieces = sb("query_pieces", [P, 3, C, S], BF16)
        key_rest = sb("key_rest", [P, C, S])
        query_rest = key_rest
        probs = sb("probs", [P, PROB_BUFS, T, 2, S])
        neg_max = sb("neg_max", [P, 2, T, HC])
        max_rest = sb("max_rest", [P, 2, T, HC])
        max_pieces = sb("max_pieces", [P, 2, T, 3, HC], BF16)
        max_rows = sb("max_rows", [3 * HC, 2, S], BF16)
        out_t = sb("out_t", [P, NG, S])
        recip = sb("recip", [P, T, H])
        out_tok = sb("out_tok", [P, T, E])
        turned_t = sb("turned_t", [P, C, S])
        hidden_t = sb("hidden_t", [P, FC, S])
        norm = sb("norm", [P, T, E])
        resid = sb("resid", [P, T, E])
        xhat = sb("xhat", [P, T, E])
        stats = sb("stats", [P, T, 6])
        mv = sb("mv", [P, T, 2])
        sumsq = sb("sumsq", [P, T])
        var_eps = sb("var_eps", [P, T])
        rstd = sb("rstd", [P, T])
        result = sb("result", [P, T, E])
        attn, diff, gate_in, gate = (hidden_t[:, T * i:T * (i + 1), :] for i in range(4))
        scaled = attn
        flat = probs[:].rearrange("p b k i s -> p (b k i s)")
        setup = {name: flat[:, n * P:(n + 1) * P] for n, name in enumerate(SETUP)}
        used = len(SETUP) * P
        bv_wide = flat[:, used:used + 3 * C * P].rearrange("p (i c n) -> p i c n", i=3, c=C)
        used += 3 * C * P
        ones = flat[:, used:used + P]
        used += P
        band = flat[:, used:used + T * S].rearrange("p (t s) -> p t s", t=T)

        unit_psum = [ps(f"unit{i}", [P, T, 2, S]) for i in range(UNIT_BUFS)]
        out_psum = [ps(f"out{a}", [P, 2, S]) for a in range(2)]
        work_psum = [ps(f"work{i}", [P, 2, S]) for i in range(WORK)]

        ev = {n: [sem(f"{n}_{s}") for s in range(STREAMS)] for n in [
            "values_self", "values_cross", "negs", "bias_self", "bias_cross", "bias_ff", "bias_l1", "diff",
            "bias_l3", "bias_mlp", "ctx_norm", "ln1", "ln2", "lnq", "gate_tanh", "xhat", "lnin", "lnmlp",
            "c_loaded"]}
        x_loaded = sem("x_loaded")
        m_loaded = sem("m_loaded")
        stored = sem("stored")
        keys_placed = sem("keys_placed")
        queries_placed = sem("queries_placed")
        max_placed = sem("max_placed")
        unit_filled = [sem(f"unit_filled{i}") for i in range(UNIT_BUFS)]
        work_filled = [sem(f"work_filled{i}") for i in range(WORK)]
        work_emptied = [sem(f"work_emptied{i}") for i in range(WORK)]
        maxed = sem("maxed")
        exped = sem("exped")
        weighed = sem("weighed")
        out_taken = sem("out_taken")
        max_cut = sem("max_cut")
        key_high = sem("key_high")
        key_low = sem("key_low")
        query_high = sem("query_high")
        query_low = sem("query_low")
        stats_ready = sem("stats_ready")
        rstd_ready = sem("rstd_ready")
        const_ready = sem("const_ready")
        sp_waits = sem("sp_waits")
        pool_waits = sem("pool_waits")
        loaded = sem("loaded")
        fold_products = sem("fold_products")
        fold_wide = sem("fold_wide")
        fold_rows = sem("fold_rows")
        folded = sem("folded")
        first_done = sem("first_done")
        met = sem("met")

        def count(numbers, r, key):
            return numbers.done(r, key)

        def unit_buffer(r, key):
            return UNIT_NO.position(r, key) % UNIT_BUFS

        def wait_free_unit(pe, r, key):
            before = UNIT_NO.buffer_before(r, key, UNIT_BUFS)
            if before:
                if before[0][2][:3] == "max":
                    pe.wait_ge(maxed, MAX_NO.done_in_round(r, *before))
                else:
                    pe.wait_ge(exped, EXP_NO.done_in_round(r, *before))
            n = unit_buffer(r, key)
            return unit_psum[n], unit_filled[n]

        def bank_count(numbers, r, key, buffers, rounds=0):
            if r.i is None:
                return numbers.round // buffers + (numbers.first_place[key] // buffers + 1)
            at = numbers.first + numbers.place[key]
            return r.value(numbers.round // buffers, numbers.round // buffers * (1 - ahead(key) + rounds)
                           + (at // buffers + 1))

        def wait_full_unit(eng, r, key):
            n = unit_buffer(r, key)
            eng.wait_ge(unit_filled[n], bank_count(UNIT_NO, r, key, UNIT_BUFS))
            return unit_psum[n]

        def wait_free_work(pe, r, key):
            n = WORK_NO.position(r, key) % WORK
            if WORK_NO.buffer_before(r, key, WORK):
                pe.wait_ge(work_emptied[n], bank_count(WORK_NO, r, key, WORK) - 1)
            return work_psum[n], work_filled[n]

        def wait_full_work(eng, r, key, rounds=0):
            n = WORK_NO.position(r, key) % WORK
            eng.wait_ge(work_filled[n], bank_count(WORK_NO, r, key, WORK, rounds))
            return work_psum[n], work_emptied[n]

        def wait_taken(eng, r, *keys, before=None, rounds=0):
            last = {}
            for key in keys:
                n = WORK_NO.position(r, key)
                if before is None or n % WORK != WORK_NO.position(r, before) % WORK:
                    if n % WORK not in last or n > last[n % WORK][0]:
                        last[n % WORK] = (n, key)
            for i, (_, key) in last.items():
                eng.wait_ge(work_emptied[i], bank_count(WORK_NO, r, key, WORK, rounds))

        def meet(eng):
            eng.sem_inc(first_done, 1)
            eng.wait_ge(first_done, 5)
            eng.sem_inc(met, 1)

        def flatten(t):
            return t.rearrange("p a n -> p (a n)")

        block = stack.enter_context(nc.Block())

        @block.sync
        def _(sp):
            x_tok = x.rearrange("b (t p) e -> b p t e", p=P)
            c_tok = ctx.rearrange("b (t p) e -> b p t e", p=P)
            ms_tok = mask_self.rearrange("b o (t p) k -> (b o) p t k", p=P)
            mc_tok = mask_cross.rearrange("b o (t p) k -> (b o) p t k", p=P)
            o_tok = out.rearrange("b (t p) e -> b p t e", p=P)

            def one(v, b):
                return v[bass.ds(b, 1)].rearrange("o p t e -> p (o t) e")

            def load_x(b):
                sp.dma_start(x_in[:], one(x_tok, b)).then_inc(x_loaded, 16)
                sp.dma_start(m_self[:], one(ms_tok, b)).then_inc(m_loaded, 16)
                sp.dma_start(m_cross[:], one(mc_tok, b)).then_inc(m_loaded, 16)

            def load_c(s, b):
                sp.dma_start(c_in[s][:], one(c_tok, b)).then_inc(ev["c_loaded"][s], 16)

            sp.sem_inc(stored, 16)
            sp.sem_inc(keys_placed, 96 * KSPLIT_NO.start)
            sp.sem_inc(queries_placed, 96 * QSPLIT_NO.start)
            sp.sem_inc(max_placed, 16 * TURN_NO.start)
            load_x(0)
            load_c(0, 0)
            load_c(1, 1)
            sp.dma_start(flat[:, 0:len(SETUP) * P], setup_params).then_inc(loaded, 16)
            cut = [0, PACKED // 3, 2 * PACKED // 3, PACKED]
            for i in range(3):
                sp.dma_start(par[:, cut[i]:cut[i + 1]], params[:, cut[i]:cut[i + 1]]).then_inc(loaded, 16)

            def run(i, keys):
                if i is not None:
                    now = [sp.snap(i * STREAMS + s) for s in range(STREAMS)]
                    later = [sp.snap((i * STREAMS + (STREAMS + a)) % B) for a in range(2 * STREAMS + 1)]

                def wait(s, value):
                    sp.wait_ge(s, value)
                    sp.sem_inc(sp_waits, 1)

                def split(s, l, what):
                    keys = what == "ksplit"
                    pieces, stack_, rows = ((key_pieces, key_stack[s], KEY_PIECES) if keys
                                            else (query_pieces, query_stack[s], QUERY_PIECES))
                    high, low, placed = ((key_high, key_low, keys_placed) if keys
                                         else (query_high, query_low, queries_placed))
                    no = KSPLIT_NO if keys else QSPLIT_NO
                    if l != "self":
                        wait(weighed, WEIGH_NO.done(r, (s, BEFORE[l], "weigh3")))
                    elif i is not None:
                        wait(weighed, WEIGH_NO.done(r, (s, LAYERS[-1], "weigh3"), -1))
                    for piece in range(3):
                        if piece == 0:
                            sp.wait_ge(high, no.done(r, key))
                        else:
                            sp.wait_ge(low, no.done(r, key, times=2) - (2 - piece))
                        for at, which in enumerate(rows):
                            if which != piece:
                                continue
                            dst = stack_[HD * at:HD * (at + 1), :, :]
                            if keys and l == "l2":
                                sp.dma_start(dst[:, 0, :], pieces[0:HD, piece, 0, :]).then_inc(placed, 16)
                            else:
                                sp.dma_start(dst.rearrange("d h n -> d (h n)"),
                                             pieces[:, piece].rearrange("p c n -> p (c n)")).then_inc(placed, 16)

                for key in keys:
                    r = Round(i, key)
                    s, l, step = key
                    if step in ("ksplit", "qsplit"):
                        split(s, l, step)
                    elif step in ("turn0", "turn1"):
                        a = int(step[-1])
                        wait_taken(sp, r, key)
                        sp.dma_start(query_stack[s][ROWS:MAX_ROWS, HC * a:HC * (a + 1), :],
                                     max_rows[:, a, :]).then_inc(max_placed, 16)
                    elif step == "next_x":
                        wait_taken(sp, r, (s, "self", "xT"))
                        sp.sem_inc(sp_waits, 1)
                        wait(ev["negs"][s], r.value(1, 1))
                        if i is None:
                            load_x((s + 1) % B)
                        else:
                            load_x(later[s + 1])
                    elif step == "next_c":
                        wait_taken(sp, r, (s, "self", "ctxT"))
                        sp.sem_inc(sp_waits, 1)
                        wait(ev["ctx_norm"][s], r.value(1, 1))
                        wait(ev["values_cross"][s], r.value(1, 1))
                        load_c(s, later[s])
                    elif step == "store":
                        wait_taken(sp, r, (s, l, "hid_out"))
                        sp.sem_inc(sp_waits, 1)
                        sp.dma_start(one(o_tok, now[s]), result[:]).then_inc(stored, 16)

            run(None, FIRST)
            sp.wait_ge(keys_placed, 96 * (KSPLIT_NO.start + KSPLIT_NO.first))
            sp.wait_ge(queries_placed, 96 * (QSPLIT_NO.start + QSPLIT_NO.first))
            sp.wait_ge(max_placed, 16 * (TURN_NO.start + TURN_NO.first))
            meet(sp)
            with sp.Fori(0, PAIRS) as i:
                run(i, SCHEDULE)
            sp.wait_ge(keys_placed, 96 * (KSPLIT_NO.start + KSPLIT_NO.first + PAIRS * KSPLIT_NO.round))
            sp.wait_ge(queries_placed, 96 * (QSPLIT_NO.start + QSPLIT_NO.first + PAIRS * QSPLIT_NO.round))
            sp.wait_ge(max_placed, 16 * (TURN_NO.start + TURN_NO.first + PAIRS * TURN_NO.round))
            sp.wait_ge(stored, 16 * B + 16)
            sp.wait_ge(x_loaded, 16 * (B + STREAMS + 1))
            sp.wait_ge(m_loaded, 32 * (B + STREAMS + 1))
            for s in range(STREAMS):
                sp.wait_ge(ev["c_loaded"][s], 16 * (PAIRS + 1))

        @block.gpsimd
        def _(pool):
            g = nc.gpsimd
            g.memset(ident[:], 0.0)
            g.memset(ones, 1.0)
            g.memset(mean_w[:], 1.0 / S)
            g.memset(minus_half[:], -0.5)
            g.memset(band, 0.0)
            for s in range(STREAMS):
                g.memset(values[s][:], 1.0)
                g.memset(values_l2[s][:], 1.0)
            g.drain()
            for s in range(STREAMS):
                g.memset(key_stack[s][ROWS:P, :, :], 1.0)
            g.drain()
            g.affine_select(out=ident[:], in_=ident[:], compare_op=ALU.not_equal, fill=1.0, base=0,
                            pattern=[[-1, P]], channel_multiplier=1)
            g.affine_select(out=band, in_=band, compare_op=ALU.is_ge, fill=MASKED, base=WINDOW_HALF,
                            pattern=[[-P, T], [1, S]], channel_multiplier=-1)
            g.drain()
            g.affine_select(out=band, in_=band, compare_op=ALU.is_ge, fill=MASKED, base=WINDOW_HALF,
                            pattern=[[P, T], [-1, S]], channel_multiplier=1)
            g.drain()
            g.tensor_copy(neg_band[:], band)
            g.tensor_copy(ident_b[:], ident[:]).then_inc(const_ready, 1)
            pool.wait_ge(folded, 1)

            pool.sem_inc(rstd_ready, NORM_NO.start)
            pool.sem_inc(max_cut, PIECES_NO.start)

            def run(i, keys):
                def wait(s, value):
                    pool.wait_ge(s, value)
                    pool.sem_inc(pool_waits, 1)

                def wait_step(key):
                    wait_taken(pool, r, key)
                    pool.sem_inc(pool_waits, 1)

                def reciprocal_root(key):
                    wait(stats_ready, count(NORM_NO, r, key))
                    if key[2] == "rms":
                        g.tensor_scalar(var_eps[:], sumsq[:], 1.0 / E, RMS_EPS, ALU.mult, ALU.add)
                    else:
                        g.tensor_scalar(var_eps[:], mv[:, :, 1], EPS, None, ALU.add)
                    g.drain()
                    g.tensor_tensor(rstd[:], var_eps[:], minus_half[:], ALU.pow).then_inc(rstd_ready, 1)

                def spread(dst, src):
                    for t in range(T):
                        last = g.tensor_copy(dst[:, t, :, 0:HD].rearrange("p (c h) d -> p c h d", c=C),
                                             src[:, t, :].rearrange("p (c d h) -> p c h d", c=C, d=HD))
                    return last

                def with_bias(s, src, bias, done):
                    g.tensor_tensor(x_b[s][:], src, row(bias), ALU.add).then_inc(ev[done][s], 1)

                for key in keys:
                    r = Round(i, key)
                    s, l, step = key
                    if step in NORMS:
                        reciprocal_root(key)
                    if step == "inputs":
                        if i is not None:
                            wait(weighed, WEIGH_NO.done(r, (s, LAYERS[-1], "weigh3"), -1))
                        wait(x_loaded, r.value(16 * STREAMS, 16 * (s + 1)))
                        spread(values[s], x_in).then_inc(ev["values_self"][s], 1)
                        if i is not None:
                            wait_taken(pool, r, (s, "end", "hid_out"), rounds=-1)
                            pool.sem_inc(pool_waits, 1)
                        with_bias(s, x_in[:], "bo_self", "bias_self")
                        wait(m_loaded, r.value(32 * STREAMS, 32 * (s + 1)))
                        for name, m in (("self", m_self), ("cross", m_cross)):
                            last = g.tensor_scalar(neg[name][s][:], m[:], 0, MASKED, ALU.is_equal, ALU.mult)
                        last.then_inc(ev["negs"][s], 1)
                    elif step == "values":
                        wait(weighed, count(WEIGH_NO, r, (s, "self", "weigh3")))
                        wait(ev["c_loaded"][s], r.value(16, 16))
                        spread(values[s], c_in[s]).then_inc(ev["values_cross"][s], 1)
                    elif step == "ln1":
                        wait(ev["ln1"][s], r.value(1, 1))
                        with_bias(s, resid[:], "bo_cross", "bias_cross")
                    elif step == "ln2":
                        wait(ev["ln2"][s], r.value(1, 1))
                        with_bias(s, resid[:], "l0_b2", "bias_ff")
                    elif step == "lnq":
                        wait(ev["lnq"][s], r.value(1, 1))
                        with_bias(s, resid[:], "bo_l1", "bias_l1")
                    elif step == "attnT":
                        wait_step((s, l, "proj"))
                        g.tensor_tensor(diff, attn, summed[s][:], ALU.subtract).then_inc(ev["diff"][s], 1)
                    elif step == "mean":
                        wait_step(key)
                        with_bias(s, summed[s][:], "bo_l3", "bias_l3")
                    elif step == "proj" and l == "end":
                        wait_step(key)
                        with_bias(s, resid[:], "l3_b2", "bias_mlp")
                    elif step in ("pieces0", "pieces1"):
                        a = int(step[-1])
                        wait(maxed, count(MAX_NO, r, (s, l, f"max{4 * a + 3}")))
                        for piece in range(3):
                            src = neg_max if piece == 0 else max_rest
                            last = g.tensor_copy(max_pieces[:, a, :, piece, :], src[:, a])
                            if piece < 2:
                                g.drain()
                                g.tensor_tensor(max_rest[:, a], src[:, a], max_pieces[:, a, :, piece, :], ALU.subtract)
                                g.drain()
                        last.then_inc(max_cut, 1)

            run(None, FIRST)
            meet(pool)
            with pool.Fori(0, PAIRS) as i:
                run(i, SCHEDULE)

        @block.scalar
        def _(act):
            a_ = nc.scalar
            act.wait_ge(folded, 1)
            for s, numbers in ((exped, EXP_NO), (out_taken, OUT_NO), (key_high, KSPLIT_NO), (query_high, QSPLIT_NO)):
                act.sem_inc(s, numbers.start)

            def run(i, keys):
                def take(key, dst):
                    bank, taken = wait_full_work(act, r, key)
                    a_.copy(dst[:], bank[:]).then_inc(taken, 1)

                def high(s, l, what):
                    of_keys = what == "ksplit"
                    pieces, done, placed, no = ((key_pieces, key_high, keys_placed, KSPLIT_NO) if of_keys
                                                else (query_pieces, query_high, queries_placed, QSPLIT_NO))
                    act.wait_ge(placed, no.done(r, key, less=1, times=96))
                    dst = pieces[:, 0]
                    if of_keys and l in ("self", "cross"):
                        src = (tok_t if l == "self" else ctx_t)[s]
                        wait_taken(act, r, (s, "self", "xT" if l == "self" else "ctxT"))
                        last = a_.copy(dst, src[:])
                    else:
                        bank, _ = wait_full_work(act, r, (s, l, "keys" if of_keys else "q"))
                        if l in ("self", "cross"):
                            last = a_.copy(dst, bank[:])
                        elif of_keys and l == "l2":
                            last = a_.activation(dst[0:HD, 0, :], bank[0:HD, 0, :], ACT.Identity,
                                                 bias=pv("bk_l2")[0:HD, :])
                        else:
                            bias = pv(("bk_" if of_keys else "bq_") + l)
                            for c in range(C):
                                last = a_.activation(dst[:, c, :], bank[:, c, :], ACT.Identity, bias=bias[:, c:c + 1])
                    last.then_inc(done, 1)

                for key in keys:
                    r = Round(i, key)
                    s, l, step = key
                    if step[:3] == "exp":
                        n = EXP_NO.position(r, key)
                        bank = wait_full_unit(act, r, key)
                        before = EXP_NO.buffer_before(r, key, PROB_BUFS)
                        if before:
                            (bs, bl, bstep), back = before
                            act.wait_ge(weighed, WEIGH_NO.done_in_round(r, (bs, bl, f"weigh{int(bstep[3:]) // 2}"), back))
                        a_.activation(probs[:, n % PROB_BUFS], bank[:], ACT.Exp, scale=SCALE[l]).then_inc(exped, 1)
                    elif step in ("turn0", "turn1"):
                        bank, taken = wait_full_work(act, r, key)
                        a_.copy(max_rows[:, int(step[-1]), :], bank[0:3 * HC, 0, :]).then_inc(taken, 1)
                    elif step == "out0":
                        act.wait_ge(weighed, count(WEIGH_NO, r, (s, l, "weigh1")))
                        a_.copy(out_t[:, 0:2, :], out_psum[0][:])
                    elif step == "out1":
                        act.wait_ge(weighed, count(WEIGH_NO, r, (s, BEFORE[l], "weigh3")))
                        a_.copy(out_t[:, 2:4, :], out_psum[1][:]).then_inc(out_taken, 1)
                    elif step in ("ksplit", "qsplit"):
                        high(s, l, step)
                    elif step in ("xT", "lnT", "lnqT"):
                        take(key, tok_t[s])
                    elif step == "ctxT":
                        take(key, ctx_t[s])
                    elif step == "ctxnT":
                        take(key, ctxn_t[s])
                    elif step in ("outT", "attnT"):
                        take(key, turned_t)
                    elif step[:3] == "hid" and step != "hid_out":
                        bank, taken = wait_full_work(act, r, key)
                        func, bias = (ACT.Relu, "l0_b1") if l == "l1" else (ACT.Gelu, "l3_b1")
                        for k in range(2):
                            f = 2 * int(step[-1]) + k
                            last = a_.activation(hidden_t[:, f, :], bank[:, k, :], func, bias=pv(bias)[:, f:f + 1])
                        last.then_inc(taken, 1)
                    elif step == "rms":
                        wait_taken(act, r, (s, l, "gate"))
                        a_.activation(gate, gate_in, ACT.Tanh, scale=0.5).then_inc(ev["gate_tanh"][s], 1)
                    elif step == "v":
                        bank, taken = wait_full_work(act, r, key)
                        for t in range(T):
                            last = a_.copy(values[s][:, t, :, 0:HD].rearrange("p (c h) d -> p c h d", c=C),
                                           bank[:, t, :].rearrange("p (c d h) -> p c h d", c=C, d=HD))
                        last.then_inc(taken, 1)

            run(None, FIRST)
            meet(act)
            with act.Fori(0, PAIRS) as i:
                run(i, SCHEDULE)

        @block.vector
        def _(dve):
            v = nc.vector
            dve.wait_ge(loaded, 64)
            dve.wait_ge(const_ready, 1)
            dve.wait_ge(fold_products, 1)
            v.tensor_copy(fold["self"][:], unit_psum[0][:, 0, 0, 0:P])
            v.tensor_copy(fold["cross"][:], unit_psum[0][:, 0, 0, P:2 * P])
            v.tensor_copy(pv("wo_self", C), unit_psum[0][:, 1])
            v.tensor_copy(pv("wo_cross", C), unit_psum[1][:, 0])
            sums = flatten(unit_psum[1][:, 1])
            for name, a in BIAS_COLUMNS.items():
                w = AT[name][1]
                dst = bv_col[:, VALUE_BIASES.index(name), :] if name in VALUE_BIASES else pv(name)
                v.tensor_tensor(dst, sums[:, a:a + w], pv(name), ALU.add)
            v.tensor_copy(bv_col[:, 1, :], pv("bv_l2"))
            v.drain()
            for i in range(3):
                for c in range(C):
                    last = v.tensor_scalar(bv_wide[:, i, c, :], ones, bv_col[:, i, c:c + 1], None, ALU.mult)
            last.then_inc(fold_wide, 1)
            for name, gain in (("wk_l1", "g_kv"), ("wv_l1", "g_kv"), ("wq_l3", "g_in"), ("wk_l3", "g_in"),
                               ("wv_l3", "g_in"), ("l3_w1", "g_mlp")):
                for c in range(C):
                    w = pv(name, C)[:, c, :]
                    v.tensor_scalar(w, w, pv(gain)[:, c:c + 1], None, ALU.mult)
            dve.wait_ge(fold_rows, 1)
            for i, name in enumerate(("bo_l1", "bo_l2", "bo_l3")):
                last = v.tensor_tensor(pv(name), (out_psum + work_psum)[i][:, 0, :], pv(name), ALU.add)
            last.then_inc(folded, 1)
            for i in range(WORK):
                dve.sem_inc(work_emptied[i], WORK_NO.start // WORK)
            for s, n in ((maxed, MAX_NO.start), (stats_ready, NORM_NO.start), (key_low, 2 * KSPLIT_NO.start),
                         (query_low, 2 * QSPLIT_NO.start)):
                dve.sem_inc(s, n)

            def run(i, keys):
                def moments(src):
                    for t in range(T):
                        v.bn_stats(stats[:, t, :], src[:, t, :])
                    v.drain()
                    for t in range(T):
                        last = v.bn_aggr(mv[:, t, :], stats[:, t, :])
                    last.then_inc(stats_ready, 1)

                def layer_norm(src, key, done):
                    moments(src)
                    dve.wait_ge(rstd_ready, count(NORM_NO, r, key))
                    for t in range(T):
                        last = v.tensor_scalar(norm[:, t, :], src[:, t, :], mv[:, t, 0:1], rstd[:, t:t + 1],
                                               ALU.subtract, ALU.mult)
                    last.then_inc(ev[done][key[0]], 1)

                def layer_norm_affine(src, dst, key, gain, bias, done=None):
                    moments(src)
                    v.drain()
                    for t in range(T):
                        v.scalar_tensor_tensor(out=scaled[:, t, :], in0=src[:, t, :], scalar=mv[:, t, 0:1],
                                               in1=pv(gain), op0=ALU.subtract, op1=ALU.mult)
                    v.drain()
                    dve.wait_ge(rstd_ready, count(NORM_NO, r, key))
                    for t in range(T):
                        last = v.scalar_tensor_tensor(out=dst[:, t, :], in0=scaled[:, t, :],
                                                      scalar=rstd[:, t:t + 1], in1=pv(bias),
                                                      op0=ALU.mult, op1=ALU.add)
                    if done:
                        last.then_inc(ev[done][key[0]], 1)
                    else:
                        v.drain()

                def plus(key, addend, dst):
                    bank, taken = wait_full_work(dve, r, key)
                    v.tensor_tensor(dst, bank[:], addend, ALU.add).then_inc(taken, 1)

                def low(s, l, what):
                    of_keys = what == "ksplit"
                    pieces, rest, done, ready, no = (
                        (key_pieces, key_rest, key_low, key_high, KSPLIT_NO) if of_keys
                        else (query_pieces, query_rest, query_low, query_high, QSPLIT_NO))
                    dve.wait_ge(ready, count(no, r, (s, l, what)))
                    if of_keys and l in ("self", "cross"):
                        v.tensor_tensor(rest[:], (tok_t if l == "self" else ctx_t)[s][:], pieces[:, 0], ALU.subtract)
                    else:
                        bank, taken = wait_full_work(dve, r, (s, l, "keys" if of_keys else "q"))
                        if l in ("self", "cross"):
                            last = v.tensor_tensor(rest[:], bank[:], pieces[:, 0], ALU.subtract)
                        elif of_keys and l == "l2":
                            v.tensor_copy(values_l2[s][:, :, 0:HD],
                                          bank[:, 1, 0:T * HD].rearrange("p (t d) -> p t d", t=T))
                            last = v.scalar_tensor_tensor(
                                out=rest[0:HD, 0, :], in0=bank[0:HD, 0, :], scalar=pv("bk_l2")[0:HD, :],
                                in1=pieces[0:HD, 0, 0, :], op0=ALU.add, op1=ALU.subtract)
                        else:
                            bias = pv(("bk_" if of_keys else "bq_") + l)
                            for c in range(C):
                                last = v.scalar_tensor_tensor(
                                    out=rest[:, c, :], in0=bank[:, c, :], scalar=bias[:, c:c + 1],
                                    in1=pieces[:, 0, c, :], op0=ALU.add, op1=ALU.subtract)
                        last.then_inc(taken, 1)
                    v.drain()
                    part = (slice(0, HD), slice(0, 1)) if of_keys and l == "l2" else (slice(0, P), slice(0, C))
                    v.tensor_copy(pieces[part[0], 1, part[1], :], rest[part[0], part[1], :]).then_inc(done, 1)
                    v.drain()
                    v.tensor_tensor(pieces[part[0], 2, part[1], :], rest[part[0], part[1], :],
                                    pieces[part[0], 1, part[1], :], ALU.subtract).then_inc(done, 1)
                    v.drain()

                for key in keys:
                    r = Round(i, key)
                    s, l, step = key
                    if step[:3] == "max":
                        u = int(step[3:])
                        bank = wait_full_unit(dve, r, key)
                        v.tensor_reduce(neg_max[:, u // 4, :, 2 * (u % 4):2 * (u % 4) + 2], bank[:], AX.X, ALU.max,
                                        negate=True).then_inc(maxed, 1)
                    elif step in ("ksplit", "qsplit"):
                        low(s, l, step)
                    elif step == "ctxln":
                        if i is None and s:
                            wait_full_work(dve, r, (0, "self", "ctxnT"))
                        elif i is not None:
                            wait_full_work(dve, r, (s, "end", "lnT"), rounds=-1)
                        dve.wait_ge(ev["c_loaded"][s], r.value(16, 16))
                        layer_norm(c_in[s], key, "ctx_norm")
                    elif step in ("mix0", "mix1"):
                        t = int(step[-1])
                        bank, taken = wait_full_work(dve, r, key)
                        slots = flatten(bank[:, :, :]).rearrange("p (h n) -> p h n", h=H)
                        v.reciprocal(recip[:, t, :], slots[:, :, HD])
                        v.drain()
                        for c in range(C):
                            last = v.tensor_tensor(
                                out_tok[:, t, c * P:(c + 1) * P].rearrange("p (d h) -> p h d", h=HC),
                                slots[:, c::C, 0:HD], recip[:, t, c::C].unsqueeze(2).broadcast_to((P, HC, HD)),
                                ALU.mult)
                        last.then_inc(taken, 1)
                    elif step == "proj":
                        if l == "l3":
                            plus(key, row("bo_l2"), attn)
                            continue
                        wait_for = {"cross": "bias_self", "l1": "bias_cross", "l2": "bias_l1", "end": "bias_l3"}[l]
                        dve.wait_ge(ev[wait_for][s], r.value(1, 1))
                        plus(key, x_b[s][:], resid[:] if l == "end" else summed[s][:])
                        v.drain()
                    elif step == "ln1":
                        layer_norm_affine(summed[s], resid, key, "ln1_g", "ln1_b", "ln1")
                    elif step == "ln2":
                        layer_norm_affine(summed[s], resid, key, "ln2_g", "ln2_b", "ln2")
                    elif step == "ln3":
                        layer_norm_affine(summed[s], norm, key, "ln3_g", "ln3_b")
                    elif step == "lnq":
                        layer_norm_affine(norm, resid, key, "g_q", "b_q", "lnq")
                    elif step == "hid_out" and l == "l1":
                        dve.wait_ge(ev["bias_ff"][s], r.value(1, 1))
                        plus(key, x_b[s][:], summed[s][:])
                        v.drain()
                    elif step == "gate":
                        plus(key, row("bg"), gate_in)
                    elif step == "rms":
                        dve.wait_ge(ev["gate_tanh"][s], r.value(1, 1))
                        v.scalar_tensor_tensor(out=gate, in0=gate, scalar=1.0, in1=gate_in, op0=ALU.add, op1=ALU.mult)
                        v.drain()
                        dve.wait_ge(ev["diff"][s], r.value(1, 1))
                        v.scalar_tensor_tensor(out=gate, in0=gate, scalar=0.5, in1=diff, op0=ALU.mult, op1=ALU.mult)
                        v.drain()
                        v.tensor_tensor(norm[:], gate, summed[s][:], ALU.add)
                        v.drain()
                        for t in range(T):
                            last = v.tensor_tensor_reduce(gate[:, t, :], norm[:, t, :], norm[:, t, :], 1.0, 0.0,
                                                          ALU.mult, ALU.add, sumsq[:, t:t + 1])
                        last.then_inc(stats_ready, 1)
                        dve.wait_ge(rstd_ready, count(NORM_NO, r, key))
                        for t in range(T):
                            last = v.scalar_tensor_tensor(out=xhat[:, t, :], in0=norm[:, t, :],
                                                          scalar=rstd[:, t:t + 1], in1=pv("rms_w"),
                                                          op0=ALU.mult, op1=ALU.mult)
                        last.then_inc(ev["xhat"][s], 1)
                    elif step == "mean":
                        bank, taken = wait_full_work(dve, r, key)
                        v.tensor_tensor(summed[s][:], xhat[:], bank[:, 0, :].unsqueeze(1).broadcast_to((P, T, E)),
                                        ALU.subtract).then_inc(taken, 1)
                        v.drain()
                    elif step == "lnin":
                        layer_norm(summed[s], key, "lnin")
                    elif step == "lnmlp":
                        layer_norm(resid, key, "lnmlp")
                    elif step == "hid_out" and l == "end":
                        dve.wait_ge(ev["bias_mlp"][s], r.value(1, 1))
                        dve.wait_ge(stored, r.value(16 * STREAMS, 16 * (s + 1)))
                        plus(key, x_b[s][:], result[:])

            run(None, FIRST)
            meet(dve)
            with dve.Fori(0, PAIRS) as i:
                run(i, SCHEDULE)

        @block.tensor
        def _(pe):
            pe.wait_ge(loaded, 64)
            pe.wait_ge(const_ready, 1)
            for n, l in enumerate(("self", "cross")):
                pe.matmul(unit_psum[0][:, 0, 0, n * P:(n + 1) * P], setup[f"wq_{l}"], setup[f"wk_{l}"],
                          start=True, stop=True)
            pe.matmul(unit_psum[0][:, 1], setup["wv_self"], pv("wo_self", C), start=True, stop=True)
            pe.matmul(unit_psum[1][:, 0], setup["wv_cross"], pv("wo_cross", C), start=True, stop=True)
            sums = flatten(unit_psum[1][:, 1])
            for name, a in BIAS_COLUMNS.items():
                weight, vector = BIAS_SOURCES[name]
                for m in range(AT[name][1]):
                    for c in range(C):
                        last = pe.matmul(sums[:, a + m:a + m + 1], pv(weight, C)[:, c, m * P:(m + 1) * P],
                                         pv(vector)[:, c:c + 1], start=(c == 0), stop=(c == C - 1))
            last.then_inc(fold_products, 1)
            pe.wait_ge(fold_wide, 1)
            for i, name in enumerate(("wo_l1", "wo_l2", "wo_l3")):
                for c in range(C):
                    last = pe.matmul((out_psum + work_psum)[i][:, 0, :], bv_wide[:, i, c, :], pv(name, C)[:, c, :],
                                     start=(c == 0), stop=(c == C - 1))
            last.then_inc(fold_rows, 1)
            pe.wait_ge(folded, 1)
            pe.sem_inc(weighed, WEIGH_NO.start)
            for n in range(UNIT_BUFS):
                pe.sem_inc(unit_filled[n], UNIT_NO.start // UNIT_BUFS)
            for n in range(WORK):
                pe.sem_inc(work_filled[n], WORK_NO.start // WORK)

            def run(i, keys):
                def turn(key, src):
                    bank, filled = wait_free_work(pe, r, key)
                    for c in range(C):
                        for t in range(T):
                            last = pe.transpose(bank[:, c, t * P:(t + 1) * P], src[:, t, c * P:(c + 1) * P], ident[:])
                    last.then_inc(filled, 1)

                def to_features(key, weight, src, column=0):
                    bank, filled = wait_free_work(pe, r, key)
                    for k in range(2):
                        for c in range(C):
                            last = pe.matmul(bank[:, k, :], pv(weight, C)[:, c, column + k * P:column + (k + 1) * P],
                                             src[:, c, :], start=(c == 0), stop=(c == C - 1))
                    last.then_inc(filled, 1)

                def to_tokens(key, parts):
                    bank, filled = wait_free_work(pe, r, key)
                    for t in range(T):
                        for n, (src, weight) in enumerate(parts):
                            last = pe.matmul(bank[:, t, :], src[:, t * P:(t + 1) * P], weight,
                                             start=(n == 0), stop=(n == len(parts) - 1))
                    last.then_inc(filled, 1)

                def dense(src, weight, n=C):
                    return [(src[:, c, :], pv(weight, n)[:, c, :]) for c in range(n)]

                def twice(ap, n):
                    return ap.unsqueeze(1).broadcast_to((P, 2, n))

                def scores_for_max(key):
                    s, l, step = key
                    u = int(step[3:])
                    if u == 0:
                        pe.wait_ge(keys_placed, KSPLIT_NO.done(r, (s, l, "ksplit"), times=96))
                        pe.wait_ge(queries_placed, QSPLIT_NO.done(r, (s, l, "qsplit"), times=96))
                        if l == "self":
                            pe.wait_ge(ev["negs"][s], r.value(1, 1))
                    bank, filled = wait_free_unit(pe, r, key)
                    masked = neg[l][s] if l in neg else None
                    for t in range(T):
                        if masked is not None:
                            pe.matmul(bank[:, t], ident_b[:], twice(masked[:, t, :], S), start=True, stop=False)
                        for i in range(2):
                            h = 2 * u + i
                            last = pe.matmul(bank[:, t, i, :], query_stack[s][0:ROWS, h, t * P:(t + 1) * P],
                                             key_stack[s][0:ROWS, 0 if l == "l2" else h, :],
                                             start=masked is None, stop=masked is None or i == 1)
                    last.then_inc(filled, 1)

                def scores_for_exp(key):
                    s, l, step = key
                    u = int(step[3:])
                    if u % 4 == 0:
                        pe.wait_ge(max_placed, TURN_NO.done(r, (s, l, f"turn{u // 4}"), times=16))
                    bank, filled = wait_free_unit(pe, r, key)
                    masked = neg[l][s] if l in neg else None
                    for k in range(T):
                        if masked is not None:
                            for t in range(T):
                                pe.matmul(bank[:, k, :, t * P:(t + 1) * P], masked[:, t, k * P:(k + 1) * P],
                                          twice(ident_b[:], P), start=(t == 0), stop=False)
                        for i in range(2):
                            h = 2 * u + i
                            last = pe.matmul(bank[:, k, i, :],
                                             key_stack[s][0:MAX_ROWS, 0 if l == "l2" else h, k * P:(k + 1) * P],
                                             query_stack[s][0:MAX_ROWS, h, :],
                                             start=masked is None, stop=masked is None or i == 1)
                    last.then_inc(filled, 1)

                def weigh(key):
                    s, l, step = key
                    g = int(step[-1])
                    if g == 0:
                        if l == "self":
                            pe.wait_ge(ev["values_self"][s], r.value(1, 1))
                        elif l == "cross":
                            pe.wait_ge(ev["values_cross"][s], r.value(1, 1))
                        if i is not None:
                            outs = sum(1 for k in SCHEDULE[:SCHEDULE.index(key)] if k[2] == "out1")
                            pe.wait_ge(out_taken, i * OUT_NO.round + (OUT_NO.start + outs))
                    pe.wait_ge(exped, count(EXP_NO, r, (s, l, f"exp{2 * g + 1}")))
                    for k in range(T):
                        for j in range(NJ):
                            n = EXP_NO.position(r, (s, l, f"exp{2 * g + j // 2}"))
                            w = values_l2[s][:, k, :] if l == "l2" else values[s][:, k, head_in(NJ * g + j), :]
                            last = pe.matmul(out_psum[g // 2][Q * j:Q * (j + 1), g % 2, :], w,
                                             probs[:, n % PROB_BUFS, k, j % 2, :], start=(k == 0), stop=(k == T - 1))
                    last.then_inc(weighed, 1)

                for key in keys:
                    r = Round(i, key)
                    s, l, step = key
                    if step[:3] == "max":
                        scores_for_max(key)
                    elif step[:3] == "exp":
                        scores_for_exp(key)
                    elif step.startswith("weigh"):
                        weigh(key)
                    elif step in ("turn0", "turn1"):
                        a = int(step[-1])
                        pe.wait_ge(max_cut, count(PIECES_NO, r, (s, l, f"pieces{a}")))
                        bank, filled = wait_free_work(pe, r, key)
                        for t in range(T):
                            last = pe.matmul(bank[0:3 * HC, 0, t * P:(t + 1) * P],
                                             max_pieces[:, a, t].rearrange("p i h -> p (i h)"), ident_b[:],
                                             start=True, stop=True)
                        last.then_inc(filled, 1)
                    elif step == "xT":
                        pe.wait_ge(x_loaded, r.value(16 * STREAMS, 16 * (s + 1)))
                        turn(key, x_in)
                    elif step == "ctxT":
                        pe.wait_ge(ev["c_loaded"][s], r.value(16, 16))
                        turn(key, c_in[s])
                    elif step == "ctxnT":
                        pe.wait_ge(ev["ctx_norm"][s], r.value(1, 1))
                        turn(key, norm)
                    elif step == "keys" and l == "l2":
                        bank, filled = wait_free_work(pe, r, key)
                        for c in range(C):
                            pe.matmul(bank[0:HD, 0, :], pv("wk_l2", C)[:, c, :], ctx_t[s][:, c, :],
                                      start=(c == 0), stop=(c == C - 1))
                        for t in range(T):
                            for c in range(C):
                                last = pe.matmul(bank[:, 1, t * HD:(t + 1) * HD], ctx_t[s][:, c, t * P:(t + 1) * P],
                                                 pv("wv_l2", C)[:, c, :], start=(c == 0), stop=(c == C - 1))
                        last.then_inc(filled, 1)
                    elif step == "keys":
                        if l == "l1":
                            wait_taken(pe, r, (s, "self", "ctxnT"), before=key)
                        to_features(key, f"wk_{l}", ctxn_t[s])
                    elif step == "v":
                        to_tokens(key, dense(ctxn_t[s], f"wv_{l}"))
                    elif step in ("mix0", "mix1"):
                        t = int(step[-1])
                        pe.wait_ge(out_taken, count(OUT_NO, r, (s, l, "out1")))
                        bank, filled = wait_free_work(pe, r, key)
                        for g in range(NG):
                            last = pe.transpose(flatten(bank[:])[:, g * P:(g + 1) * P],
                                                out_t[:, g, t * P:(t + 1) * P], ident[:])
                        last.then_inc(filled, 1)
                    elif step == "outT":
                        wait_taken(pe, r, (s, l, "mix0"), (s, l, "mix1"), before=key)
                        turn(key, out_tok)
                    elif step == "proj":
                        wait_taken(pe, r, (s, l, "outT"), before=key)
                        to_tokens(key, dense(turned_t, f"wo_{BEFORE[l]}"))
                    elif step in ("lnT", "lnqT"):
                        if l == "l2":
                            wait_taken(pe, r, (s, l, "proj"), before=key)
                            turn(key, summed[s])
                        else:
                            done, src = {"cross": ("ln1", resid), "l1": ("ln2", resid), "l3": ("lnin", norm),
                                         "end": ("lnmlp", norm)}[l]
                            if step == "lnqT":
                                done = "lnq"
                            pe.wait_ge(ev[done][s], r.value(1, 1))
                            turn(key, src)
                    elif step == "q":
                        wait_taken(pe, r, (s, l, {"self": "xT", "l1": "lnqT"}.get(l, "lnT")), before=key)
                        if l in ("self", "cross"):
                            bank, filled = wait_free_work(pe, r, key)
                            for c in range(C):
                                last = pe.matmul(bank[:, c, :], fold[l][:], tok_t[s][:, c, :], start=True, stop=True)
                            last.then_inc(filled, 1)
                        else:
                            to_features(key, f"wq_{l}", tok_t[s])
                    elif step == "hid_out":
                        wait_taken(pe, r, *[(s, l, f"hid{i}") for i in range(FC // 2)], before=key)
                        to_tokens(key, dense(hidden_t, "l0_w2" if l == "l1" else "l3_w2", FC))
                    elif step[:3] == "hid":
                        if step == "hid0":
                            wait_taken(pe, r, (s, l, "lnT"), before=key)
                        to_features(key, "l0_w1" if l == "l1" else "l3_w1", tok_t[s], int(step[-1]) * 2 * P)
                    elif step == "attnT":
                        wait_taken(pe, r, (s, l, "proj"), before=key)
                        turn(key, attn)
                    elif step == "gate":
                        wait_taken(pe, r, (s, l, "attnT"), before=key)
                        w = pv("wg", 2 * C)
                        to_tokens(key, [(turned_t[:, c, :], w[:, c, :]) for c in range(C)]
                                  + [(tok_t[s][:, c, :], w[:, C + c, :]) for c in range(C)])
                    elif step == "mean":
                        pe.wait_ge(ev["xhat"][s], r.value(1, 1))
                        bank, filled = wait_free_work(pe, r, key)
                        for t in range(T):
                            last = pe.matmul(bank[:, 0, :], mean_w[:], xhat[:, t, :], start=(t == 0), stop=(t == T - 1))
                        last.then_inc(filled, 1)

            run(None, FIRST)
            meet(pe)
            with pe.Fori(0, PAIRS) as i:
                run(i, SCHEDULE)


def heads_first(w, axis=0):
    w = np.moveaxis(w, axis, 0)
    w = w.reshape((C, HC, HD) + w.shape[1:]).swapaxes(1, 2).reshape(w.shape)
    return np.moveaxis(w, 0, axis)


def pack(i):
    got = {}

    def chunks(w):
        k, n = w.shape
        return w.reshape(k // P, P, n).transpose(1, 0, 2).reshape(P, -1)

    def column(v):
        return v.reshape(-1, P).T


    def rows(v):
        return np.repeat(heads_first(v).reshape(1, -1), P, axis=0)

    def both(w):
        return heads_first(heads_first(w), 1)

    got["wo_self"] = chunks(both(i["L0_xattn_msa_Wo"].T))
    got["wo_cross"] = chunks(both(i["L0_xattn_ca_Wo"].T))
    got["l0_w1"] = chunks(heads_first(i["L0_xattn_ff_W1"].T))
    got["l0_w2"] = chunks(heads_first(i["L0_xattn_ff_W2"].T, 1))
    got["l0_b1"] = column(i["L0_xattn_ff_b1"])
    for n in (1, 2, 3):
        got[f"ln{n}_g"] = rows(i[f"L0_xattn_ln{n}_g"])
        got[f"ln{n}_b"] = rows(i[f"L0_xattn_ln{n}_b"])
    got["bo_self"] = rows(i["L0_xattn_msa_bo"])
    got["bo_cross"] = rows(i["L0_xattn_ca_bo"])
    got["l0_b2"] = rows(i["L0_xattn_ff_b2"])
    L1, L2, L3 = "L1_xattn_", "L2_xattn_", "L3_xattn_"
    got["wq_l1"] = chunks(both(i[L1 + "wq"].T))
    got["wk_l1"] = chunks(both(i[L1 + "wk"].T))
    got["wv_l1"] = chunks(both(i[L1 + "wv"].T))
    got["wo_l1"] = chunks(both(i[L1 + "wo"].T))
    got["bq_l1"] = column(heads_first(i[L1 + "bq"]))
    got["bk_l1"] = column(heads_first(i[L1 + "bk"]))
    got["g_kv"] = column(heads_first(i[L1 + "g_kv"]))
    got["b_kv"] = column(heads_first(i[L1 + "b_kv"]))
    got["bv_l1"] = column(heads_first(i[L1 + "bv"]))
    got["g_q"] = rows(i[L1 + "g_q"])
    got["b_q"] = rows(i[L1 + "b_q"])
    got["bo_l1"] = rows(i[L1 + "bo"])
    got["wq_l2"] = chunks(both(i[L2 + "Wq"]))
    got["wk_l2"] = chunks(heads_first(i[L2 + "Wk"]))
    got["wv_l2"] = chunks(heads_first(i[L2 + "Wv"]))
    got["wo_l2"] = chunks(both(i[L2 + "Wo"]))
    got["wg"] = np.concatenate([chunks(both(w)) for w in (i[L2 + "Wg"][:E], i[L2 + "Wg"][E:])], axis=1)
    got["bq_l2"] = column(heads_first(i[L2 + "bq"]))
    one = np.zeros((P, 1), np.float32)
    one[:HD, 0] = i[L2 + "bk"]
    got["bk_l2"] = one
    got["bv_l2"] = column(heads_first(np.tile(i[L2 + "bv"], H)))
    got["bo_l2"] = rows(i[L2 + "bo"])
    got["bg"] = rows(i[L2 + "bg"])
    got["rms_w"] = rows(i[L2 + "rms_w"])
    got["wq_l3"] = chunks(both(i[L3 + "wq"]))
    got["wk_l3"] = chunks(both(i[L3 + "wk"]))
    got["wv_l3"] = chunks(both(i[L3 + "wv"]))
    got["wo_l3"] = chunks(both(i[L3 + "wo"]))
    got["l3_w1"] = chunks(heads_first(i[L3 + "w1"]))
    got["l3_w2"] = chunks(heads_first(i[L3 + "w2"], 1))
    got["bq_l3"] = column(heads_first(i[L3 + "bq"]))
    got["bk_l3"] = column(heads_first(i[L3 + "bk"]))
    got["g_in"] = column(heads_first(i[L3 + "ln1_g"]))
    got["b_in"] = column(heads_first(i[L3 + "ln1_b"]))
    got["bv_l3"] = column(heads_first(i[L3 + "bv"]))
    got["g_mlp"] = column(heads_first(i[L3 + "ln2_g"]))
    got["b_mlp"] = column(heads_first(i[L3 + "ln2_b"]))
    got["l3_b1"] = column(i[L3 + "b1"])
    got["bo_l3"] = rows(i[L3 + "bo"])
    got["l3_b2"] = rows(i[L3 + "b2"])
    return np.ascontiguousarray(np.concatenate([got[name] for name, _ in PACK], axis=1))


def pack_setup(i):
    blocks = np.zeros((P, len(SETUP), P), np.float32)
    for n, name in enumerate(SETUP):
        w = i["L0_xattn_" + {"self": "msa_W", "cross": "ca_W"}[name[3:]] + name[1]]
        for k in range(HC):
            blocks[k::HC, n, k::HC] = w
    return blocks.reshape(P, -1)


def kernel(**inputs):
    import concourse.bacc as bacc
    from concourse.bass_utils import run_bass_kernel_spmd

    i = {k: np.asarray(v) for k, v in inputs.items()}
    arrays = {
        "in_x": np.ascontiguousarray(heads_first(i["x"], 2)),
        "in_ctx": np.ascontiguousarray(heads_first(i["ctx_1024"], 2)),
        "in_mask_cross": np.ascontiguousarray(i["mask_Bx1xSxS2_if1"]),
        "in_mask_self": np.ascontiguousarray(i["mask_Bx1xSxS2_ik0"]),
        "in_params": pack(i),
        "in_setup": pack_setup(i),
    }
    nc = bacc.Bacc("TRN2", target_bir_lowering=False, num_devices=1)
    args = [nc.dram_tensor(n, a.shape, mybir.dt.from_np(a.dtype), kind="ExternalInput").ap()
            for n, a in arrays.items()]
    args.append(nc.dram_tensor("out", (B, S, E), FP32, kind="ExternalOutput").ap())
    build(nc, *args)
    r = run_bass_kernel_spmd(nc, [arrays], core_ids=[0])
    return r.results[0]["out"].reshape(B, S, C, HD, HC).swapaxes(3, 4).reshape(B, S, E)
```

```python
import concourse.bass as bass
import concourse.mybir as mybir
import numpy as np
from contextlib import ExitStack

FP32 = mybir.dt.float32
BF16 = mybir.dt.bfloat16
I32 = mybir.dt.int32
ALU = mybir.AluOpType
ACT = mybir.ActivationFunctionType
AX = mybir.AxisListType

B, S, E, H, HD, FF = 16, 256, 256, 16, 16, 1024
P = 128
T = S // P
C = E // P
FC = FF // P
HC = P // HD
NG, NJ = 4, 4
Q = 32
STREAMS = 2
PAIRS = B // STREAMS
WINDOW_HALF = 64
MASKED = -float(2 ** 66)
LAYERS = ["self", "cross", "l1", "l2", "l3"]
SCALE = {"self": 1 / 16, "cross": 1 / 16, "l1": 0.25, "l2": 0.25, "l3": 0.25}
EPS = 1e-5
RMS_EPS = 1e-6

QUERY_PIECES = [0, 0, 0, 1, 1, 2]
KEY_PIECES = [0, 1, 2, 0, 1, 0]
ROWS = HD * len(QUERY_PIECES)
MAX_ROWS = ROWS + 3

PACK = [
    ("bo_self", E),
    ("wo_self", 512), ("wo_cross", 512),
    ("l0_w1", C * FF), ("l0_w2", FC * E), ("l0_b1", FC),
    ("ln1_g", E), ("ln1_b", E), ("ln2_g", E), ("ln2_b", E), ("ln3_g", E), ("ln3_b", E),
    ("bo_cross", E), ("l0_b2", E),
    ("wq_l1", C * E), ("wk_l1", C * E), ("wv_l1", C * E), ("wo_l1", C * E),
    ("bq_l1", C), ("bk_l1", C), ("g_kv", C), ("b_kv", C), ("bv_l1", C),
    ("g_q", E), ("b_q", E), ("bo_l1", E),
    ("wq_l2", C * E), ("wk_l2", C * HD), ("wv_l2", C * HD), ("wo_l2", C * E), ("wg", 2 * C * E),
    ("bq_l2", C), ("bk_l2", 1), ("bv_l2", C), ("bo_l2", E), ("bg", E), ("rms_w", E),
    ("wq_l3", C * E), ("wk_l3", C * E), ("wv_l3", C * E), ("wo_l3", C * E),
    ("l3_w1", C * FF), ("l3_w2", FC * E),
    ("bq_l3", C), ("bk_l3", C), ("g_in", C), ("b_in", C), ("bv_l3", C), ("g_mlp", C), ("b_mlp", C),
    ("l3_b1", FC), ("bo_l3", E), ("l3_b2", E),
]
SETUP = ["wq_self", "wk_self", "wq_cross", "wk_cross", "wv_self", "wv_cross"]
AT = {}
_n = 0
for _name, _w in PACK:
    AT[_name] = (_n, _w)
    _n += _w
PACKED = _n

LOADS = 4
BIAS_SOURCES = {"bk_l1": ("wk_l1", "b_kv"), "bv_l1": ("wv_l1", "b_kv"), "bq_l3": ("wq_l3", "b_in"),
                "bk_l3": ("wk_l3", "b_in"), "bv_l3": ("wv_l3", "b_in"), "l3_b1": ("l3_w1", "b_mlp")}
BIAS_COLUMNS = {}
_n = 0
for _name in BIAS_SOURCES:
    BIAS_COLUMNS[_name] = _n
    _n += AT[_name][1]
VALUE_BIASES = ["bv_l1", "bv_l2", "bv_l3"]

UNITS = H // 2
UNIT_BUFS = 2
PROB_BUFS = 4
WORK = 2

ATTENTION = (
    "max0", "max2", "max1", "max3", "pieces0", "max5", "max4", "turn0", "max6", "max7", "pieces1", "exp0",
    "exp1", "turn1", "exp3", "exp2", "weigh0", "exp4", "exp5", "weigh1", "exp6", "exp7", "weigh2", "out0",
    "weigh3",
)
DENSE = {
    "cross": [
        "out1", "ksplit", "mix1", "values", "mix0", "outT", "proj", "ln1", "lnT", "qsplit", "q",
    ],
    "l1": [
        "out1", "mix1", "mix0", "outT", "proj", "keys", "ln2", "ksplit", "lnT", "next_c", "hid0", "hid3",
        "hid1", "hid2", "hid_out", "ln3", "lnq", "v", "lnqT", "qsplit", "q",
    ],
    "l2": [
        "out1", "mix0", "mix1", "outT", "proj", "keys", "ksplit", "lnT", "q", "qsplit",
    ],
    "l3": [
        "out1", "mix0", "mix1", "outT", "proj", "attnT", "gate", "keys", "rms", "ksplit", "mean", "v",
        "lnin", "lnT", "q", "qsplit",
    ],
    "end": [
        "mix0", "out1", "mix1", "outT", "proj", "+ctxT", "lnmlp", "lnT", "+ctxln", "hid0", "hid1", "hid2",
        "+ctxnT", "hid3", "hid_out", "store", "+inputs", "+xT", "+ksplit", "+q", "+next_x", "+qsplit",
    ],
}
ORDER = (
    "10101100101101100111011001111111111100101011010001011000100101000000011111000011"
    "00001000100010101001101100100101111111101100001001111110010101011100100100101100"
    "00001101001110001011100011111111111111100101101001101000110100000010000000001001"
    "01100100001110001101111100111111111001110001101101001010011011000110000000010011"
    "00110110001111010000001011010000101101111111111100000011001000111111010111001000"
    "1101000000"
)
NORMS = ("ctxln", "ln1", "ln2", "ln3", "lnq", "rms", "lnin", "lnmlp")
THROUGH_WORK = ("xT", "q", "ctxT", "ctxnT", "mix0", "mix1", "outT", "proj", "lnT", "lnqT", "keys", "v",
                "hid0", "hid1", "hid2", "hid3", "hid_out", "attnT", "gate", "mean", "turn0", "turn1")


def attention(s, l):
    return [(s, l, step) for step in ATTENTION]


def dense(s, l):
    return [(s, "self", step[1:]) if step[0] == "+" else (s, l, step) for step in DENSE[l]]


def stream_steps(s):
    out = []
    for l, after in zip(LAYERS, LAYERS[1:] + ["end"]):
        out += (attention(1, l) if s == 1 else []) + dense(s, after)
        out += attention(0, LAYERS[(LAYERS.index(l) + 1) % len(LAYERS)]) if s == 0 else []
    return out


def round_steps():
    steps = [iter(stream_steps(s)) for s in range(STREAMS)]
    out = [next(steps[int(s)]) for s in ORDER]
    assert len(out) == sum(len(stream_steps(s)) for s in range(STREAMS))
    return out


SCHEDULE = round_steps()
BEFORE = {l: p for p, l in zip(LAYERS, LAYERS[1:] + ["end"])}


def ahead(key):
    s, l, step = key
    return l == "self" and (s == 0 or step not in ATTENTION)


FIRST = [(s, "self", step[1:]) for s in range(STREAMS) for step in DENSE["end"] if step[0] == "+"] + attention(0, "self")
assert sorted(FIRST) == sorted(k for k in SCHEDULE if ahead(k))


class Numbers:

    def __init__(self, chosen):
        self.keys = [k for k in SCHEDULE if chosen(k[2])]
        self.place = {k: n for n, k in enumerate(self.keys)}
        self.first_keys = [k for k in FIRST if chosen(k[2])]
        self.first_place = {k: n for n, k in enumerate(self.first_keys)}
        self.round = len(self.keys)
        self.first = len(self.first_keys)
        self.start = self.round

    def done(self, r, key, rounds=0, less=0, times=1):
        if r.i is None:
            return times * (self.start + self.first_place[key] + 1 - less)
        return r.value(times * self.round, times * (self.start + self.first + self.place[key] + 1 - less
                                                    + (rounds - ahead(key)) * self.round))

    def position(self, r, key):
        return self.first_place[key] if r.i is None else self.first + self.place[key]

    def buffer_before(self, r, key, buffers):
        if r.i is None:
            n = self.first_place[key] - buffers
            return (self.first_keys[n], 0) if n >= 0 else None
        n = self.place[key] - buffers
        return (self.keys[n], 0) if n >= 0 else (self.keys[n + self.round], -1)

    def done_in_round(self, r, key, back):
        if r.i is None:
            return self.start + self.first_place[key] + 1
        return r.i * self.round + (self.start + self.first + self.place[key] + 1 + back * self.round)


class Round:

    def __init__(self, i, key):
        self.i = i
        self.shift = 1 if i is not None and ahead(key) else 0

    def value(self, per, constant):
        if self.i is None:
            return constant
        return self.i * per + (self.shift * per + constant)


WORK_NO = Numbers(lambda step: step in THROUGH_WORK)
UNIT_NO = Numbers(lambda step: step[:3] in ("max", "exp"))
MAX_NO = Numbers(lambda step: step[:3] == "max")
EXP_NO = Numbers(lambda step: step[:3] == "exp")
WEIGH_NO = Numbers(lambda step: step.startswith("weigh"))
PIECES_NO = Numbers(lambda step: step.startswith("pieces"))
TURN_NO = Numbers(lambda step: step.startswith("turn"))
KSPLIT_NO = Numbers(lambda step: step == "ksplit")
QSPLIT_NO = Numbers(lambda step: step == "qsplit")
OUT_NO = Numbers(lambda step: step == "out1")
NORM_NO = Numbers(lambda step: step in NORMS)
for _n, (_s, _l, _step) in enumerate(WORK_NO.keys[:-WORK]):
    if _step in ("keys", "q"):
        _take = (_s, _l, "ksplit" if _step == "keys" else "qsplit")
        assert SCHEDULE.index(_take) < SCHEDULE.index(WORK_NO.keys[_n + WORK]), _take
for _numbers, _buffers in ((WORK_NO, WORK), (UNIT_NO, UNIT_BUFS), (EXP_NO, PROB_BUFS)):
    assert _numbers.round % _buffers == 0 and _numbers.first % _buffers == 0


def head_in(slot):
    return slot % C * HC + slot // C


def build(nc, x, ctx, mask_cross, mask_self, params, setup_params, out):
    stack = ExitStack()
    with stack:
        def sb(name, shape, dt=FP32):
            return stack.enter_context(nc.sbuf_tensor(name, shape, dt))

        def ps(name, shape, dt=FP32):
            return stack.enter_context(nc.psum_tensor(name, shape, dt))

        def sem(name):
            return stack.enter_context(nc.semaphore(name))

        def each(name, shape, dt=FP32):
            return [sb(f"{name}_{s}", shape, dt) for s in range(STREAMS)]

        par = sb("par", [P, PACKED])

        def pv(name, parts=1):
            a, w = AT[name]
            v = par[:, a:a + w]
            return v if parts == 1 else v.rearrange("p (c n) -> p c n", c=parts)

        def row(name):
            return pv(name).unsqueeze(1).broadcast_to((P, T, E))

        ident = sb("ident", [P, P])
        ident_b = sb("ident_b", [P, P], BF16)
        mean_w = sb("mean_w", [P, P])
        minus_half = sb("minus_half", [P, T])
        neg_band = sb("neg_band", [P, T, S], BF16)
        fold = {l: sb(f"fold_{l}", [P, P]) for l in ("self", "cross")}
        bv_col = sb("bv_col", [P, 3, C])
        c_in = each("c_in", [P, T, E])
        neg = {l: each(f"neg_{l}", [P, T, S], BF16) for l in ("self", "cross")}
        neg["l2"] = [neg_band] * STREAMS
        tok_t = each("tok_t", [P, C, S])
        ctx_t = each("ctx_t", [P, C, S])
        ctxn_t = each("ctxn_t", [P, C, S])
        query_stack = each("query_stack", [P, H, S], BF16)
        key_stack = each("key_stack", [P, H, S], BF16)
        values = each("values", [P, T, H, Q])
        values_l2 = each("values_l2", [P, T, Q])
        x_b = each("x_b", [P, T, E])
        summed = each("summed", [P, T, E])
        hidden_t = each("hidden_t", [P, FC, S])
        norm = each("norm", [P, T, E])
        resid = each("resid", [P, T, E])
        xhat = norm
        out_t = [hidden_t[s][:, 0:NG, :] for s in range(STREAMS)]
        out_tok = [hidden_t[s][:, NG:NG + T, :] for s in range(STREAMS)]
        turned_t = [hidden_t[s][:, NG + T:, :] for s in range(STREAMS)]
        attn, diff, gate_in, gate = ([hidden_t[s][:, T * i:T * (i + 1), :] for s in range(STREAMS)] for i in range(4))
        scaled = attn
        x_in = sb("x_in", [P, T, E])
        m_self = sb("m_self", [P, T, S], I32)
        m_cross = sb("m_cross", [P, T, S], I32)
        key_pieces = sb("key_pieces", [P, 3, C, S], BF16)
        query_pieces = sb("query_pieces", [P, 3, C, S], BF16)
        key_rest = sb("key_rest", [P, C, S])
        query_rest = key_rest
        probs = sb("probs", [P, PROB_BUFS, T, 2, S])
        neg_max = sb("neg_max", [P, 2, T, HC])
        max_rest = sb("max_rest", [P, 2, T, HC])
        max_pieces = sb("max_pieces", [P, 2, T, 3, HC], BF16)
        max_rows = sb("max_rows", [3 * HC, 2, S], BF16)
        recip = sb("recip", [P, T, H])
        stats = sb("stats", [P, T, 6])
        mv = sb("mv", [P, T, 2])
        sumsq = sb("sumsq", [P, T])
        var_eps = sb("var_eps", [P, T])
        rstd = sb("rstd", [P, T])
        result = sb("result", [P, T, E])
        flat = hidden_t[1][:].rearrange("p f s -> p (f s)")
        setup = {name: flat[:, n * P:(n + 1) * P] for n, name in enumerate(SETUP)}
        used = len(SETUP) * P
        bv_wide = flat[:, used:used + 3 * C * P].rearrange("p (i c n) -> p i c n", i=3, c=C)
        used += 3 * C * P
        ones = resid[1][:, 0, 0:P]
        band = flat[:, used:used + T * S].rearrange("p (t s) -> p t s", t=T)

        unit_psum = [ps(f"unit{i}", [P, T, 2, S]) for i in range(UNIT_BUFS)]
        out_psum = [ps(f"out{a}", [P, 2, S]) for a in range(2)]
        work_psum = [ps(f"work{i}", [P, 2, S]) for i in range(WORK)]
        row_psum = [work_psum[0][:, 0, :], work_psum[1][:, 0, :], unit_psum[0][:, 0, 0, :]]

        ev = {n: [sem(f"{n}_{s}") for s in range(STREAMS)] for n in [
            "values_self", "values_cross", "negs", "bias_self", "bias_cross", "bias_ff", "bias_l1", "diff",
            "bias_l3", "bias_mlp", "ctx_norm", "ln1", "ln2", "lnq", "gate_tanh", "xhat", "lnin", "lnmlp",
            "c_loaded"]}
        x_loaded = sem("x_loaded")
        m_loaded = sem("m_loaded")
        stored = sem("stored")
        keys_placed = sem("keys_placed")
        queries_placed = sem("queries_placed")
        max_placed = sem("max_placed")
        unit_filled = [sem(f"unit_filled{i}") for i in range(UNIT_BUFS)]
        work_filled = [sem(f"work_filled{i}") for i in range(WORK)]
        work_emptied = [sem(f"work_emptied{i}") for i in range(WORK)]
        maxed = sem("maxed")
        exped = sem("exped")
        weighed = sem("weighed")
        out_taken = sem("out_taken")
        max_cut = sem("max_cut")
        key_high = sem("key_high")
        key_low = sem("key_low")
        query_high = sem("query_high")
        query_low = sem("query_low")
        stats_ready = sem("stats_ready")
        rstd_ready = sem("rstd_ready")
        const_ready = sem("const_ready")
        sp_waits = sem("sp_waits")
        pool_waits = sem("pool_waits")
        setup_loaded = sem("setup_loaded")
        loaded = sem("loaded")
        first_products = sem("first_products")
        first_folded = sem("first_folded")
        fold_products = sem("fold_products")
        fold_wide = sem("fold_wide")
        fold_rows = sem("fold_rows")
        folded = sem("folded")
        first_done = sem("first_done")
        met = sem("met")

        def count(numbers, r, key):
            return numbers.done(r, key)

        def unit_buffer(r, key):
            return UNIT_NO.position(r, key) % UNIT_BUFS

        def wait_free_unit(pe, r, key):
            before = UNIT_NO.buffer_before(r, key, UNIT_BUFS)
            if before:
                if before[0][2][:3] == "max":
                    pe.wait_ge(maxed, MAX_NO.done_in_round(r, *before))
                else:
                    pe.wait_ge(exped, EXP_NO.done_in_round(r, *before))
            n = unit_buffer(r, key)
            return unit_psum[n], unit_filled[n]

        def bank_count(numbers, r, key, buffers, rounds=0):
            if r.i is None:
                return numbers.round // buffers + (numbers.first_place[key] // buffers + 1)
            at = numbers.first + numbers.place[key]
            return r.value(numbers.round // buffers, numbers.round // buffers * (1 - ahead(key) + rounds)
                           + (at // buffers + 1))

        def wait_full_unit(eng, r, key):
            n = unit_buffer(r, key)
            eng.wait_ge(unit_filled[n], bank_count(UNIT_NO, r, key, UNIT_BUFS))
            return unit_psum[n]

        def wait_free_work(pe, r, key):
            n = WORK_NO.position(r, key) % WORK
            if WORK_NO.buffer_before(r, key, WORK):
                pe.wait_ge(work_emptied[n], bank_count(WORK_NO, r, key, WORK) - 1)
            return work_psum[n], work_filled[n]

        def wait_full_work(eng, r, key, rounds=0):
            n = WORK_NO.position(r, key) % WORK
            eng.wait_ge(work_filled[n], bank_count(WORK_NO, r, key, WORK, rounds))
            return work_psum[n], work_emptied[n]

        def wait_taken(eng, r, *keys, before=None, rounds=0):
            last = {}
            for key in keys:
                n = WORK_NO.position(r, key)
                if before is None or n % WORK != WORK_NO.position(r, before) % WORK:
                    if n % WORK not in last or n > last[n % WORK][0]:
                        last[n % WORK] = (n, key)
            for i, (_, key) in last.items():
                eng.wait_ge(work_emptied[i], bank_count(WORK_NO, r, key, WORK, rounds))

        def meet(eng):
            eng.sem_inc(first_done, 1)
            eng.wait_ge(first_done, 5)
            eng.sem_inc(met, 1)

        def wait_folded(eng):
            eng.wait_ge(folded, 1)
            eng.sem_inc(met, 1)

        def flatten(t):
            return t.rearrange("p a n -> p (a n)")

        block = stack.enter_context(nc.Block())

        @block.sync
        def _(sp):
            x_tok = x.rearrange("b (t p) e -> b p t e", p=P)
            c_tok = ctx.rearrange("b (t p) e -> b p t e", p=P)
            ms_tok = mask_self.rearrange("b o (t p) k -> (b o) p t k", p=P)
            mc_tok = mask_cross.rearrange("b o (t p) k -> (b o) p t k", p=P)
            o_tok = out.rearrange("b (t p) e -> b p t e", p=P)

            def one(v, b):
                return v[bass.ds(b, 1)].rearrange("o p t e -> p (o t) e")

            def load_x(b):
                sp.dma_start(x_in[:], one(x_tok, b)).then_inc(x_loaded, 16)
                sp.dma_start(m_self[:], one(ms_tok, b)).then_inc(m_loaded, 16)
                sp.dma_start(m_cross[:], one(mc_tok, b)).then_inc(m_loaded, 16)

            def load_c(s, b):
                sp.dma_start(c_in[s][:], one(c_tok, b)).then_inc(ev["c_loaded"][s], 16)

            sp.sem_inc(stored, 16)
            sp.sem_inc(keys_placed, 96 * KSPLIT_NO.start)
            sp.sem_inc(queries_placed, 96 * QSPLIT_NO.start)
            sp.sem_inc(max_placed, 16 * TURN_NO.start)
            sp.dma_start(flat[:, 0:len(SETUP) * P], setup_params).then_inc(setup_loaded, 16)
            sp.dma_start(pv("bo_self"), params[:, 0:E]).then_inc(setup_loaded, 16)
            load_x(0)
            load_c(0, 0)
            load_c(1, 1)
            cut = [E + n * (PACKED - E) // LOADS for n in range(LOADS + 1)]
            for i in range(LOADS):
                sp.dma_start(par[:, cut[i]:cut[i + 1]], params[:, cut[i]:cut[i + 1]]).then_inc(loaded, 16)

            def run(i, keys):
                if i is not None:
                    now = [sp.snap(i * STREAMS + s) for s in range(STREAMS)]
                    later = [sp.snap((i * STREAMS + (STREAMS + a)) % B) for a in range(2 * STREAMS + 1)]

                def wait(s, value):
                    sp.wait_ge(s, value)
                    sp.sem_inc(sp_waits, 1)

                def split(s, l, what):
                    keys = what == "ksplit"
                    pieces, stack_, rows = ((key_pieces, key_stack[s], KEY_PIECES) if keys
                                            else (query_pieces, query_stack[s], QUERY_PIECES))
                    high, low, placed = ((key_high, key_low, keys_placed) if keys
                                         else (query_high, query_low, queries_placed))
                    no = KSPLIT_NO if keys else QSPLIT_NO
                    if l != "self":
                        wait(weighed, WEIGH_NO.done(r, (s, BEFORE[l], "weigh3")))
                    elif i is not None:
                        wait(weighed, WEIGH_NO.done(r, (s, LAYERS[-1], "weigh3"), -1))
                    for piece in range(3):
                        if piece == 0:
                            sp.wait_ge(high, no.done(r, key))
                        else:
                            sp.wait_ge(low, no.done(r, key, times=2) - (2 - piece))
                        for at, which in enumerate(rows):
                            if which != piece:
                                continue
                            dst = stack_[HD * at:HD * (at + 1), :, :]
                            if keys and l == "l2":
                                sp.dma_start(dst[:, 0, :], pieces[0:HD, piece, 0, :]).then_inc(placed, 16)
                            else:
                                sp.dma_start(dst.rearrange("d h n -> d (h n)"),
                                             pieces[:, piece].rearrange("p c n -> p (c n)")).then_inc(placed, 16)

                for key in keys:
                    r = Round(i, key)
                    s, l, step = key
                    if step in ("ksplit", "qsplit"):
                        split(s, l, step)
                    elif step in ("turn0", "turn1"):
                        a = int(step[-1])
                        wait_taken(sp, r, key)
                        sp.dma_start(query_stack[s][ROWS:MAX_ROWS, HC * a:HC * (a + 1), :],
                                     max_rows[:, a, :]).then_inc(max_placed, 16)
                    elif step == "next_x":
                        wait_taken(sp, r, (s, "self", "xT"))
                        sp.sem_inc(sp_waits, 1)
                        wait(ev["negs"][s], r.value(1, 1))
                        if i is None:
                            load_x((s + 1) % B)
                        else:
                            load_x(later[s + 1])
                    elif step == "next_c":
                        wait_taken(sp, r, (s, "self", "ctxT"))
                        sp.sem_inc(sp_waits, 1)
                        wait(ev["ctx_norm"][s], r.value(T, T))
                        wait(ev["values_cross"][s], r.value(1, 1))
                        load_c(s, later[s])
                    elif step == "store":
                        wait_taken(sp, r, (s, l, "hid_out"))
                        sp.sem_inc(sp_waits, 1)
                        sp.dma_start(one(o_tok, now[s]), result[:]).then_inc(stored, 16)

            run(None, FIRST)
            sp.wait_ge(keys_placed, 96 * (KSPLIT_NO.start + KSPLIT_NO.first))
            sp.wait_ge(queries_placed, 96 * (QSPLIT_NO.start + QSPLIT_NO.first))
            sp.wait_ge(max_placed, 16 * (TURN_NO.start + TURN_NO.first))
            meet(sp)
            wait_folded(sp)
            with sp.Fori(0, PAIRS) as i:
                run(i, SCHEDULE)
            sp.wait_ge(keys_placed, 96 * (KSPLIT_NO.start + KSPLIT_NO.first + PAIRS * KSPLIT_NO.round))
            sp.wait_ge(queries_placed, 96 * (QSPLIT_NO.start + QSPLIT_NO.first + PAIRS * QSPLIT_NO.round))
            sp.wait_ge(max_placed, 16 * (TURN_NO.start + TURN_NO.first + PAIRS * TURN_NO.round))
            sp.wait_ge(stored, 16 * B + 16)
            sp.wait_ge(x_loaded, 16 * (B + STREAMS + 1))
            sp.wait_ge(m_loaded, 32 * (B + STREAMS + 1))
            for s in range(STREAMS):
                sp.wait_ge(ev["c_loaded"][s], 16 * (PAIRS + 1))

        @block.gpsimd
        def _(pool):
            g = nc.gpsimd
            g.memset(ident[:], 0.0)
            g.memset(ones, 1.0)
            g.memset(mean_w[:], 1.0 / S)
            g.memset(minus_half[:], -0.5)
            g.memset(band, 0.0)
            for s in range(STREAMS):
                g.memset(values[s][:], 1.0)
                g.memset(values_l2[s][:], 1.0)
            g.drain()
            for s in range(STREAMS):
                g.memset(key_stack[s][ROWS:P, :, :], 1.0)
            g.drain()
            g.affine_select(out=ident[:], in_=ident[:], compare_op=ALU.not_equal, fill=1.0, base=0,
                            pattern=[[-1, P]], channel_multiplier=1)
            g.affine_select(out=band, in_=band, compare_op=ALU.is_ge, fill=MASKED, base=WINDOW_HALF,
                            pattern=[[-P, T], [1, S]], channel_multiplier=-1)
            g.drain()
            g.affine_select(out=band, in_=band, compare_op=ALU.is_ge, fill=MASKED, base=WINDOW_HALF,
                            pattern=[[P, T], [-1, S]], channel_multiplier=1)
            g.drain()
            g.tensor_copy(neg_band[:], band)
            g.tensor_copy(ident_b[:], ident[:]).then_inc(const_ready, 1)
            pool.wait_ge(first_folded, 1)

            pool.sem_inc(rstd_ready, NORM_NO.start)
            pool.sem_inc(max_cut, PIECES_NO.start)

            def run(i, keys):
                def wait(s, value):
                    pool.wait_ge(s, value)
                    pool.sem_inc(pool_waits, 1)

                def wait_step(key):
                    wait_taken(pool, r, key)
                    pool.sem_inc(pool_waits, 1)

                def reciprocal_root(key):
                    wait(stats_ready, count(NORM_NO, r, key))
                    if key[2] == "rms":
                        g.tensor_scalar(var_eps[:], sumsq[:], 1.0 / E, RMS_EPS, ALU.mult, ALU.add)
                    else:
                        g.tensor_scalar(var_eps[:], mv[:, :, 1], EPS, None, ALU.add)
                    g.drain()
                    g.tensor_tensor(rstd[:], var_eps[:], minus_half[:], ALU.pow).then_inc(rstd_ready, 1)

                def spread(dst, src):
                    for t in range(T):
                        last = g.tensor_copy(dst[:, t, :, 0:HD].rearrange("p (c h) d -> p c h d", c=C),
                                             src[:, t, :].rearrange("p (c d h) -> p c h d", c=C, d=HD))
                    return last

                def with_bias(s, src, bias, done):
                    g.tensor_tensor(x_b[s][:], src, row(bias), ALU.add).then_inc(ev[done][s], 1)

                for key in keys:
                    r = Round(i, key)
                    s, l, step = key
                    if step in NORMS:
                        reciprocal_root(key)
                    if step == "inputs":
                        if i is not None:
                            wait(weighed, WEIGH_NO.done(r, (s, LAYERS[-1], "weigh3"), -1))
                        wait(x_loaded, r.value(16 * STREAMS, 16 * (s + 1)))
                        spread(values[s], x_in).then_inc(ev["values_self"][s], 1)
                        if i is not None:
                            wait_taken(pool, r, (s, "end", "hid_out"), rounds=-1)
                            pool.sem_inc(pool_waits, 1)
                        with_bias(s, x_in[:], "bo_self", "bias_self")
                        wait(m_loaded, r.value(32 * STREAMS, 32 * (s + 1)))
                        for name, m in (("self", m_self), ("cross", m_cross)):
                            last = g.tensor_scalar(neg[name][s][:], m[:], 0, MASKED, ALU.is_equal, ALU.mult)
                        last.then_inc(ev["negs"][s], 1)
                    elif step == "values":
                        wait(weighed, count(WEIGH_NO, r, (s, "self", "weigh3")))
                        wait(ev["c_loaded"][s], r.value(16, 16))
                        spread(values[s], c_in[s]).then_inc(ev["values_cross"][s], 1)
                    elif step == "ln1":
                        wait(ev["ln1"][s], r.value(T, T))
                        with_bias(s, resid[s][:], "bo_cross", "bias_cross")
                    elif step == "ln2":
                        wait(ev["ln2"][s], r.value(T, T))
                        with_bias(s, resid[s][:], "l0_b2", "bias_ff")
                    elif step == "lnq":
                        wait(ev["lnq"][s], r.value(T, T))
                        with_bias(s, resid[s][:], "bo_l1", "bias_l1")
                    elif step == "attnT":
                        wait_step((s, l, "proj"))
                        g.tensor_tensor(diff[s], attn[s], summed[s][:], ALU.subtract).then_inc(ev["diff"][s], 1)
                    elif step == "mean":
                        wait_step(key)
                        with_bias(s, summed[s][:], "bo_l3", "bias_l3")
                    elif step == "proj" and l == "end":
                        wait_step(key)
                        with_bias(s, resid[s][:], "l3_b2", "bias_mlp")
                    elif step in ("pieces0", "pieces1"):
                        a = int(step[-1])
                        wait(maxed, count(MAX_NO, r, (s, l, f"max{4 * a + 3}")))
                        for piece in range(3):
                            src = neg_max if piece == 0 else max_rest
                            last = g.tensor_copy(max_pieces[:, a, :, piece, :], src[:, a])
                            if piece < 2:
                                g.drain()
                                g.tensor_tensor(max_rest[:, a], src[:, a], max_pieces[:, a, :, piece, :], ALU.subtract)
                                g.drain()
                        last.then_inc(max_cut, 1)

            run(None, FIRST)
            nc.gpsimd.drain()
            meet(pool)
            wait_folded(pool)
            with pool.Fori(0, PAIRS) as i:
                run(i, SCHEDULE)

        @block.scalar
        def _(act):
            a_ = nc.scalar
            act.wait_ge(first_folded, 1)
            for s, numbers in ((exped, EXP_NO), (out_taken, OUT_NO), (key_high, KSPLIT_NO), (query_high, QSPLIT_NO)):
                act.sem_inc(s, numbers.start)

            def run(i, keys):
                def take(key, dst):
                    bank, taken = wait_full_work(act, r, key)
                    a_.copy(dst[:], bank[:]).then_inc(taken, 1)

                def high(s, l, what):
                    of_keys = what == "ksplit"
                    pieces, done, placed, no = ((key_pieces, key_high, keys_placed, KSPLIT_NO) if of_keys
                                                else (query_pieces, query_high, queries_placed, QSPLIT_NO))
                    act.wait_ge(placed, no.done(r, key, less=1, times=96))
                    dst = pieces[:, 0]
                    if of_keys and l in ("self", "cross"):
                        src = (tok_t if l == "self" else ctx_t)[s]
                        wait_taken(act, r, (s, "self", "xT" if l == "self" else "ctxT"))
                        last = a_.copy(dst, src[:])
                    else:
                        bank, _ = wait_full_work(act, r, (s, l, "keys" if of_keys else "q"))
                        if l in ("self", "cross"):
                            last = a_.copy(dst, bank[:])
                        elif of_keys and l == "l2":
                            last = a_.activation(dst[0:HD, 0, :], bank[0:HD, 0, :], ACT.Identity,
                                                 bias=pv("bk_l2")[0:HD, :])
                        else:
                            bias = pv(("bk_" if of_keys else "bq_") + l)
                            for c in range(C):
                                last = a_.activation(dst[:, c, :], bank[:, c, :], ACT.Identity, bias=bias[:, c:c + 1])
                    last.then_inc(done, 1)

                for key in keys:
                    r = Round(i, key)
                    s, l, step = key
                    if step[:3] == "exp":
                        n = EXP_NO.position(r, key)
                        bank = wait_full_unit(act, r, key)
                        before = EXP_NO.buffer_before(r, key, PROB_BUFS)
                        if before:
                            (bs, bl, bstep), back = before
                            act.wait_ge(weighed, WEIGH_NO.done_in_round(r, (bs, bl, f"weigh{int(bstep[3:]) // 2}"), back))
                        a_.activation(probs[:, n % PROB_BUFS], bank[:], ACT.Exp, scale=SCALE[l]).then_inc(exped, 1)
                    elif step in ("turn0", "turn1"):
                        bank, taken = wait_full_work(act, r, key)
                        a_.copy(max_rows[:, int(step[-1]), :], bank[0:3 * HC, 0, :]).then_inc(taken, 1)
                    elif step == "out0":
                        act.wait_ge(weighed, count(WEIGH_NO, r, (s, l, "weigh1")))
                        a_.copy(out_t[s][:, 0:2, :], out_psum[0][:])
                    elif step == "out1":
                        act.wait_ge(weighed, count(WEIGH_NO, r, (s, BEFORE[l], "weigh3")))
                        a_.copy(out_t[s][:, 2:4, :], out_psum[1][:]).then_inc(out_taken, 1)
                    elif step in ("ksplit", "qsplit"):
                        high(s, l, step)
                    elif step in ("xT", "lnT", "lnqT"):
                        take(key, tok_t[s])
                    elif step == "ctxT":
                        take(key, ctx_t[s])
                    elif step == "ctxnT":
                        take(key, ctxn_t[s])
                    elif step in ("outT", "attnT"):
                        take(key, turned_t[s])
                    elif step[:3] == "hid" and step != "hid_out":
                        bank, taken = wait_full_work(act, r, key)
                        func, bias = (ACT.Relu, "l0_b1") if l == "l1" else (ACT.Gelu, "l3_b1")
                        for k in range(2):
                            f = 2 * int(step[-1]) + k
                            last = a_.activation(hidden_t[s][:, f, :], bank[:, k, :], func, bias=pv(bias)[:, f:f + 1])
                        last.then_inc(taken, 1)
                    elif step == "rms":
                        wait_taken(act, r, (s, l, "gate"))
                        a_.activation(gate[s], gate_in[s], ACT.Tanh, scale=0.5).then_inc(ev["gate_tanh"][s], 1)
                    elif step == "v":
                        bank, taken = wait_full_work(act, r, key)
                        for t in range(T):
                            last = a_.copy(values[s][:, t, :, 0:HD].rearrange("p (c h) d -> p c h d", c=C),
                                           bank[:, t, :].rearrange("p (c d h) -> p c h d", c=C, d=HD))
                        last.then_inc(taken, 1)

            run(None, FIRST)
            nc.scalar.drain()
            meet(act)
            wait_folded(act)
            with act.Fori(0, PAIRS) as i:
                run(i, SCHEDULE)

        @block.vector
        def _(dve):
            v = nc.vector
            dve.wait_ge(first_products, 1)
            v.tensor_copy(fold["self"][:], unit_psum[0][:, 0, 0, 0:P])
            v.tensor_copy(fold["cross"][:], unit_psum[0][:, 0, 0, P:2 * P])
            for i in range(WORK):
                dve.sem_inc(work_emptied[i], WORK_NO.start // WORK)
            for s, n in ((maxed, MAX_NO.start), (stats_ready, NORM_NO.start), (key_low, 2 * KSPLIT_NO.start),
                         (query_low, 2 * QSPLIT_NO.start)):
                dve.sem_inc(s, n)
            v.drain()
            dve.sem_inc(first_folded, 1)

            def run(i, keys):
                def moments(src):
                    for t in range(T):
                        v.bn_stats(stats[:, t, :], src[:, t, :])
                    v.drain()
                    for t in range(T):
                        last = v.bn_aggr(mv[:, t, :], stats[:, t, :])
                    last.then_inc(stats_ready, 1)

                def layer_norm(src, key, done):
                    moments(src)
                    dve.wait_ge(rstd_ready, count(NORM_NO, r, key))
                    for t in range(T):
                        v.tensor_scalar(norm[s][:, t, :], src[:, t, :], mv[:, t, 0:1], rstd[:, t:t + 1],
                                        ALU.subtract, ALU.mult).then_inc(ev[done][key[0]], 1)

                def layer_norm_affine(src, dst, key, gain, bias, done=None):
                    moments(src)
                    v.drain()
                    for t in range(T):
                        v.scalar_tensor_tensor(out=scaled[s][:, t, :], in0=src[:, t, :], scalar=mv[:, t, 0:1],
                                               in1=pv(gain), op0=ALU.subtract, op1=ALU.mult)
                    v.drain()
                    dve.wait_ge(rstd_ready, count(NORM_NO, r, key))
                    for t in range(T):
                        last = v.scalar_tensor_tensor(out=dst[:, t, :], in0=scaled[s][:, t, :],
                                                      scalar=rstd[:, t:t + 1], in1=pv(bias),
                                                      op0=ALU.mult, op1=ALU.add)
                        if done:
                            last.then_inc(ev[done][key[0]], 1)
                    if not done:
                        v.drain()

                def plus(key, addend, dst):
                    bank, taken = wait_full_work(dve, r, key)
                    v.tensor_tensor(dst, bank[:], addend, ALU.add).then_inc(taken, 1)

                def low(s, l, what):
                    of_keys = what == "ksplit"
                    pieces, rest, done, ready, no = (
                        (key_pieces, key_rest, key_low, key_high, KSPLIT_NO) if of_keys
                        else (query_pieces, query_rest, query_low, query_high, QSPLIT_NO))
                    dve.wait_ge(ready, count(no, r, (s, l, what)))
                    if of_keys and l in ("self", "cross"):
                        v.tensor_tensor(rest[:], (tok_t if l == "self" else ctx_t)[s][:], pieces[:, 0], ALU.subtract)
                    else:
                        bank, taken = wait_full_work(dve, r, (s, l, "keys" if of_keys else "q"))
                        if l in ("self", "cross"):
                            last = v.tensor_tensor(rest[:], bank[:], pieces[:, 0], ALU.subtract)
                        elif of_keys and l == "l2":
                            v.tensor_copy(values_l2[s][:, :, 0:HD],
                                          bank[:, 1, 0:T * HD].rearrange("p (t d) -> p t d", t=T))
                            last = v.scalar_tensor_tensor(
                                out=rest[0:HD, 0, :], in0=bank[0:HD, 0, :], scalar=pv("bk_l2")[0:HD, :],
                                in1=pieces[0:HD, 0, 0, :], op0=ALU.add, op1=ALU.subtract)
                        else:
                            bias = pv(("bk_" if of_keys else "bq_") + l)
                            for c in range(C):
                                last = v.scalar_tensor_tensor(
                                    out=rest[:, c, :], in0=bank[:, c, :], scalar=bias[:, c:c + 1],
                                    in1=pieces[:, 0, c, :], op0=ALU.add, op1=ALU.subtract)
                        last.then_inc(taken, 1)
                    v.drain()
                    part = (slice(0, HD), slice(0, 1)) if of_keys and l == "l2" else (slice(0, P), slice(0, C))
                    v.tensor_copy(pieces[part[0], 1, part[1], :], rest[part[0], part[1], :]).then_inc(done, 1)
                    v.drain()
                    v.tensor_tensor(pieces[part[0], 2, part[1], :], rest[part[0], part[1], :],
                                    pieces[part[0], 1, part[1], :], ALU.subtract).then_inc(done, 1)
                    v.drain()

                for key in keys:
                    r = Round(i, key)
                    s, l, step = key
                    if step[:3] == "max":
                        u = int(step[3:])
                        bank = wait_full_unit(dve, r, key)
                        v.tensor_reduce(neg_max[:, u // 4, :, 2 * (u % 4):2 * (u % 4) + 2], bank[:], AX.X, ALU.max,
                                        negate=True).then_inc(maxed, 1)
                    elif step in ("ksplit", "qsplit"):
                        low(s, l, step)
                    elif step == "ctxln":
                        if i is not None:
                            wait_full_work(dve, r, (s, "end", "lnT"), rounds=-1)
                        dve.wait_ge(ev["c_loaded"][s], r.value(16, 16))
                        layer_norm(c_in[s], key, "ctx_norm")
                    elif step in ("mix0", "mix1"):
                        t = int(step[-1])
                        bank, taken = wait_full_work(dve, r, key)
                        slots = flatten(bank[:, :, :]).rearrange("p (h n) -> p h n", h=H)
                        v.reciprocal(recip[:, t, :], slots[:, :, HD])
                        v.drain()
                        for c in range(C):
                            last = v.tensor_tensor(
                                out_tok[s][:, t, c * P:(c + 1) * P].rearrange("p (d h) -> p h d", h=HC),
                                slots[:, c::C, 0:HD], recip[:, t, c::C].unsqueeze(2).broadcast_to((P, HC, HD)),
                                ALU.mult)
                        last.then_inc(taken, 1)
                    elif step == "proj":
                        if l == "l3":
                            plus(key, row("bo_l2"), attn[s])
                            continue
                        wait_for = {"cross": "bias_self", "l1": "bias_cross", "l2": "bias_l1", "end": "bias_l3"}[l]
                        dve.wait_ge(ev[wait_for][s], r.value(1, 1))
                        plus(key, x_b[s][:], resid[s][:] if l == "end" else summed[s][:])
                        v.drain()
                    elif step == "ln1":
                        layer_norm_affine(summed[s], resid[s], key, "ln1_g", "ln1_b", "ln1")
                    elif step == "ln2":
                        layer_norm_affine(summed[s], resid[s], key, "ln2_g", "ln2_b", "ln2")
                    elif step == "ln3":
                        layer_norm_affine(summed[s], norm[s], key, "ln3_g", "ln3_b")
                    elif step == "lnq":
                        layer_norm_affine(norm[s], resid[s], key, "g_q", "b_q", "lnq")
                    elif step == "hid_out" and l == "l1":
                        dve.wait_ge(ev["bias_ff"][s], r.value(1, 1))
                        plus(key, x_b[s][:], summed[s][:])
                        v.drain()
                    elif step == "gate":
                        plus(key, row("bg"), gate_in[s])
                    elif step == "rms":
                        dve.wait_ge(ev["gate_tanh"][s], r.value(1, 1))
                        v.scalar_tensor_tensor(out=gate[s], in0=gate[s], scalar=1.0, in1=gate_in[s], op0=ALU.add, op1=ALU.mult)
                        v.drain()
                        dve.wait_ge(ev["diff"][s], r.value(1, 1))
                        v.scalar_tensor_tensor(out=gate[s], in0=gate[s], scalar=0.5, in1=diff[s], op0=ALU.mult, op1=ALU.mult)
                        v.drain()
                        v.tensor_tensor(norm[s][:], gate[s], summed[s][:], ALU.add)
                        v.drain()
                        for t in range(T):
                            last = v.tensor_tensor_reduce(gate[s][:, t, :], norm[s][:, t, :], norm[s][:, t, :], 1.0, 0.0,
                                                          ALU.mult, ALU.add, sumsq[:, t:t + 1])
                        last.then_inc(stats_ready, 1)
                        dve.wait_ge(rstd_ready, count(NORM_NO, r, key))
                        for t in range(T):
                            last = v.scalar_tensor_tensor(out=xhat[s][:, t, :], in0=norm[s][:, t, :],
                                                          scalar=rstd[:, t:t + 1], in1=pv("rms_w"),
                                                          op0=ALU.mult, op1=ALU.mult)
                        last.then_inc(ev["xhat"][s], 1)
                    elif step == "mean":
                        bank, taken = wait_full_work(dve, r, key)
                        v.tensor_tensor(summed[s][:], xhat[s][:], bank[:, 0, :].unsqueeze(1).broadcast_to((P, T, E)),
                                        ALU.subtract).then_inc(taken, 1)
                        v.drain()
                    elif step == "lnin":
                        layer_norm(summed[s], key, "lnin")
                    elif step == "lnmlp":
                        layer_norm(resid[s], key, "lnmlp")
                    elif step == "hid_out" and l == "end":
                        dve.wait_ge(ev["bias_mlp"][s], r.value(1, 1))
                        dve.wait_ge(stored, r.value(16 * STREAMS, 16 * (s + 1)))
                        plus(key, x_b[s][:], result[:])

            run(None, FIRST)
            nc.vector.drain()
            meet(dve)
            dve.wait_ge(loaded, 16 * LOADS)
            dve.wait_ge(fold_products, 1)
            v.tensor_copy(pv("wo_self", C), unit_psum[0][:, 1])
            v.tensor_copy(pv("wo_cross", C), unit_psum[1][:, 0])
            sums = flatten(unit_psum[1][:, 1])
            for name, a in BIAS_COLUMNS.items():
                w = AT[name][1]
                dst = bv_col[:, VALUE_BIASES.index(name), :] if name in VALUE_BIASES else pv(name)
                v.tensor_tensor(dst, sums[:, a:a + w], pv(name), ALU.add)
            v.tensor_copy(bv_col[:, 1, :], pv("bv_l2"))
            v.drain()
            for i in range(3):
                for c in range(C):
                    last = v.tensor_scalar(bv_wide[:, i, c, :], ones, bv_col[:, i, c:c + 1], None, ALU.mult)
            last.then_inc(fold_wide, 1)
            for name, gain in (("wk_l1", "g_kv"), ("wv_l1", "g_kv"), ("wq_l3", "g_in"), ("wk_l3", "g_in"),
                               ("wv_l3", "g_in"), ("l3_w1", "g_mlp")):
                for c in range(C):
                    w = pv(name, C)[:, c, :]
                    v.tensor_scalar(w, w, pv(gain)[:, c:c + 1], None, ALU.mult)
            dve.wait_ge(fold_rows, 1)
            for i, name in enumerate(("bo_l1", "bo_l2", "bo_l3")):
                last = v.tensor_tensor(pv(name), row_psum[i], pv(name), ALU.add)
            last.then_inc(folded, 1)

            with dve.Fori(0, PAIRS) as i:
                run(i, SCHEDULE)

        @block.tensor
        def _(pe):
            pe.wait_ge(setup_loaded, 32)
            pe.wait_ge(const_ready, 1)
            for n, l in enumerate(("self", "cross")):
                last = pe.matmul(unit_psum[0][:, 0, 0, n * P:(n + 1) * P], setup[f"wq_{l}"], setup[f"wk_{l}"],
                          start=True, stop=True)
            last.then_inc(first_products, 1)
            pe.wait_ge(first_folded, 1)
            pe.sem_inc(weighed, WEIGH_NO.start)
            for n in range(UNIT_BUFS):
                pe.sem_inc(unit_filled[n], UNIT_NO.start // UNIT_BUFS)
            for n in range(WORK):
                pe.sem_inc(work_filled[n], WORK_NO.start // WORK)

            def run(i, keys):
                def turn(key, src, tiles_ready=None):
                    bank, filled = wait_free_work(pe, r, key)
                    for t in range(T):
                        if tiles_ready:
                            pe.wait_ge(tiles_ready, r.value(T, t + 1))
                        for c in range(C):
                            last = pe.transpose(bank[:, c, t * P:(t + 1) * P], src[:, t, c * P:(c + 1) * P], ident[:])
                    last.then_inc(filled, 1)

                def to_features(key, weight, src, column=0):
                    bank, filled = wait_free_work(pe, r, key)
                    for k in range(2):
                        for c in range(C):
                            last = pe.matmul(bank[:, k, :], pv(weight, C)[:, c, column + k * P:column + (k + 1) * P],
                                             src[:, c, :], start=(c == 0), stop=(c == C - 1))
                    last.then_inc(filled, 1)

                def to_tokens(key, parts):
                    bank, filled = wait_free_work(pe, r, key)
                    for t in range(T):
                        for n, (src, weight) in enumerate(parts):
                            last = pe.matmul(bank[:, t, :], src[:, t * P:(t + 1) * P], weight,
                                             start=(n == 0), stop=(n == len(parts) - 1))
                    last.then_inc(filled, 1)

                def dense(src, weight, n=C):
                    return [(src[:, c, :], pv(weight, n)[:, c, :]) for c in range(n)]

                def twice(ap, n):
                    return ap.unsqueeze(1).broadcast_to((P, 2, n))

                def scores_for_max(key):
                    s, l, step = key
                    u = int(step[3:])
                    if u == 0:
                        pe.wait_ge(keys_placed, KSPLIT_NO.done(r, (s, l, "ksplit"), times=96))
                        pe.wait_ge(queries_placed, QSPLIT_NO.done(r, (s, l, "qsplit"), times=96))
                        if l == "self":
                            pe.wait_ge(ev["negs"][s], r.value(1, 1))
                    bank, filled = wait_free_unit(pe, r, key)
                    masked = neg[l][s] if l in neg else None
                    for t in range(T):
                        if masked is not None:
                            pe.matmul(bank[:, t], ident_b[:], twice(masked[:, t, :], S), start=True, stop=False)
                        for i in range(2):
                            h = 2 * u + i
                            last = pe.matmul(bank[:, t, i, :], query_stack[s][0:ROWS, h, t * P:(t + 1) * P],
                                             key_stack[s][0:ROWS, 0 if l == "l2" else h, :],
                                             start=masked is None, stop=masked is None or i == 1)
                    last.then_inc(filled, 1)

                def scores_for_exp(key):
                    s, l, step = key
                    u = int(step[3:])
                    if u % 4 == 0:
                        pe.wait_ge(max_placed, TURN_NO.done(r, (s, l, f"turn{u // 4}"), times=16))
                    bank, filled = wait_free_unit(pe, r, key)
                    masked = neg[l][s] if l in neg else None
                    for k in range(T):
                        if masked is not None:
                            for t in range(T):
                                pe.matmul(bank[:, k, :, t * P:(t + 1) * P], masked[:, t, k * P:(k + 1) * P],
                                          twice(ident_b[:], P), start=(t == 0), stop=False)
                        for i in range(2):
                            h = 2 * u + i
                            last = pe.matmul(bank[:, k, i, :],
                                             key_stack[s][0:MAX_ROWS, 0 if l == "l2" else h, k * P:(k + 1) * P],
                                             query_stack[s][0:MAX_ROWS, h, :],
                                             start=masked is None, stop=masked is None or i == 1)
                    last.then_inc(filled, 1)

                def weigh(key):
                    s, l, step = key
                    g = int(step[-1])
                    if g == 0:
                        if l == "self":
                            pe.wait_ge(ev["values_self"][s], r.value(1, 1))
                        elif l == "cross":
                            pe.wait_ge(ev["values_cross"][s], r.value(1, 1))
                        if i is not None:
                            outs = sum(1 for k in SCHEDULE[:SCHEDULE.index(key)] if k[2] == "out1")
                            pe.wait_ge(out_taken, i * OUT_NO.round + (OUT_NO.start + outs))
                    pe.wait_ge(exped, count(EXP_NO, r, (s, l, f"exp{2 * g + 1}")))
                    for k in range(T):
                        for j in range(NJ):
                            n = EXP_NO.position(r, (s, l, f"exp{2 * g + j // 2}"))
                            w = values_l2[s][:, k, :] if l == "l2" else values[s][:, k, head_in(NJ * g + j), :]
                            last = pe.matmul(out_psum[g // 2][Q * j:Q * (j + 1), g % 2, :], w,
                                             probs[:, n % PROB_BUFS, k, j % 2, :], start=(k == 0), stop=(k == T - 1))
                    last.then_inc(weighed, 1)

                for key in keys:
                    r = Round(i, key)
                    s, l, step = key
                    if step[:3] == "max":
                        scores_for_max(key)
                    elif step[:3] == "exp":
                        scores_for_exp(key)
                    elif step.startswith("weigh"):
                        weigh(key)
                    elif step in ("turn0", "turn1"):
                        a = int(step[-1])
                        pe.wait_ge(max_cut, count(PIECES_NO, r, (s, l, f"pieces{a}")))
                        bank, filled = wait_free_work(pe, r, key)
                        for t in range(T):
                            last = pe.matmul(bank[0:3 * HC, 0, t * P:(t + 1) * P],
                                             max_pieces[:, a, t].rearrange("p i h -> p (i h)"), ident_b[:],
                                             start=True, stop=True)
                        last.then_inc(filled, 1)
                    elif step == "xT":
                        pe.wait_ge(x_loaded, r.value(16 * STREAMS, 16 * (s + 1)))
                        turn(key, x_in)
                    elif step == "ctxT":
                        pe.wait_ge(ev["c_loaded"][s], r.value(16, 16))
                        turn(key, c_in[s])
                    elif step == "ctxnT":
                        turn(key, norm[s], ev["ctx_norm"][s])
                    elif step == "keys" and l == "l2":
                        bank, filled = wait_free_work(pe, r, key)
                        for c in range(C):
                            pe.matmul(bank[0:HD, 0, :], pv("wk_l2", C)[:, c, :], ctx_t[s][:, c, :],
                                      start=(c == 0), stop=(c == C - 1))
                        for t in range(T):
                            for c in range(C):
                                last = pe.matmul(bank[:, 1, t * HD:(t + 1) * HD], ctx_t[s][:, c, t * P:(t + 1) * P],
                                                 pv("wv_l2", C)[:, c, :], start=(c == 0), stop=(c == C - 1))
                        last.then_inc(filled, 1)
                    elif step == "keys":
                        if l == "l1":
                            wait_taken(pe, r, (s, "self", "ctxnT"), before=key)
                        to_features(key, f"wk_{l}", ctxn_t[s])
                    elif step == "v":
                        to_tokens(key, dense(ctxn_t[s], f"wv_{l}"))
                    elif step in ("mix0", "mix1"):
                        t = int(step[-1])
                        pe.wait_ge(out_taken, count(OUT_NO, r, (s, l, "out1")))
                        bank, filled = wait_free_work(pe, r, key)
                        for g in range(NG):
                            last = pe.transpose(flatten(bank[:])[:, g * P:(g + 1) * P],
                                                out_t[s][:, g, t * P:(t + 1) * P], ident[:])
                        last.then_inc(filled, 1)
                    elif step == "outT":
                        wait_taken(pe, r, (s, l, "mix0"), (s, l, "mix1"), before=key)
                        turn(key, out_tok[s])
                    elif step == "proj":
                        wait_taken(pe, r, (s, l, "outT"), before=key)
                        to_tokens(key, dense(turned_t[s], f"wo_{BEFORE[l]}"))
                    elif step in ("lnT", "lnqT"):
                        if l == "l2":
                            wait_taken(pe, r, (s, l, "proj"), before=key)
                            turn(key, summed[s])
                        else:
                            done, src = {"cross": ("ln1", resid[s]), "l1": ("ln2", resid[s]), "l3": ("lnin", norm[s]),
                                         "end": ("lnmlp", norm[s])}[l]
                            if step == "lnqT":
                                done = "lnq"
                            turn(key, src, ev[done][s])
                    elif step == "q":
                        wait_taken(pe, r, (s, l, {"self": "xT", "l1": "lnqT"}.get(l, "lnT")), before=key)
                        if l in ("self", "cross"):
                            bank, filled = wait_free_work(pe, r, key)
                            for c in range(C):
                                last = pe.matmul(bank[:, c, :], fold[l][:], tok_t[s][:, c, :], start=True, stop=True)
                            last.then_inc(filled, 1)
                        else:
                            to_features(key, f"wq_{l}", tok_t[s])
                    elif step == "hid_out":
                        wait_taken(pe, r, *[(s, l, f"hid{i}") for i in range(FC // 2)], before=key)
                        to_tokens(key, dense(hidden_t[s], "l0_w2" if l == "l1" else "l3_w2", FC))
                    elif step[:3] == "hid":
                        if step == "hid0":
                            wait_taken(pe, r, (s, l, "lnT"), before=key)
                        to_features(key, "l0_w1" if l == "l1" else "l3_w1", tok_t[s], int(step[-1]) * 2 * P)
                    elif step == "attnT":
                        wait_taken(pe, r, (s, l, "proj"), before=key)
                        turn(key, attn[s])
                    elif step == "gate":
                        wait_taken(pe, r, (s, l, "attnT"), before=key)
                        w = pv("wg", 2 * C)
                        to_tokens(key, [(turned_t[s][:, c, :], w[:, c, :]) for c in range(C)]
                                  + [(tok_t[s][:, c, :], w[:, C + c, :]) for c in range(C)])
                    elif step == "mean":
                        pe.wait_ge(ev["xhat"][s], r.value(1, 1))
                        bank, filled = wait_free_work(pe, r, key)
                        for t in range(T):
                            last = pe.matmul(bank[:, 0, :], mean_w[:], xhat[s][:, t, :], start=(t == 0), stop=(t == T - 1))
                        last.then_inc(filled, 1)

            run(None, FIRST)
            meet(pe)
            pe.wait_ge(loaded, 16 * LOADS)
            pe.matmul(unit_psum[0][:, 1], setup["wv_self"], pv("wo_self", C), start=True, stop=True)
            pe.matmul(unit_psum[1][:, 0], setup["wv_cross"], pv("wo_cross", C), start=True, stop=True)
            sums = flatten(unit_psum[1][:, 1])
            for name, a in BIAS_COLUMNS.items():
                weight, vector = BIAS_SOURCES[name]
                for m in range(AT[name][1]):
                    for c in range(C):
                        last = pe.matmul(sums[:, a + m:a + m + 1], pv(weight, C)[:, c, m * P:(m + 1) * P],
                                         pv(vector)[:, c:c + 1], start=(c == 0), stop=(c == C - 1))
            last.then_inc(fold_products, 1)
            pe.wait_ge(fold_wide, 1)
            for i, name in enumerate(("wo_l1", "wo_l2", "wo_l3")):
                for c in range(C):
                    last = pe.matmul(row_psum[i], bv_wide[:, i, c, :], pv(name, C)[:, c, :],
                                     start=(c == 0), stop=(c == C - 1))
            last.then_inc(fold_rows, 1)
            pe.wait_ge(folded, 1)
            with pe.Fori(0, PAIRS) as i:
                run(i, SCHEDULE)


def heads_first(w, axis=0):
    w = np.moveaxis(w, axis, 0)
    w = w.reshape((C, HC, HD) + w.shape[1:]).swapaxes(1, 2).reshape(w.shape)
    return np.moveaxis(w, 0, axis)


def pack(i):
    got = {}

    def chunks(w):
        k, n = w.shape
        return w.reshape(k // P, P, n).transpose(1, 0, 2).reshape(P, -1)

    def column(v):
        return v.reshape(-1, P).T


    def rows(v):
        return np.repeat(heads_first(v).reshape(1, -1), P, axis=0)

    def both(w):
        return heads_first(heads_first(w), 1)

    got["wo_self"] = chunks(both(i["L0_xattn_msa_Wo"].T))
    got["wo_cross"] = chunks(both(i["L0_xattn_ca_Wo"].T))
    got["l0_w1"] = chunks(heads_first(i["L0_xattn_ff_W1"].T))
    got["l0_w2"] = chunks(heads_first(i["L0_xattn_ff_W2"].T, 1))
    got["l0_b1"] = column(i["L0_xattn_ff_b1"])
    for n in (1, 2, 3):
        got[f"ln{n}_g"] = rows(i[f"L0_xattn_ln{n}_g"])
        got[f"ln{n}_b"] = rows(i[f"L0_xattn_ln{n}_b"])
    got["bo_self"] = rows(i["L0_xattn_msa_bo"])
    got["bo_cross"] = rows(i["L0_xattn_ca_bo"])
    got["l0_b2"] = rows(i["L0_xattn_ff_b2"])
    L1, L2, L3 = "L1_xattn_", "L2_xattn_", "L3_xattn_"
    got["wq_l1"] = chunks(both(i[L1 + "wq"].T))
    got["wk_l1"] = chunks(both(i[L1 + "wk"].T))
    got["wv_l1"] = chunks(both(i[L1 + "wv"].T))
    got["wo_l1"] = chunks(both(i[L1 + "wo"].T))
    got["bq_l1"] = column(heads_first(i[L1 + "bq"]))
    got["bk_l1"] = column(heads_first(i[L1 + "bk"]))
    got["g_kv"] = column(heads_first(i[L1 + "g_kv"]))
    got["b_kv"] = column(heads_first(i[L1 + "b_kv"]))
    got["bv_l1"] = column(heads_first(i[L1 + "bv"]))
    got["g_q"] = rows(i[L1 + "g_q"])
    got["b_q"] = rows(i[L1 + "b_q"])
    got["bo_l1"] = rows(i[L1 + "bo"])
    got["wq_l2"] = chunks(both(i[L2 + "Wq"]))
    got["wk_l2"] = chunks(heads_first(i[L2 + "Wk"]))
    got["wv_l2"] = chunks(heads_first(i[L2 + "Wv"]))
    got["wo_l2"] = chunks(both(i[L2 + "Wo"]))
    got["wg"] = np.concatenate([chunks(both(w)) for w in (i[L2 + "Wg"][:E], i[L2 + "Wg"][E:])], axis=1)
    got["bq_l2"] = column(heads_first(i[L2 + "bq"]))
    one = np.zeros((P, 1), np.float32)
    one[:HD, 0] = i[L2 + "bk"]
    got["bk_l2"] = one
    got["bv_l2"] = column(heads_first(np.tile(i[L2 + "bv"], H)))
    got["bo_l2"] = rows(i[L2 + "bo"])
    got["bg"] = rows(i[L2 + "bg"])
    got["rms_w"] = rows(i[L2 + "rms_w"])
    got["wq_l3"] = chunks(both(i[L3 + "wq"]))
    got["wk_l3"] = chunks(both(i[L3 + "wk"]))
    got["wv_l3"] = chunks(both(i[L3 + "wv"]))
    got["wo_l3"] = chunks(both(i[L3 + "wo"]))
    got["l3_w1"] = chunks(heads_first(i[L3 + "w1"]))
    got["l3_w2"] = chunks(heads_first(i[L3 + "w2"], 1))
    got["bq_l3"] = column(heads_first(i[L3 + "bq"]))
    got["bk_l3"] = column(heads_first(i[L3 + "bk"]))
    got["g_in"] = column(heads_first(i[L3 + "ln1_g"]))
    got["b_in"] = column(heads_first(i[L3 + "ln1_b"]))
    got["bv_l3"] = column(heads_first(i[L3 + "bv"]))
    got["g_mlp"] = column(heads_first(i[L3 + "ln2_g"]))
    got["b_mlp"] = column(heads_first(i[L3 + "ln2_b"]))
    got["l3_b1"] = column(i[L3 + "b1"])
    got["bo_l3"] = rows(i[L3 + "bo"])
    got["l3_b2"] = rows(i[L3 + "b2"])
    return np.ascontiguousarray(np.concatenate([got[name] for name, _ in PACK], axis=1))


def pack_setup(i):
    blocks = np.zeros((P, len(SETUP), P), np.float32)
    for n, name in enumerate(SETUP):
        w = i["L0_xattn_" + {"self": "msa_W", "cross": "ca_W"}[name[3:]] + name[1]]
        for k in range(HC):
            blocks[k::HC, n, k::HC] = w
    return blocks.reshape(P, -1)


def kernel(**inputs):
    import concourse.bacc as bacc
    from concourse.bass_utils import run_bass_kernel_spmd

    i = {k: np.asarray(v) for k, v in inputs.items()}
    arrays = {
        "in_x": np.ascontiguousarray(heads_first(i["x"], 2)),
        "in_ctx": np.ascontiguousarray(heads_first(i["ctx_1024"], 2)),
        "in_mask_cross": np.ascontiguousarray(i["mask_Bx1xSxS2_if1"]),
        "in_mask_self": np.ascontiguousarray(i["mask_Bx1xSxS2_ik0"]),
        "in_params": pack(i),
        "in_setup": pack_setup(i),
    }
    nc = bacc.Bacc("TRN2", target_bir_lowering=False, num_devices=1)
    args = [nc.dram_tensor(n, a.shape, mybir.dt.from_np(a.dtype), kind="ExternalInput").ap()
            for n, a in arrays.items()]
    args.append(nc.dram_tensor("out", (B, S, E), FP32, kind="ExternalOutput").ap())
    build(nc, *args)
    r = run_bass_kernel_spmd(nc, [arrays], core_ids=[0])
    return r.results[0]["out"].reshape(B, S, C, HD, HC).swapaxes(3, 4).reshape(B, S, E)
```
